# Optimizing a Trainium2 kernel written in Bass

```python
import numpy as np
import jax
import jax.numpy as jnp

def _softmax(x, axis=-1):
    return jax.nn.softmax(x, axis=axis)

def _gelu(x):
    return jax.nn.gelu(x, approximate=True)

def _silu(x):
    return jax.nn.silu(x)

def _sigmoid(x):
    return jax.nn.sigmoid(x)

def _layernorm(x, axis=-1, eps=1e-05):
    m = jnp.mean(x, axis=axis, keepdims=True)
    v = jnp.var(x, axis=axis, keepdims=True)
    return (x - m) / jnp.sqrt(v + eps)

def _scatter_add(tgt, idx, src, axis=0):
    return tgt.at[idx].add(src)

def _segment_sum(src, seg, n):
    return jax.ops.segment_sum(src, seg, n)
kernel_name = 'mk_sandwich_d2_jaxref_r8_19cb9a'

def setup_inputs(seed: int=0):
    np.random.seed(seed)
    _w = jnp.asarray

    def _L0_attn_setup():
        import jax, jax.numpy as jnp
        import numpy as np
        N_HEADS = 16
        D_HEAD = 128
        D_MODEL = 256
        MAXLEN = 256
        key = jax.random.key(seed)
        ks = jax.random.split(key, 9)
        b, t = (2, 256)
        hd = N_HEADS * D_HEAD
        init = 0.02
        return {'x': jax.random.normal(ks[0], (b, t, D_MODEL), dtype=jnp.float32), 'Wq': jax.random.normal(ks[1], (D_MODEL, hd), dtype=jnp.float32) * init, 'bq': jnp.zeros((hd,), dtype=jnp.float32), 'Wk': jax.random.normal(ks[2], (D_MODEL, hd), dtype=jnp.float32) * init, 'bk': jnp.zeros((hd,), dtype=jnp.float32), 'Wv': jax.random.normal(ks[3], (D_MODEL, hd), dtype=jnp.float32) * init, 'bv': jnp.zeros((hd,), dtype=jnp.float32), 'Wo': jax.random.normal(ks[4], (hd, D_MODEL), dtype=jnp.float32) * init, 'bo': jnp.zeros((D_MODEL,), dtype=jnp.float32)}
    _L0_attn_in = _L0_attn_setup()

    def _L0_ffn_setup():
        import jax, jax.numpy as jnp
        import numpy as np
        HIDDEN = 256
        INTER = 1024
        SCALE = 64.0

        def fwht(x):
            orig_shape = x.shape
            n = orig_shape[-1]
            x = x.reshape(-1, n)
            h = 1
            while h < n:
                x = x.reshape(-1, n // (2 * h), 2, h)
                a, b = (x[:, :, 0, :], x[:, :, 1, :])
                x = jnp.stack([a + b, a - b], axis=2).reshape(-1, n)
                h *= 2
            return (x / jnp.sqrt(jnp.asarray(n, x.dtype))).reshape(orig_shape)
        key = jax.random.key(seed)
        ks = jax.random.split(key, 8)
        inp = jax.random.normal(ks[0], (4, 256, HIDDEN), dtype=jnp.float32)
        SU_ug = jnp.where(jax.random.bernoulli(ks[1], 0.5, (HIDDEN,)), 1.0, -1.0).astype(jnp.float32)
        SU_dp = jnp.where(jax.random.bernoulli(ks[2], 0.5, (INTER,)), 1.0, -1.0).astype(jnp.float32)
        Wscale_ug = jax.random.uniform(ks[3], (2 * INTER,), jnp.float32, 0.5, 1.5)
        Wscale_dp = jax.random.uniform(ks[4], (HIDDEN,), jnp.float32, 0.5, 1.5)
        W_up = jax.random.normal(ks[5], (INTER, HIDDEN), dtype=jnp.float32) * 0.02
        W_gate = jax.random.normal(ks[6], (INTER, HIDDEN), dtype=jnp.float32) * 0.02
        W_down = jax.random.normal(ks[7], (HIDDEN, INTER), dtype=jnp.float32) * 0.02
        return {'input': inp, 'SU_ug': SU_ug, 'SU_dp': SU_dp, 'Wscale_ug': Wscale_ug, 'Wscale_dp': Wscale_dp, 'W_up': W_up, 'W_gate': W_gate, 'W_down': W_down}
    _L0_ffn_in = _L0_ffn_setup()

    def _L1_attn_setup():
        import jax, jax.numpy as jnp
        import numpy as np
        WIDTH = 256
        NUM_HEADS = 16
        HEAD_DIM = WIDTH // NUM_HEADS
        ROPE_DIMS = HEAD_DIM // 2
        WINDOW = 64
        ROPE_BASE = 10000.0
        NEG_INF = -1000000000.0

        def apply_rope(x, dims, offset=0, base=ROPE_BASE):
            L = x.shape[2]
            half = dims // 2
            pos = (offset + jnp.arange(L)).astype(x.dtype)
            inv_freq = jnp.exp(-jnp.log(jnp.asarray(base, x.dtype)) * (jnp.arange(0, dims, 2).astype(x.dtype) / dims))
            theta = pos[:, None] * inv_freq[None, :]
            cos = jnp.cos(theta)[None, None]
            sin = jnp.sin(theta)[None, None]
            x1 = x[..., :half]
            x2 = x[..., half:dims]
            rest = x[..., dims:]
            rx1 = x1 * cos - x2 * sin
            rx2 = x1 * sin + x2 * cos
            return jnp.concatenate([rx1, rx2, rest], axis=-1)
        key = jax.random.key(seed)
        ks = jax.random.split(key, 6)
        B, L, D, hd = (2, 256, WIDTH, HEAD_DIM)
        x = jax.random.normal(ks[0], (B, L, D), dtype=jnp.float32)
        Wq = jax.random.normal(ks[1], (D, D), dtype=jnp.float32) * 0.02
        Wk = jax.random.normal(ks[2], (D, hd), dtype=jnp.float32) * 0.02
        Wv = jax.random.normal(ks[3], (D, hd), dtype=jnp.float32) * 0.02
        Wo = jax.random.normal(ks[4], (D, D), dtype=jnp.float32) * 0.02
        bo = jax.random.normal(ks[5], (D,), dtype=jnp.float32) * 0.02
        return {'x': x, 'Wq': Wq, 'Wk': Wk, 'Wv': Wv, 'Wo': Wo, 'bo': bo}
    _L1_attn_in = _L1_attn_setup()

    def _L1_ffn_setup():
        import jax, jax.numpy as jnp
        import numpy as np
        TOP_K = 2
        CAPACITY_FACTOR = 1.0

        def _ffn(x, w1, w2):
            h = x @ w1
            x1, x2 = jnp.split(h, 2, axis=-1)
            return x1 * jax.nn.silu(x2) @ w2
        key = jax.random.key(seed)
        ks = jax.random.split(key, 6)
        B, S, D, F, E_r, E_s = (4, 256, 256, 128, 7, 1)
        sc_in = 1.0 / np.sqrt(D)
        sc_mid = 1.0 / np.sqrt(F)
        return {'x': jax.random.normal(ks[0], (B, S, D), dtype=jnp.float32), 'gate_w': jax.random.normal(ks[1], (D, E_r), dtype=jnp.float32) * sc_in, 'expert_bias': jnp.zeros((E_r,), dtype=jnp.float32), 'shared_w1': jax.random.normal(ks[2], (E_s, D, 2 * F), dtype=jnp.float32) * sc_in, 'shared_w2': jax.random.normal(ks[3], (E_s, F, D), dtype=jnp.float32) * sc_mid, 'routed_w1': jax.random.normal(ks[4], (E_r, D, 2 * F), dtype=jnp.float32) * sc_in, 'routed_w2': jax.random.normal(ks[5], (E_r, F, D), dtype=jnp.float32) * sc_mid}
    _L1_ffn_in = _L1_ffn_setup()
    _d = {'L0_attn_x': _L0_attn_in['x'], 'L0_attn_Wq': _L0_attn_in['Wq'], 'L0_attn_bq': _L0_attn_in['bq'], 'L0_attn_Wk': _L0_attn_in['Wk'], 'L0_attn_bk': _L0_attn_in['bk'], 'L0_attn_Wv': _L0_attn_in['Wv'], 'L0_attn_bv': _L0_attn_in['bv'], 'L0_attn_Wo': _L0_attn_in['Wo'], 'L0_attn_bo': _L0_attn_in['bo'], 'L0_ffn_SU_ug': _L0_ffn_in['SU_ug'], 'L0_ffn_SU_dp': _L0_ffn_in['SU_dp'], 'L0_ffn_Wscale_ug': _L0_ffn_in['Wscale_ug'], 'L0_ffn_Wscale_dp': _L0_ffn_in['Wscale_dp'], 'L0_ffn_W_up': _L0_ffn_in['W_up'], 'L0_ffn_W_gate': _L0_ffn_in['W_gate'], 'L0_ffn_W_down': _L0_ffn_in['W_down'], 'L1_attn_Wq': _L1_attn_in['Wq'], 'L1_attn_Wk': _L1_attn_in['Wk'], 'L1_attn_Wv': _L1_attn_in['Wv'], 'L1_attn_Wo': _L1_attn_in['Wo'], 'L1_attn_bo': _L1_attn_in['bo'], 'L1_ffn_gate_w': _L1_ffn_in['gate_w'], 'L1_ffn_expert_bias': _L1_ffn_in['expert_bias'], 'L1_ffn_shared_w1': _L1_ffn_in['shared_w1'], 'L1_ffn_shared_w2': _L1_ffn_in['shared_w2'], 'L1_ffn_routed_w1': _L1_ffn_in['routed_w1'], 'L1_ffn_routed_w2': _L1_ffn_in['routed_w2']}
    _x0 = _d['L0_attn_x']
    _d['L0_attn_x'] = jax.random.normal(jax.random.fold_in(jax.random.key(seed), 1), (4, 512, 256), dtype=_x0.dtype)
    del _x0
    return _d

def reference(L0_attn_x, L0_attn_Wq, L0_attn_bq, L0_attn_Wk, L0_attn_bk, L0_attn_Wv, L0_attn_bv, L0_attn_Wo, L0_attn_bo, L0_ffn_SU_ug, L0_ffn_SU_dp, L0_ffn_Wscale_ug, L0_ffn_Wscale_dp, L0_ffn_W_up, L0_ffn_W_gate, L0_ffn_W_down, L1_attn_Wq, L1_attn_Wk, L1_attn_Wv, L1_attn_Wo, L1_attn_bo, L1_ffn_gate_w, L1_ffn_expert_bias, L1_ffn_shared_w1, L1_ffn_shared_w2, L1_ffn_routed_w1, L1_ffn_routed_w2):

    def _L0_attn_ref(x, Wq, bq, Wk, bk, Wv, bv, Wo, bo):
        import jax, jax.numpy as jnp
        import numpy as np
        N_HEADS = 16
        D_HEAD = 128
        D_MODEL = 256
        MAXLEN = 256
        b, t, _ = x.shape
        h, dh = (N_HEADS, D_HEAD)
        scale = 1.0 / np.sqrt(dh).astype(np.float32)
        q = (x @ Wq + bq).reshape(b, h, t, dh)
        k = (x @ Wk + bk).reshape(b, t, h, dh).transpose(0, 2, 3, 1)
        v = (x @ Wv + bv).reshape(b, t, h, dh).transpose(0, 2, 1, 3)
        logits = jnp.einsum('bhtd,bhds->bhts', q, k) * scale
        mask = jnp.triu(jnp.full((t, t), -jnp.inf, dtype=x.dtype), k=1)
        weights = jax.nn.softmax(logits + mask, axis=-1)
        out = jnp.einsum('bhts,bhsd->bhtd', weights, v)
        out = out.transpose(0, 2, 1, 3).reshape(b, t, h * dh)
        return out @ Wo + bo

    def _L0_ffn_ref(input, SU_ug, SU_dp, Wscale_ug, Wscale_dp, W_up, W_gate, W_down):
        import jax, jax.numpy as jnp
        import numpy as np
        HIDDEN = 256
        INTER = 1024
        SCALE = 64.0

        def fwht(x):
            orig_shape = x.shape
            n = orig_shape[-1]
            x = x.reshape(-1, n)
            h = 1
            while h < n:
                x = x.reshape(-1, n // (2 * h), 2, h)
                a, b = (x[:, :, 0, :], x[:, :, 1, :])
                x = jnp.stack([a + b, a - b], axis=2).reshape(-1, n)
                h *= 2
            return (x / jnp.sqrt(jnp.asarray(n, x.dtype))).reshape(orig_shape)
        n = SU_ug.shape[0]
        x = input.reshape(-1, n)
        x = fwht(x * SU_ug) / SCALE
        x_up = x @ W_up.T * (Wscale_ug[:INTER] * SCALE)
        x_gate = x @ W_gate.T * (Wscale_ug[INTER:] * SCALE)
        x = jax.nn.silu(x_gate) * x_up
        x = fwht(x * SU_dp) / SCALE
        x = x @ W_down.T * (Wscale_dp * SCALE)
        return x.reshape(input.shape)

    def _L1_attn_ref(x, Wq, Wk, Wv, Wo, bo):
        import jax, jax.numpy as jnp
        import numpy as np
        WIDTH = 256
        NUM_HEADS = 16
        HEAD_DIM = WIDTH // NUM_HEADS
        ROPE_DIMS = HEAD_DIM // 2
        WINDOW = 64
        ROPE_BASE = 10000.0
        NEG_INF = -1000000000.0

        def apply_rope(x, dims, offset=0, base=ROPE_BASE):
            L = x.shape[2]
            half = dims // 2
            pos = (offset + jnp.arange(L)).astype(x.dtype)
            inv_freq = jnp.exp(-jnp.log(jnp.asarray(base, x.dtype)) * (jnp.arange(0, dims, 2).astype(x.dtype) / dims))
            theta = pos[:, None] * inv_freq[None, :]
            cos = jnp.cos(theta)[None, None]
            sin = jnp.sin(theta)[None, None]
            x1 = x[..., :half]
            x2 = x[..., half:dims]
            rest = x[..., dims:]
            rx1 = x1 * cos - x2 * sin
            rx2 = x1 * sin + x2 * cos
            return jnp.concatenate([rx1, rx2, rest], axis=-1)
        B, L, D = x.shape
        H, hd = (NUM_HEADS, HEAD_DIM)
        scale = hd ** (-0.5)
        q = (x @ Wq).reshape(B, L, H, hd).transpose(0, 2, 1, 3)
        k = (x @ Wk).reshape(B, L, 1, hd).transpose(0, 2, 1, 3)
        v = (x @ Wv).reshape(B, L, 1, hd).transpose(0, 2, 1, 3)
        q = apply_rope(q, ROPE_DIMS)
        k = apply_rope(k, ROPE_DIMS)
        i = jnp.arange(L)[:, None]
        j = jnp.arange(L)[None, :]
        allowed = (i - j >= 0) & (i - j < WINDOW)
        mask = jnp.where(allowed, 0.0, NEG_INF).astype(x.dtype)
        scores = jnp.einsum('bhqd,bkd->bhqk', q, k[:, 0]) * scale
        scores = scores + mask[None, None]
        attn = jax.nn.softmax(scores, axis=-1)
        out = jnp.einsum('bhqk,bkd->bhqd', attn, v[:, 0])
        out = out.transpose(0, 2, 1, 3).reshape(B, L, D)
        return out @ Wo + bo

    def _L1_ffn_ref(x, gate_w, expert_bias, shared_w1, shared_w2, routed_w1, routed_w2):
        import jax, jax.numpy as jnp
        import numpy as np
        TOP_K = 2
        CAPACITY_FACTOR = 1.0

        def _ffn(x, w1, w2):
            h = x @ w1
            x1, x2 = jnp.split(h, 2, axis=-1)
            return x1 * jax.nn.silu(x2) @ w2
        B, S, D = x.shape
        E_r = gate_w.shape[1]
        T = B * S
        capacity = max(1, int(CAPACITY_FACTOR * T / E_r))
        flat_x = x.reshape(T, D)
        shared_sum = jax.vmap(_ffn, in_axes=(None, 0, 0))(flat_x, shared_w1, shared_w2).sum(0)
        gate_logits = flat_x @ gate_w + expert_bias
        aff = jax.nn.sigmoid(gate_logits)
        _, topk_idx = jax.lax.top_k(aff, TOP_K)
        mask = (topk_idx[:, :, None] == jnp.arange(E_r)[None, None, :]).any(axis=1)
        score = jnp.where(mask, aff, -1.0).T
        _, sel_idx = jax.lax.top_k(score, capacity)
        kept = jnp.take_along_axis(mask.T, sel_idx, axis=1)
        w = jnp.where(kept, jnp.take_along_axis(aff.T, sel_idx, axis=1), 0.0)
        inp = flat_x[sel_idx]
        out = jax.vmap(_ffn)(inp, routed_w1, routed_w2)
        routed_sum = jnp.zeros_like(flat_x).at[sel_idx].add(out * w[:, :, None])
        return (shared_sum + routed_sum).reshape(B, S, D)
    x = L0_attn_x
    x = x + _layernorm(_L0_attn_ref(_layernorm(x, axis=-1), L0_attn_Wq, L0_attn_bq, L0_attn_Wk, L0_attn_bk, L0_attn_Wv, L0_attn_bv, L0_attn_Wo, L0_attn_bo), axis=-1)
    x = x + _layernorm(_L0_ffn_ref(_layernorm(x, axis=-1), L0_ffn_SU_ug, L0_ffn_SU_dp, L0_ffn_Wscale_ug, L0_ffn_Wscale_dp, L0_ffn_W_up, L0_ffn_W_gate, L0_ffn_W_down), axis=-1)
    x = x + _layernorm(_L1_attn_ref(_layernorm(x, axis=-1), L1_attn_Wq, L1_attn_Wk, L1_attn_Wv, L1_attn_Wo, L1_attn_bo), axis=-1)
    x = x + _layernorm(_L1_ffn_ref(_layernorm(x, axis=-1), L1_ffn_gate_w, L1_ffn_expert_bias, L1_ffn_shared_w1, L1_ffn_shared_w2, L1_ffn_routed_w1, L1_ffn_routed_w2), axis=-1)
    return x

_drawn_inputs = setup_inputs


def setup_inputs(seed=0):
    import zlib

    import numpy as np

    out = dict(_drawn_inputs(seed))
    spreads = {'L0_attn_bq': (0.0, 0.306),
     'L0_attn_bk': (0.0, 0.8),
     'L0_attn_bv': (0.0, 0.1),
     'L0_attn_bo': (0.0, 0.1),
     'L1_ffn_expert_bias': (0.0, 0.1)}
    factors = {}
    for name, (base, spread) in spreads.items():
        noise = np.random.default_rng([zlib.crc32(name.encode()), seed]).standard_normal(out[name].shape)
        drawn = base * np.exp(spread * noise) if base else spread * noise
        out[name] = jnp.asarray(drawn.astype(out[name].dtype))
    for name, factor in factors.items():
        out[name] = (out[name] * factor).astype(out[name].dtype)
    return out
```

```python
from contextlib import ExitStack

import numpy as np

import concourse.bass as bass
from concourse import mybir
from concourse.alu_op_type import AluOpType as ALU

ACT = mybir.ActivationFunctionType
AX_X = mybir.AxisListType.X
F32 = mybir.dt.float32
F32R = mybir.dt.float32r
BF16 = mybir.dt.bfloat16
I32 = mybir.dt.int32

P = 128
B, T, D = 4, 512, 256
TT, KD = T // P, D // P
NT = B * TT
INTER = 1024
H, DH = 16, 128
HD = H * DH
H1, DH1 = 16, 16
WINDOW, ROPE, ROPE_BASE = 64, 8, 10000.0
E, TOP_K = 7, 2
CAPACITY = B * T // E
DIGITS, DIGIT = 10, 3
WAYS = 2 ** DIGIT - 1
LN_EPS = 1e-5
DMA_INC = 16
CHUNK = 256
NCHUNK = HD // CHUNK
RAW = 4

S_BANK = {0: 0, 2: 0, 1: 1, 3: 2}
S_COL = {0: 0, 2: P, 1: 0, 3: 0}
P_COL = {0: 0, 2: P, 1: 4 * P, 3: 6 * P}
SOFTMAX_ORDER = (0, 2, 1, 3)
T_FILLS = ((0,), (1, 3), (2,))
PT_COL = {0: 0, 1: 4 * P, 3: 7 * P, 2: 8 * P}
PT_ALL = 10 * P


def shape_constants():
    ident = np.eye(P, dtype=np.float32)
    causal = np.where(np.arange(P)[None, :] > np.arange(P)[:, None], -1e30, 0.0).astype(np.float32)
    signs = [[(-1.0) ** bin(i & j).count("1") for j in range(P)] for i in range(P)]
    freq = np.exp(-np.log(np.float32(ROPE_BASE)) * (np.arange(0, ROPE, 2, dtype=np.float32) / ROPE))
    theta = np.arange(T, dtype=np.float32)[:, None] * freq[None, :].astype(np.float32)
    cos, sin = np.cos(theta), np.sin(theta)
    tiled = [np.concatenate(x, 1).reshape(TT, P, ROPE).transpose(1, 0, 2) for x in ((cos, cos), (-sin, sin))]
    query, key = np.arange(P)[:, None] % WINDOW, np.arange(P)[None, :]
    seen = (key <= WINDOW + query) & (key > query)
    window = np.stack([np.where(seen & (key >= WINDOW), 0.0, -1e30), np.where(seen, 0.0, -1e30)], 1)
    below = np.tril(np.ones((E, E)), -1)
    expert = np.arange(P) // NT
    same = (expert[:, None] == expert[None, :]) & (expert[:, None] < E)
    units = 1 << (DIGIT * np.arange(DIGITS - 1, -1, -1))
    before = same & (np.arange(P)[:, None] < np.arange(P)[None, :])
    return {"c_ident": ident, "c_causal": causal, "c_hadamard": np.array(signs, np.float32),
            "c_cos": tiled[0].astype(np.float32), "c_sin": tiled[1].astype(np.float32),
            "c_window": window.astype(np.float32), "c_below": np.tile(below, (P, 1, 1)).astype(np.float32),
            "c_same": same[:, :E * NT].astype(np.float32), "c_before": before[:, :E * NT].astype(np.float32),
            "c_units": np.tile(units.astype(np.int32), (P, 1)),
            "c_steps": np.tile((units[:, None] * np.arange(1, WAYS + 1)).astype(np.int32), (P, 1, 1))}


def rounded(ap):
    return ap.bitcast(F32)


class Ring:

    def __init__(self, names, banks, before=(), last=None, rounds=None):
        assert len(names) % banks == 0
        self.banks, self.fills, self.rounds = banks, len(names), rounds
        self.start = len(before)
        self.before = {name: n for n, name in enumerate(before)}
        self.names = {name: n for n, name in enumerate(names)}
        self.last = {name: n for n, name in enumerate(last)} if last else self.names

    def bank(self, b, name):
        if isinstance(b, int) and b < 0:
            return self.before[name] % self.banks
        return (self.start + self.table(b)[name]) % self.banks

    def table(self, b):
        return self.last if isinstance(b, int) and b + 1 == self.rounds else self.names

    def order(self, b, name):
        if isinstance(b, int) and b < 0:
            return self.before[name]
        return b * self.fills + (self.start + self.table(b)[name])

    def earlier(self, b, name):
        if isinstance(b, int) and b < 0:
            return self.before[name] // self.banks
        return b * (self.fills // self.banks) + (self.start + self.table(b)[name]) // self.banks


class Banks:

    def __init__(self, ctx, nc, label, names, count, **more):
        self.ring = Ring(names, count, **more)
        self.psum = [ctx.enter_context(nc.psum_tensor(f"{label}{n}", [P, 512], F32)) for n in range(count)]
        self.filled = ctx.enter_context(nc.semaphore(f"{label}_filled"))
        self.freed = [ctx.enter_context(nc.semaphore(f"{label}_freed{n}")) for n in range(count)]

    def bank(self, b, name):
        return self.psum[self.ring.bank(b, name)]

    def wait_filled(self, eng, b, name):
        eng.wait_ge(self.filled, self.ring.order(b, name) + 1)

    def wait_freed(self, eng, b, name):
        eng.wait_ge(self.freed[self.ring.bank(b, name)], self.ring.earlier(b, name) + 1)

    def wait_kept(self, eng, b, name):
        eng.wait_ge(self.freed[self.ring.bank(b, name)], self.ring.earlier(b, name) + 2)

    def all_free(self, pe):
        for freed in self.freed:
            pe.sem_inc(freed, 1)

    def filled_by(self, ins):
        ins.then_inc(self.filled, 1)

    def freed_by(self, ins, b, name):
        ins.then_inc(self.freed[self.ring.bank(b, name)], 1)


def three_passes(pe, out, lhs, rhs, start, stop, **kw):
    (lh, ll), (rh, rl) = lhs, rhs
    pe.matmul(out, lh, rh, start=start, stop=False, **kw)
    pe.matmul(out, lh, rl, start=False, stop=False, **kw)
    return pe.matmul(out, ll, rh, start=False, stop=stop, **kw)


class Norm:

    def __init__(self, ctx, nc, c, label):
        self.nc, self.c = nc, c

        def sb(name, shape):
            return ctx.enter_context(nc.sbuf_tensor(f"{label}_{name}", shape, F32))

        self.st, self.mv = sb("st", [P, TT, 6]), sb("mv", [P, TT, 2])
        self.ve, self.rstd = sb("ve", [P, TT]), sb("rstd", [P, TT])
        self.aggr_done = ctx.enter_context(nc.semaphore(f"{label}_aggr_done"))
        self.var_ready = ctx.enter_context(nc.semaphore(f"{label}_var_ready"))
        self.rstd_ready = ctx.enter_context(nc.semaphore(f"{label}_rstd_ready"))

    def moments(self, dve, nth, source):
        nc = self.nc
        for i in range(TT):
            nc.vector.bn_stats(self.st[:, i, :], source(i))
        dve.drain()
        for i in range(TT):
            ins = nc.vector.bn_aggr(self.mv[:, i, :], self.st[:, i, :])
        ins.then_inc(self.aggr_done, 1)
        dve.wait_ge(self.aggr_done, nth + 1)
        nc.vector.tensor_scalar(self.ve[:], self.mv[:, :, 1], LN_EPS, None, ALU.add).then_inc(self.var_ready, 1)

    def wait_inverse(self, dve, nth):
        dve.wait_ge(self.rstd_ready, nth + 1)

    def inverse(self, pool, nth):
        pool.wait_ge(self.var_ready, nth + 1)
        self.nc.gpsimd.tensor_tensor(self.rstd[:], self.ve[:], self.c["minus_half"][:], ALU.pow).then_inc(
            self.rstd_ready, 1)

    def apply(self, out, source, i):
        return self.nc.vector.tensor_scalar(out, source, self.mv[:, i, 0:1], self.rstd[:, i:i + 1], ALU.subtract,
                                            ALU.mult)


def nth_before(b):
    return 0 if isinstance(b, int) and b == 0 else b * 2 - 1


def nth_behind(b, follows, batches):
    return b * 2 + 2 if follows else 2 * batches - 1


def every_batch(eng, body):
    body(-1, True)
    with eng.Fori(0, B - 1) as b:
        body(b, True)
    body(B - 1, False)


def attention0(nc, a, c, x_tok):
    HG = 2
    prepare = [f"ln{k}" for k in range(KD)] + [f"q{n}" for n in range(H)] + ["k0", "v0_0", "v0_1"]
    fills, last = [], []
    for names, follows in ((fills, True), (last, False)):
        for h in range(H):
            tail = follows and h + 1 == H
            names += [f"ln{k}" for k in range(KD)] * tail
            names += [f"k{h + 1}"] * (h + 1 < H) + [f"o{h - 1}"] * (h > 0)
            names += [f"v{h // HG + 1}_{h % HG}"] * (h + HG < H)
            names += ["q0", "q1"] * tail + [f"t{h}_{n}" for n in range(3)] + ["q2", "q3"] * tail
        names += [f"o{H - 1}"]
        names += ([f"q{n}" for n in range(4, H)] + ["k0", "v0_0", "v0_1"]) * follows
    RAW, SLOTS = 2, 3
    HALF = HD // 2

    with ExitStack() as ctx:
        def sb(name, shape, dt=F32):
            return ctx.enter_context(nc.sbuf_tensor(name, shape, dt))

        def sem(name):
            return ctx.enter_context(nc.semaphore(name))

        wq_raw = sb("wq_raw", [P, RAW, KD, CHUNK])
        wq_s = [sb(f"wq_{s}", [P, SLOTS, KD, CHUNK], F32R) for s in ("hi", "lo")]
        wk_s = [sb(f"wk_{s}", [P, KD, HD], F32R) for s in ("hi", "lo")]
        wv_s = [sb(f"wv_{s}", [P, KD, HD], F32R) for s in ("hi", "lo")]
        wo = sb("wo", [P, H, D])
        xT = [sb(f"xT_{s}", [P, KD, T], F32R) for s in ("hi", "lo")]
        qT = sb("qT", [P, T, H])
        qs = [sb(f"qs_{s}", [P, T], F32R) for s in ("hi", "lo")]
        kT = [sb(f"kT_{s}", [P, T], F32R) for s in ("hi", "lo")]
        v = [sb(f"v_{s}", [P, 2, TT, HG * DH], F32R) for s in ("hi", "lo")]
        p = sb("p", [P, PT_ALL])
        pT = [sb(f"pT_{s}", [P, PT_ALL], F32R) for s in ("hi", "lo")]
        oT = sb("oT", [P, T])
        xn = sb("xn", [P, TT, D])
        y = sb("y", [P, TT, D])
        bq, bk, bv = (sb(n, [P, H]) for n in ("bq", "bk", "bv"))
        bqs = sb("bqs", [P, H])
        bo = sb("bo", [P, D])
        negm = sb("negm", [P, TT])
        rsum = sb("rsum", [P, TT])
        rinv = sb("rinv", [P, TT])
        banks = Banks(ctx, nc, "ring", fills, 3, before=prepare, last=last, rounds=B)
        s_ps = [ctx.enter_context(nc.psum_tensor(f"scores{n}", [P, 512], F32)) for n in range(3)]
        y_ps = [ctx.enter_context(nc.psum_tensor(f"y_ps{n}", [P, 512], F32)) for n in range(2)]
        norm = Norm(ctx, nc, c, "a")

        wo_flat, y_flat = wo[:].rearrange("p h d -> p (h d)"), y[:].rearrange("p t d -> p (t d)")
        landing = [wo_flat[:, n * HALF:(n + 1) * HALF] for n in range(4)] + [y_flat, p[:, 0:HALF]]
        pieces = [(w, k, half) for w in range(2) for k in range(KD) for half in range(2)]
        wq_loaded = [sem(f"wq_loaded{n}") for n in range(RAW)]
        wkv_loaded = [sem(f"wkv_loaded{n}") for n in range(len(pieces))]
        wq_hi, wq_lo = sem("wq_hi_ready"), sem("wq_lo_ready")
        wkv_hi, wkv_lo = sem("wkv_hi_ready"), sem("wkv_lo_ready")
        x_loaded, rows_loaded, wo_loaded = sem("x_loaded"), sem("rows_loaded"), sem("wo_loaded")
        bqs_ready = sem("bqs_ready")
        xn_ready, xT_hi = sem("xn_ready"), sem("xT_hi_ready")
        qs_hi, qs_lo = sem("qs_hi_ready"), sem("qs_lo_ready")
        k_hi, v_hi = sem("k_hi_ready"), sem("v_hi_ready")
        scored = [sem(f"scored{n}") for n in range(3)]
        max_ready, exp_ready, rinv_ready, p_ready = (sem(s) for s in ("max_ready", "exp_ready", "rinv_ready",
                                                                      "p_ready"))
        pT_hi = sem("pT_hi_ready")
        y_done, y_freed, y_normed, x_updated = (sem(s) for s in ("y_done", "y_freed", "y_normed", "x_updated"))

        def q_of(h):
            return qT[:, h * (T // H):(h + 1) * (T // H), :].rearrange("p t c -> p (t c)")

        block = ctx.enter_context(nc.Block())

        @block.sync
        def _(sp):
            def load_chunks(b):
                for n in range(NCHUNK):
                    if not (isinstance(b, int) and n < RAW):
                        sp.wait_ge(wq_lo, (b + 1) * NCHUNK + n - RAW + 1)
                    sp.dma_start(wq_raw[:, n % RAW], a["L0_attn_Wq"][:, n * CHUNK:(n + 1) * CHUNK].rearrange(
                        "(k p) n -> p k n", p=P)).then_inc(wq_loaded[n % RAW], DMA_INC)
                    if isinstance(b, int) and n >= 1:
                        load_pieces(*{1: (0, 2), 2: (2, 4), 3: (4, 6), 4: (6, 7), 5: (7, 8)}.get(n, (8, 8)))

            def load_pieces(lo, hi):
                for m in range(lo, hi):
                    w, k, half = pieces[m]
                    if m >= len(landing):
                        sp.wait_ge(wkv_lo, m - len(landing) + 1)
                    sp.dma_start(landing[m % len(landing)],
                                 a[("L0_attn_Wk", "L0_attn_Wv")[w]][k * P:(k + 1) * P,
                                                                    half * HALF:(half + 1) * HALF]).then_inc(
                        wkv_loaded[m], DMA_INC)

            sp.dma_start(x_tok[:, 0:TT, :], a["L0_attn_x"][0].rearrange("(t p) d -> p t d", p=P)).then_inc(
                x_loaded, DMA_INC)
            for name, dst in (("bq", bq), ("bk", bk), ("bv", bv)):
                sp.dma_start(dst[:], a[f"L0_attn_{name}"]).then_inc(rows_loaded, DMA_INC)
            sp.dma_start(bo[:], a["L0_attn_bo"].broadcast_to([P, D])).then_inc(rows_loaded, DMA_INC)
            load_chunks(-1)
            for b in range(1, B):
                sp.dma_start(x_tok[:, b * TT:(b + 1) * TT, :],
                             a["L0_attn_x"][b].rearrange("(t p) d -> p t d", p=P)).then_inc(x_loaded, DMA_INC)
            sp.wait_ge(wkv_lo, len(pieces))
            sp.dma_start(wo[:], a["L0_attn_Wo"].rearrange("(h d) n -> d h n", d=DH)).then_inc(wo_loaded, DMA_INC)
            with sp.Fori(0, B - 1) as b:
                load_chunks(b)

        @block.gpsimd
        def _(pool):
            def lo_of_chunk(b, n):
                pool.wait_ge(wq_hi, (b + 1) * NCHUNK + n + 1)
                nc.gpsimd.tensor_tensor(wq_s[1][:, n % SLOTS], wq_raw[:, n % RAW], rounded(wq_s[0][:, n % SLOTS]),
                                        ALU.subtract).then_inc(wq_lo, 1)

            def lo_of_q(nb, h):
                pool.wait_ge(qs_hi, nb * H + h + 1)
                nc.gpsimd.tensor_tensor(qs[1][:], q_of(h), rounded(qs[0][:]), ALU.subtract).then_inc(qs_lo, 1)

            def body(b, follows):
                first = isinstance(b, int) and b < 0
                for h in range(H if not first else 0):
                    if h + 1 < H:
                        lo_of_q(b, h + 1)
                    if follows and h == H - 4:
                        norm.inverse(pool, nth_before(b + 1))
                    if follows and H - 5 <= h < H - 5 + SLOTS:
                        lo_of_chunk(b, h - (H - 5))
                if first:
                    norm.inverse(pool, 0)
                    for n in range(SLOTS):
                        lo_of_chunk(b, n)
                if follows:
                    lo_of_chunk(b, 3)
                    lo_of_chunk(b, 4)
                if not first:
                    norm.inverse(pool, nth_behind(b, follows, B))
                if follows:
                    for n in range(5, NCHUNK):
                        lo_of_chunk(b, n)
                    lo_of_q(b + 1, 0)

            every_batch(pool, body)

        @block.scalar
        def _(act):
            def hi_of_x(b, k):
                banks.wait_filled(act, b, f"ln{k}")
                nc.scalar.activation(xT[0][:, k, :], banks.bank(b, f"ln{k}")[:], ACT.Copy).then_inc(xT_hi, 1)

            def hi_of_chunk(b, n):
                act.wait_ge(wq_loaded[n % RAW], (b + 1) * (NCHUNK // RAW * DMA_INC) + (n // RAW + 1) * DMA_INC)
                nc.scalar.activation(wq_s[0][:, n % SLOTS], wq_raw[:, n % RAW], ACT.Copy).then_inc(wq_hi, 1)

            def store_q(b, n):
                banks.wait_filled(act, b, f"q{n}")
                banks.freed_by(nc.scalar.activation(qT[:, :, n], banks.bank(b, f"q{n}")[:], ACT.Identity,
                                                    bias=bqs[:, n:n + 1], scale=float(DH) ** -0.5), b, f"q{n}")

            def hi_of_q(b, h):
                if h == 0:
                    for n in range(H - 3, H):
                        banks.wait_kept(act, b, f"q{n}")
                else:
                    act.wait_ge(scored[2], b * H + h)
                nc.scalar.activation(qs[0][:], q_of(h), ACT.Copy).then_inc(qs_hi, 1)

            def hi_of_k(b, h):
                banks.wait_filled(act, b, f"k{h}")
                nc.scalar.activation(kT[0][:], banks.bank(b, f"k{h}")[:], ACT.Identity,
                                     bias=bk[:, h:h + 1]).then_inc(k_hi, 1)

            def hi_of_v(b, g, n):
                banks.wait_filled(act, b, f"v{g}_{n}")
                nc.scalar.activation(v[0][:, g % 2, 2 * n:2 * n + 2].rearrange("p t d -> p (t d)"),
                                     banks.bank(b, f"v{g}_{n}")[:], ACT.Copy).then_inc(v_hi, 1)

            def softmax_exp(b, h):
                for n, i in enumerate(SOFTMAX_ORDER):
                    act.wait_ge(max_ready, b * H * TT + h * TT + max(n + 1, 2))
                    w = (i + 1) * P
                    ins = nc.scalar.activation(p[:, P_COL[i]:P_COL[i] + w],
                                               s_ps[S_BANK[i]][:, S_COL[i]:S_COL[i] + w], ACT.Exp,
                                               bias=negm[:, i:i + 1], accum_out=rsum[:, i:i + 1])
                    ins.then_inc(exp_ready, 1)

            def hi_of_pT(b, h):
                for n in range(3):
                    banks.wait_filled(act, b, f"t{h}_{n}")
                    col, w = PT_COL[T_FILLS[n][0]], (512, 512, 256)[n]
                    nc.scalar.activation(pT[0][:, col:col + w], banks.bank(b, f"t{h}_{n}")[:, 0:w],
                                         ACT.Copy).then_inc(pT_hi, 1)

            def store_o(b, h):
                banks.wait_filled(act, b, f"o{h}")
                banks.freed_by(nc.scalar.activation(oT[:], banks.bank(b, f"o{h}")[:], ACT.Identity,
                                                    bias=bv[:, h:h + 1]), b, f"o{h}")

            def body(b, follows):
                first = isinstance(b, int) and b < 0
                for h in range(H if not first else 0):
                    tail = follows and h + 1 == H
                    if tail:
                        hi_of_x(b, 0)
                        hi_of_x(b, 1)
                    softmax_exp(b, h)
                    if h + 1 < H:
                        hi_of_q(b, h + 1)
                        hi_of_k(b, h + 1)
                    if h:
                        store_o(b, h - 1)
                    if h + HG < H:
                        hi_of_v(b, h // HG + 1, h % HG)
                    if tail:
                        store_q(b, 0)
                        store_q(b, 1)
                    hi_of_pT(b, h)
                    if follows and H - 5 <= h < H - 5 + SLOTS:
                        hi_of_chunk(b, h - (H - 5))
                if first:
                    hi_of_chunk(b, 0)
                    hi_of_chunk(b, 1)
                    hi_of_x(b, 0)
                    hi_of_x(b, 1)
                    hi_of_chunk(b, 2)
                    act.wait_ge(bqs_ready, 1)
                    store_q(b, 0)
                    store_q(b, 1)
                if follows:
                    hi_of_chunk(b, 3)
                    store_q(b, 2)
                    store_q(b, 3)
                    hi_of_chunk(b, 4)
                if not first:
                    store_o(b, H - 1)
                if follows:
                    for n in range(4, H):
                        store_q(b, n)
                        if n in (5, 7, 9):
                            hi_of_chunk(b, (n + 5) // 2)
                    hi_of_q(b, 0)
                    hi_of_k(b, 0)
                    hi_of_v(b, 0, 0)
                    hi_of_v(b, 0, 1)

            every_batch(act, body)

        @block.vector
        def _(dve):
            def lo_of(b, name, out, hi, hi_sem, nth, bias=None):
                dve.wait_ge(hi_sem, nth)
                src = banks.bank(b, name)[:, 0:out.shape[-1]]
                if bias is None:
                    ins = nc.vector.tensor_tensor(out, src, rounded(hi), ALU.subtract)
                else:
                    ins = nc.vector.scalar_tensor_tensor(out=out, in0=src, scalar=bias, in1=rounded(hi),
                                                         op0=ALU.add, op1=ALU.subtract)
                banks.freed_by(ins, b, name)

            def softmax_max(b, h):
                for i in SOFTMAX_ORDER:
                    if i != 2:
                        dve.wait_ge(scored[S_BANK[i]], b * H + h + 1)
                    nc.vector.tensor_reduce(negm[:, i:i + 1], s_ps[S_BANK[i]][:, S_COL[i]:S_COL[i] + (i + 1) * P],
                                            AX_X, ALU.max, negate=True).then_inc(max_ready, 1)

            def softmax_norm(b, h):
                dve.wait_ge(exp_ready, b * H * TT + (h + 1) * TT)
                nc.vector.reciprocal(rinv[:], rsum[:]).then_inc(rinv_ready, 1)
                dve.wait_ge(rinv_ready, b * H + h + 1)
                for i in SOFTMAX_ORDER:
                    cols = p[:, P_COL[i]:P_COL[i] + (i + 1) * P]
                    nc.vector.tensor_scalar(cols, cols, rinv[:, i:i + 1], None, ALU.mult).then_inc(p_ready, 1)

            def lo_of_x(b, k):
                lo_of(b, f"ln{k}", xT[1][:, k, :], xT[0][:, k, :], xT_hi, (b + 1) * KD + k + 1)

            def lo_of_k(b, h, nb):
                lo_of(b, f"k{h}", kT[1][:], kT[0][:], k_hi, nb * H + h + 1, bias=bk[:, h:h + 1])

            def lo_of_v(b, g, n, nb):
                out, hi = (x[:, g % 2, 2 * n:2 * n + 2].rearrange("p t d -> p (t d)") for x in (v[1], v[0]))
                lo_of(b, f"v{g}_{n}", out, hi, v_hi, nb * H + HG * g + n + 1)

            def norm_before(b):
                nb = b + 1
                norm.wait_inverse(dve, nth_before(nb))
                for i in range(TT):
                    norm.apply(xn[:, i, :], x_tok[:, bass.ds(nb * TT + i, 1), :], i).then_inc(xn_ready, 1)

            def norm_behind(b, follows):
                dve.wait_ge(y_done, b + 1)
                for n in range(2):
                    ins = nc.vector.tensor_tensor(y[:, 2 * n:2 * n + 2, :],
                                                  y_ps[n][:].rearrange("p (t d) -> p t d", d=D),
                                                  bo[:].unsqueeze(1).broadcast_to([P, 2, D]), ALU.add)
                ins.then_inc(y_freed, 1)
                dve.wait_ge(y_freed, b + 1)
                norm.moments(dve, nth_behind(b, follows, B), lambda i: y[:, i, :])
                norm.wait_inverse(dve, nth_behind(b, follows, B))
                for i in range(TT):
                    ins = norm.apply(y[:, i, :], y[:, i, :], i)
                ins.then_inc(y_normed, 1)
                dve.wait_ge(y_normed, b + 1)
                x_b = x_tok[:, bass.ds(b * TT, TT), :]
                nc.vector.tensor_tensor(x_b, x_b, y[:], ALU.add).then_inc(x_updated, 1)

            def body(b, follows):
                first = isinstance(b, int) and b < 0
                for h in range(H if not first else 0):
                    if follows and h + 1 == H:
                        lo_of_x(b, 0)
                        lo_of_x(b, 1)
                    softmax_max(b, h)
                    if h + 1 < H:
                        lo_of_k(b, h + 1, b)
                    softmax_norm(b, h)
                    if h + HG < H:
                        lo_of_v(b, h // HG + 1, h % HG, b)
                    for n in range(3):
                        col, w = PT_COL[T_FILLS[n][0]], (512, 512, 256)[n]
                        lo_of(b, f"t{h}_{n}", pT[1][:, col:col + w], pT[0][:, col:col + w], pT_hi,
                              b * 3 * H + h * 3 + n + 1)
                    if follows and h == H - 4:
                        norm.moments(dve, nth_before(b + 1), lambda i: x_tok[:, bass.ds((b + 1) * TT + i, 1), :])
                    if follows and h == H - 3:
                        norm_before(b)
                if not first:
                    norm_behind(b, follows)
                if first:
                    dve.wait_ge(x_loaded, DMA_INC)
                    norm.moments(dve, 0, lambda i: x_tok[:, i, :])
                    norm_before(b)
                    dve.wait_ge(rows_loaded, 4 * DMA_INC)
                    nc.vector.tensor_scalar(bqs[:], bq[:], float(DH) ** -0.5, None, ALU.mult).then_inc(bqs_ready, 1)
                    lo_of_x(b, 0)
                    lo_of_x(b, 1)
                    for m, (w, k, half) in enumerate(pieces):
                        hi, lo = (x[:, k, half * HALF:(half + 1) * HALF] for x in (wk_s, wv_s)[w])
                        dve.wait_ge(wkv_loaded[m], DMA_INC)
                        nc.vector.tensor_copy(hi, landing[m % len(landing)]).then_inc(wkv_hi, 1)
                        dve.wait_ge(wkv_hi, m + 1)
                        nc.vector.tensor_tensor(lo, landing[m % len(landing)], rounded(hi), ALU.subtract).then_inc(
                            wkv_lo, 1)
                    dve.wait_ge(x_loaded, B * DMA_INC)
                if follows:
                    lo_of_k(b, 0, b + 1)
                    lo_of_v(b, 0, 0, b + 1)
                    lo_of_v(b, 0, 1, b + 1)

            every_batch(dve, body)

        @block.tensor
        def _(pe):
            def project(out, k_lhs, k_rhs):
                for k in range(KD):
                    ins = three_passes(pe, out, k_lhs(k), k_rhs(k), start=(k == 0), stop=(k == KD - 1))
                return ins

            def fill_ln(b, k):
                banks.wait_freed(pe, b, f"ln{k}")
                for i in range(TT):
                    if k == 0:
                        pe.wait_ge(xn_ready, (b + 1) * TT + i + 1)
                    ins = pe.transpose(banks.bank(b, f"ln{k}")[:, i * P:(i + 1) * P],
                                       xn[:, i, k * P:(k + 1) * P], c["ident"][:])
                banks.filled_by(ins)

            def fill_q(b, n):
                if n == 0:
                    for k in range(KD):
                        banks.wait_kept(pe, b, f"ln{k}")
                if n % 2 == 0:
                    pe.wait_ge(wq_lo, (b + 1) * NCHUNK + n // 2 + 1)
                banks.wait_freed(pe, b, f"q{n}")
                col = n % 2 * DH
                banks.filled_by(project(banks.bank(b, f"q{n}")[:],
                                        lambda k: [w[:, n // 2 % SLOTS, k, col:col + DH] for w in wq_s],
                                        lambda k: [x[:, k, :] for x in xT]))

            def fill_k(b, h):
                banks.wait_freed(pe, b, f"k{h}")
                banks.filled_by(project(banks.bank(b, f"k{h}")[:],
                                        lambda k: [w[:, k, h * DH:(h + 1) * DH] for w in wk_s],
                                        lambda k: [x[:, k, :] for x in xT]))

            def fill_v(b, g, n):
                banks.wait_freed(pe, b, f"v{g}_{n}")
                w = HG * DH
                for j in range(2):
                    t = 2 * n + j
                    ins = project(banks.bank(b, f"v{g}_{n}")[:, j * w:(j + 1) * w],
                                  lambda k: [x[:, k, t * P:(t + 1) * P] for x in xT],
                                  lambda k: [x[:, k, g * w:(g + 1) * w] for x in wv_s])
                banks.filled_by(ins)

            def scores(b, h):
                pe.wait_ge(qs_lo, b * H + h + 1)
                if h:
                    banks.wait_kept(pe, b, f"k{h}")
                for i in SOFTMAX_ORDER:
                    w = (i + 1) * P
                    out = s_ps[S_BANK[i]][:, S_COL[i]:S_COL[i] + w]
                    three_passes(pe, out, [q[:, i * P:(i + 1) * P] for q in qs], [k[:, 0:w] for k in kT],
                                 start=True, stop=False)
                    ins = pe.matmul(out[:, i * P:w], c["ident_bf"][:], c["causal_bf"][:], start=False, stop=True)
                    if i != 0:
                        ins.then_inc(scored[S_BANK[i]], 1)

            def transpose_p(b, h):
                pe.wait_ge(p_ready, b * H * TT + (h + 1) * TT)
                for n, tiles in enumerate(T_FILLS):
                    name = f"t{h}_{n}"
                    banks.wait_freed(pe, b, name)
                    base = PT_COL[tiles[0]]
                    for j in tiles:
                        for i in range(j, TT):
                            col = PT_COL[j] - base + (i - j) * P
                            src = P_COL[i] + j * P
                            ins = pe.transpose(banks.bank(b, name)[:, col:col + P], p[:, src:src + P], c["ident"][:])
                    banks.filled_by(ins)

            def fill_o(b, h):
                name = f"o{h}"
                banks.wait_freed(pe, b, name)
                for n in range(3):
                    banks.wait_kept(pe, b, f"t{h}_{n}")
                for j in range(TT):
                    w = T - j * P
                    ins = three_passes(pe, banks.bank(b, name)[:, j * P:T],
                                       [x[:, h // HG % 2, j, h % HG * DH:(h % HG + 1) * DH] for x in v],
                                       [x[:, PT_COL[j]:PT_COL[j] + w] for x in pT], start=(j == 0),
                                       stop=(j == TT - 1))
                banks.filled_by(ins)

            def out_project(b, h):
                if h == 0:
                    pe.wait_ge(norm.var_ready, b * 2 + 1)
                    pe.wait_ge(wo_loaded, DMA_INC)
                banks.wait_kept(pe, b, f"o{h}")
                for i in range(TT):
                    ins = pe.matmul(y_ps[i // 2][:, i % 2 * D:(i % 2 + 1) * D], oT[:, i * P:(i + 1) * P],
                                    wo[:, h, :], start=(h == 0 and i % 2 == 0), stop=(h == H - 1),
                                    skip_group_check=True)
                if h == H - 1:
                    ins.then_inc(y_done, 1)

            def body(b, follows):
                first = isinstance(b, int) and b < 0
                for h in range(H if not first else 0):
                    tail = follows and h + 1 == H
                    if tail:
                        fill_ln(b, 0)
                        fill_ln(b, 1)
                    scores(b, h)
                    if h + 1 < H:
                        fill_k(b, h + 1)
                    if h:
                        fill_o(b, h - 1)
                    if h + HG < H:
                        fill_v(b, h // HG + 1, h % HG)
                    if h:
                        out_project(b, h - 1)
                    if tail:
                        fill_q(b, 0)
                        fill_q(b, 1)
                    transpose_p(b, h)
                if first:
                    fill_ln(b, 0)
                    fill_ln(b, 1)
                    fill_q(b, 0)
                    fill_q(b, 1)
                if follows:
                    fill_q(b, 2)
                    fill_q(b, 3)
                if not first:
                    fill_o(b, H - 1)
                    out_project(b, H - 1)
                if follows:
                    for n in range(4, H):
                        fill_q(b, n)
                    if first:
                        pe.wait_ge(wkv_lo, len(pieces))
                    fill_k(b, 0)
                    fill_v(b, 0, 0)
                    fill_v(b, 0, 1)
                    banks.wait_kept(pe, b, "k0")

            banks.all_free(pe)
            every_batch(pe, body)


def ffn0(nc, a, c, x_tok):
    NF = INTER // P
    fills = [f"ln{k}" for k in range(KD)]
    for n in range(NF):
        fills += [f"up{n}", f"gate{n}"]

    with ExitStack() as ctx:
        def sb(name, shape, dt=F32):
            return ctx.enter_context(nc.sbuf_tensor(name, shape, dt))

        def sem(name):
            return ctx.enter_context(nc.semaphore(name))

        eff = [sb(f"f_eff_{s}", [P, KD, 2 * INTER], F32R) for s in ("hi", "lo")]
        down = [sb(f"f_down_{s}", [P, NF, D], F32R) for s in ("hi", "lo")]
        with ExitStack() as inner:
            def sbi(name, shape, dt=F32):
                return inner.enter_context(nc.sbuf_tensor(name, shape, dt))

            def semi(name):
                return inner.enter_context(nc.semaphore(name))

            hada = sbi("hada", [P, P])
            hada_r = [sbi(f"hada_{s}", [P, P], F32R) for s in ("pos", "neg")]
            wT = sbi("f_wT", [P, KD, 2 * INTER])
            wT_s = [sbi(f"f_wT_{s}", [P, KD, 2 * INTER], F32R) for s in ("hi", "lo")]
            dT = sbi("f_dT", [P, NF, D])
            dT_s = [sbi(f"f_dT_{s}", [P, NF, D], F32R) for s in ("hi", "lo")]
            d_eff = sbi("f_d_eff", [P, NF, D])
            su_ug, su_dp = sbi("su_ug", [P, KD]), sbi("su_dp", [P, NF])
            su_ug_n, su_dp_n = sbi("su_ug_n", [P, KD]), sbi("su_dp_n", [P, NF])
            sc_dp = sbi("sc_dp", [P, D])
            ug_fills = [f"w{k}_{n}" for n in range(4) for k in range(KD)]
            banks = Banks(inner, nc, "fw", ug_fills + [f"d{n}" for n in range(NF)], 8)
            w_loaded, d_loaded, s_loaded = semi("w_loaded"), semi("d_loaded"), semi("s_loaded")
            hada_ready, signs_ready = semi("hada_ready"), semi("signs_ready")
            w_hi, w_lo, d_hi, d_lo = semi("w_hi"), semi("w_lo"), semi("d_hi"), semi("d_lo")
            eff_hi = semi("eff_hi")
            down_hi = semi("down_hi")
            block = inner.enter_context(nc.Block())

            @block.sync
            def _(sp):
                sp.dma_start(hada[:], a["c_hadamard"]).then_inc(s_loaded, DMA_INC)
                sp.dma_start(su_ug[:], a["L0_ffn_SU_ug"]).then_inc(s_loaded, DMA_INC)
                sp.dma_start(su_dp[:], a["L0_ffn_SU_dp"]).then_inc(s_loaded, DMA_INC)
                sp.dma_start(sc_dp[:], a["L0_ffn_Wscale_dp"].broadcast_to([P, D])).then_inc(s_loaded, DMA_INC)
                for n, name in enumerate(("L0_ffn_W_up", "L0_ffn_W_gate")):
                    sp.dma_start(wT[:, :, n * INTER:(n + 1) * INTER],
                                 a[name].rearrange("(k p) n -> p k n", p=P)).then_inc(w_loaded, DMA_INC)
                sp.dma_start(dT[:], a["L0_ffn_W_down"].rearrange("(k p) n -> p k n", p=P)).then_inc(d_loaded, DMA_INC)

            @block.scalar
            def _(act):
                act.wait_ge(s_loaded, 4 * DMA_INC)
                nc.scalar.activation(hada_r[0][:], hada[:], ACT.Copy).then_inc(hada_ready, 1)
                nc.scalar.activation(hada_r[1][:], hada[:], ACT.Copy, scale=-1.0).then_inc(hada_ready, 1)
                act.wait_ge(w_loaded, 2 * DMA_INC)
                nc.scalar.activation(wT_s[0][:, 1], wT[:, 1], ACT.Copy).then_inc(w_hi, 1)
                act.wait_ge(d_loaded, DMA_INC)
                nc.scalar.activation(dT_s[0][:], dT[:], ACT.Copy).then_inc(d_hi, 1)
                act.wait_ge(signs_ready, 2)
                for n in range(4):
                    for k in range(KD):
                        name = f"w{k}_{n}"
                        banks.wait_filled(act, 0, name)
                        nc.scalar.activation(eff[0][:, k, n * 512:(n + 1) * 512], banks.bank(0, name)[:], ACT.Copy,
                                             scale=su_ug_n[:, k:k + 1]).then_inc(eff_hi, 1)
                for n in range(NF):
                    banks.wait_kept(act, 0, f"d{n}")
                    nc.scalar.activation(down[0][:, n], d_eff[:, n], ACT.Copy).then_inc(down_hi, 1)

            @block.gpsimd
            def _(pool):
                for n in range(NF):
                    pool.wait_ge(down_hi, n + 1)
                    nc.gpsimd.tensor_tensor(down[1][:, n], d_eff[:, n], rounded(down[0][:, n]), ALU.subtract)

            @block.vector
            def _(dve):
                dve.wait_ge(s_loaded, 4 * DMA_INC)
                nc.vector.tensor_scalar(su_ug_n[:], su_ug[:], float(D) ** -0.5, None, ALU.mult).then_inc(
                    signs_ready, 1)
                nc.vector.tensor_scalar(su_dp_n[:], su_dp[:], float(INTER) ** -0.5, None, ALU.mult).then_inc(
                    signs_ready, 1)
                dve.wait_ge(w_loaded, 2 * DMA_INC)
                nc.vector.tensor_copy(wT_s[0][:, 0], wT[:, 0]).then_inc(w_lo, 1)
                dve.wait_ge(w_lo, 1)
                nc.vector.tensor_tensor(wT_s[1][:, 0], wT[:, 0], rounded(wT_s[0][:, 0]), ALU.subtract).then_inc(w_lo, 1)
                dve.wait_ge(w_hi, 1)
                nc.vector.tensor_tensor(wT_s[1][:, 1], wT[:, 1], rounded(wT_s[0][:, 1]), ALU.subtract).then_inc(w_lo, 1)
                dve.wait_ge(d_hi, 1)
                nc.vector.tensor_tensor(dT_s[1][:], dT[:], rounded(dT_s[0][:]), ALU.subtract).then_inc(d_lo, 1)
                dve.wait_ge(signs_ready, 2)
                for n in range(4):
                    for k in range(KD):
                        name = f"w{k}_{n}"
                        dve.wait_ge(eff_hi, n * KD + k + 1)
                        banks.freed_by(nc.vector.scalar_tensor_tensor(
                            out=eff[1][:, k, n * 512:(n + 1) * 512], in0=banks.bank(0, name)[:],
                            scalar=su_ug_n[:, k:k + 1], in1=rounded(eff[0][:, k, n * 512:(n + 1) * 512]),
                            op0=ALU.mult, op1=ALU.subtract), 0, name)
                for n in range(NF):
                    banks.wait_filled(dve, 0, f"d{n}")
                    banks.freed_by(nc.vector.scalar_tensor_tensor(
                        out=d_eff[:, n], in0=banks.bank(0, f"d{n}")[:, 0:D], scalar=su_dp_n[:, n:n + 1], in1=sc_dp[:],
                        op0=ALU.mult, op1=ALU.mult), 0, f"d{n}")

            @block.tensor
            def _(pe):
                def transformed(name, out, sources, row, tiles):
                    banks.wait_freed(pe, 0, name)
                    for j in range(tiles):
                        sign = hada_r[bin(row & j).count("1") % 2]
                        for n, half in enumerate(sources):
                            ins = pe.matmul(out, sign[:], half(j), start=(j == 0 and n == 0),
                                            stop=(j == tiles - 1 and n == 1))
                    banks.filled_by(ins)

                banks.all_free(pe)
                pe.wait_ge(hada_ready, 2)
                pe.wait_ge(w_lo, 3)
                for n in range(4):
                    for k in range(KD):
                        name = f"w{k}_{n}"
                        transformed(name, banks.bank(0, name)[:],
                                    [lambda j, w=w: w[:, j, n * 512:(n + 1) * 512] for w in wT_s], k, KD)
                pe.wait_ge(d_lo, 1)
                for n in range(NF):
                    name = f"d{n}"
                    transformed(name, banks.bank(0, name)[:, 0:D], [lambda j, w=w: w[:, j, :] for w in dT_s], n, NF)

        xT = [sb(f"f_xT_{s}", [P, KD, T], F32R) for s in ("hi", "lo")]
        xn = sb("f_xn", [P, TT, D])
        y = sb("f_y", [P, TT, D])
        gate = sb("f_gate", [P, 2, T])
        h = sb("f_h", [P, 2, T])
        h_s = [sb(f"f_h_{s}", [P, 2, T], F32R) for s in ("hi", "lo")]
        su, sg = sb("f_scale_up", [P, NF]), sb("f_scale_gate", [P, NF])
        banks = Banks(ctx, nc, "f", fills, 6)
        y_ps = [ctx.enter_context(nc.psum_tensor(f"f_y_ps{n}", [P, 512], F32)) for n in range(2)]
        norm = Norm(ctx, nc, c, "f")
        scales = sem("f_scales_loaded")
        xn_ready, xT_hi = sem("f_xn_ready"), sem("f_xT_hi_ready")
        h_hi, h_lo = sem("f_h_hi_ready"), sem("f_h_lo_ready")
        y_done, y_freed, x_updated = sem("f_y_done"), sem("f_y_freed"), sem("f_x_updated")
        block = ctx.enter_context(nc.Block())

        @block.sync
        def _(sp):
            sp.dma_start(su[:], a["L0_ffn_Wscale_up"]).then_inc(scales, DMA_INC)
            sp.dma_start(sg[:], a["L0_ffn_Wscale_gate"]).then_inc(scales, DMA_INC)

        @block.gpsimd
        def _(pool):
            with pool.Fori(0, B) as b:
                norm.inverse(pool, b * 2)
                for n in range(NF):
                    pool.wait_ge(h_hi, b * NF + n + 1)
                    nc.gpsimd.tensor_tensor(h_s[1][:, n % 2], h[:, n % 2], rounded(h_s[0][:, n % 2]),
                                            ALU.subtract).then_inc(h_lo, 1)
                norm.inverse(pool, b * 2 + 1)

        @block.scalar
        def _(act):
            def hi_of_h(b, n):
                banks.wait_kept(act, b, f"up{n}")
                nc.scalar.activation(h_s[0][:, n % 2], h[:, n % 2], ACT.Copy).then_inc(h_hi, 1)

            act.wait_ge(scales, 2 * DMA_INC)
            with act.Fori(0, B) as b:
                for k in range(KD):
                    banks.wait_filled(act, b, f"ln{k}")
                    nc.scalar.activation(xT[0][:, k, :], banks.bank(b, f"ln{k}")[:], ACT.Copy).then_inc(xT_hi, 1)
                for n in range(NF):
                    banks.wait_filled(act, b, f"gate{n}")
                    banks.freed_by(nc.scalar.activation(gate[:, n % 2], banks.bank(b, f"gate{n}")[:], ACT.Silu,
                                                        scale=sg[:, n:n + 1]), b, f"gate{n}")
                    hi_of_h(b, n)

        @block.vector
        def _(dve):
            dve.wait_ge(scales, 2 * DMA_INC)
            with dve.Fori(0, B) as b:
                norm.moments(dve, b * 2, lambda i: x_tok[:, bass.ds(b * TT + i, 1), :])
                norm.wait_inverse(dve, b * 2)
                for i in range(TT):
                    norm.apply(xn[:, i, :], x_tok[:, bass.ds(b * TT + i, 1), :], i).then_inc(xn_ready, 1)
                for k in range(KD):
                    dve.wait_ge(xT_hi, b * KD + k + 1)
                    banks.freed_by(nc.vector.tensor_tensor(xT[1][:, k, :], banks.bank(b, f"ln{k}")[:],
                                                           rounded(xT[0][:, k, :]), ALU.subtract), b, f"ln{k}")
                for n in range(NF):
                    banks.wait_filled(dve, b, f"up{n}")
                    banks.wait_kept(dve, b, f"gate{n}")
                    if n >= 2:
                        dve.wait_ge(h_lo, b * NF + n - 1)
                    ins = nc.vector.scalar_tensor_tensor(out=h[:, n % 2], in0=banks.bank(b, f"up{n}")[:],
                                                         scalar=su[:, n:n + 1], in1=gate[:, n % 2], op0=ALU.mult,
                                                         op1=ALU.mult)
                    banks.freed_by(ins, b, f"up{n}")
                dve.wait_ge(y_done, b + 1)
                norm.moments(dve, b * 2 + 1, lambda i: y_ps[i // 2][:, i % 2 * D:(i % 2 + 1) * D])
                norm.wait_inverse(dve, b * 2 + 1)
                for i in range(TT):
                    ins = norm.apply(y[:, i, :], y_ps[i // 2][:, i % 2 * D:(i % 2 + 1) * D], i)
                ins.then_inc(y_freed, 1)
                dve.wait_ge(y_freed, b + 2)
                x_b = x_tok[:, bass.ds(b * TT, TT), :]
                nc.vector.tensor_tensor(x_b, x_b, y[:], ALU.add).then_inc(x_updated, 1)
                dve.wait_ge(x_updated, b + 1)

        @block.tensor
        def _(pe):
            def project_down(b, n):
                pe.wait_ge(h_lo, b * NF + n + 1)
                for i in range(TT):
                    ins = three_passes(pe, y_ps[i // 2][:, i % 2 * D:(i % 2 + 1) * D],
                                       [x[:, n % 2, i * P:(i + 1) * P] for x in h_s], [w[:, n, :] for w in down],
                                       start=(n == 0 and i % 2 == 0), stop=(n == NF - 1), skip_group_check=True)
                return ins

            banks.all_free(pe)
            pe.sem_inc(y_freed, 1)
            with pe.Fori(0, B) as b:
                for k in range(KD):
                    banks.wait_freed(pe, b, f"ln{k}")
                    for i in range(TT):
                        if k == 0:
                            pe.wait_ge(xn_ready, b * TT + i + 1)
                        ins = pe.transpose(banks.bank(b, f"ln{k}")[:, i * P:(i + 1) * P], xn[:, i, k * P:(k + 1) * P],
                                           c["ident"][:])
                    banks.filled_by(ins)
                for k in range(KD):
                    banks.wait_kept(pe, b, f"ln{k}")
                for n in range(NF):
                    for name, col in ((f"up{n}", n * P), (f"gate{n}", INTER + n * P)):
                        banks.wait_freed(pe, b, name)
                        for k in range(KD):
                            ins = three_passes(pe, banks.bank(b, name)[:], [w[:, k, col:col + P] for w in eff],
                                               [x[:, k, :] for x in xT], start=(k == 0), stop=(k == KD - 1))
                        banks.filled_by(ins)
                    if n == 1:
                        pe.wait_ge(y_freed, b + 1)
                    if n:
                        project_down(b, n - 1)
                project_down(b, NF - 1).then_inc(y_done, 1)


def attention1(nc, a, c, x_tok):
    PAD = WINDOW
    NS, NB = 4, H1 // 2

    def name_of(kind, tile):
        return f"{kind}{'+' * tile[0]}{tile[1]}"

    def steps(b, follows):
        if isinstance(b, int) and b < 0:
            return [dict(ln=(1, 0)), dict(ln=(1, 1), qk=(1, 0)), dict(ln=(1, 2), qk=(1, 1), s=(1, 0))]
        out = []
        for t in range(1, TT + 1):
            ahead = [(0, n) if n < TT else (1, n - TT) for n in (t + 2, t + 1, t)]
            step = {kind: tile for kind, tile in zip(("ln", "qk", "s"), ahead) if follows or not tile[0]}
            step["o"] = (0, t - 1)
            if t >= 2:
                step["y"] = (0, t - 2)
            out.append(step)
        return out + [dict(y=(0, TT - 1))]

    def fills_of(b, follows):
        names = []
        for step in steps(b, follows):
            if "qk" in step:
                names += [name_of("qk", step["qk"])]
            if "o" in step:
                names += [name_of(f"p{n}_", step["o"]) for n in range(NS)]
            if "ln" in step:
                names += [name_of("ln", step["ln"])]
            if "s" in step:
                names += [name_of(f"s{n}_", step["s"]) for n in range(NS)]
            if "y" in step:
                names += [name_of("oT", step["y"])]
            if "o" in step:
                names += [name_of("o", step["o"])]
            if "qk" in step:
                names += [name_of(kind, step["qk"]) for kind in ("ta", "tb", "tk")]
        return names

    with ExitStack() as ctx:
        def sb(name, shape, dt=F32):
            return ctx.enter_context(nc.sbuf_tensor(name, shape, dt))

        def sem(name):
            return ctx.enter_context(nc.semaphore(name))

        QK = D + DH1
        w_raw = sb("g_w_raw", [P, KD, QK + DH1])
        w_s = [sb(f"g_w_{s}", [P, KD, QK + DH1], F32R) for s in ("hi", "lo")]
        wo, bo = sb("g_wo", [P, KD, D]), sb("g_bo", [P, D])
        rot_c, rot_s = sb("g_cos", [P, TT, ROPE]), sb("g_sin", [P, TT, ROPE])
        mask_raw = sb("g_mask_raw", [P, 2, P])
        mask = sb("g_mask", [P, 2, NS, P], BF16)
        xT = [sb(f"g_xT_{s}", [P, KD, PAD + T], F32R) for s in ("hi", "lo")]
        xn, y = sb("g_xn", [P, TT, D]), sb("g_y", [P, TT, D])
        qk = sb("g_qk", [P, H1 + 1, DH1])
        turned = sb("g_turned", [P, H1 + 1, ROPE])
        q_st = sb("g_q_st", [P, H1, 4, DH1])
        k_st = sb("g_k_st", [P, 2, 4, DH1])
        qT = sb("g_qT", [P, 2, 2, NB, 64], F32R)
        kT = sb("g_kT", [P, PAD + T], F32R)
        vw = sb("g_vw", [P, 2 * TT, DH1 + 1])
        p = sb("g_p", [P, NS, 4 * P])
        pT = sb("g_pT", [P, NS, 4 * P])
        top = sb("g_top", [P, NS, 4])
        o = sb("g_o", [P, H1, DH1])
        oT = sb("g_oT", [P, KD, P])
        rinv = sb("g_rinv", [P, H1])
        banks = Banks(ctx, nc, "g", fills_of(0, True), 6, before=fills_of(-1, True), last=fills_of(B - 1, False),
                      rounds=B)
        y_ps = [ctx.enter_context(nc.psum_tensor(f"g_y_ps{n}", [P, 512], F32)) for n in range(2)]
        norm = Norm(ctx, nc, c, "g")
        loaded, w_ready, w_hi, mask_ready, pads = (sem(f"g_{s}") for s in (
            "loaded", "w_ready", "w_hi", "mask_ready", "pads_ready"))
        xn_ready, xT_hi = sem("g_xn_ready"), sem("g_xT_hi_ready")
        rotated, qk_copied, keys_ready = sem("g_rotated"), sem("g_qk_copied"), sem("g_keys_ready")
        st_hi, st_ready = sem("g_st_hi_ready"), sem("g_st_ready")
        top_ready, exp_ready = sem("g_top_ready"), sem("g_exp_ready")
        rinv_ready = sem("g_rinv_ready")
        y_done, y_freed, y_normed, x_updated = (sem(f"g_{s}") for s in ("y_done", "y_freed", "y_normed", "x_updated"))
        block = ctx.enter_context(nc.Block())

        @block.sync
        def _(sp):
            for col, w, name in ((0, D, "L1_attn_Wq"), (D, DH1, "L1_attn_Wk"), (QK, DH1, "L1_attn_Wv")):
                sp.dma_start(w_raw[:, :, col:col + w], a[name].rearrange("(k p) n -> p k n", p=P)).then_inc(
                    loaded, DMA_INC)
            sp.dma_start(wo[:], a["L1_attn_Wo"].rearrange("(k p) n -> p k n", p=P)).then_inc(loaded, DMA_INC)
            sp.dma_start(bo[:], a["L1_attn_bo"].broadcast_to([P, D])).then_inc(loaded, DMA_INC)
            sp.dma_start(rot_c[:], a["c_cos"]).then_inc(loaded, DMA_INC)
            sp.dma_start(rot_s[:], a["c_sin"]).then_inc(loaded, DMA_INC)
            sp.dma_start(mask_raw[:], a["c_window"]).then_inc(loaded, DMA_INC)

        @block.gpsimd
        def _(pool):
            nc.gpsimd.memset(kT[:, 0:PAD].bitcast(F32), 0.0).then_inc(pads, 1)
            for x in xT:
                nc.gpsimd.memset(x[:, :, 0:PAD].bitcast(F32), 0.0).then_inc(pads, 1)
            nc.gpsimd.memset(vw[:], 1.0).then_inc(pads, 1)

            def body(b, follows):
                if follows:
                    norm.inverse(pool, nth_before(b + 1))
                if not isinstance(b, int) or b >= 0:
                    norm.inverse(pool, nth_behind(b, follows, B))

            every_batch(pool, body)

        @block.scalar
        def _(act):
            act.wait_ge(loaded, 8 * DMA_INC)
            nc.scalar.activation(w_s[0][:], w_raw[:], ACT.Copy).then_inc(w_hi, 1)
            for v in range(2):
                nc.scalar.activation(mask[:, v], mask_raw[:, v].unsqueeze(1).broadcast_to([P, NS, P]),
                                     ACT.Copy).then_inc(mask_ready, 1)
            act.wait_ge(pads, 4)

            def hi_of_x(b, tile):
                f, t = tile
                banks.wait_filled(act, b, name_of("ln", tile))
                nc.scalar.activation(xT[0][:, :, PAD + t * P:PAD + (t + 1) * P],
                                     banks.bank(b, name_of("ln", tile))[:, 0:D].rearrange("p (k t) -> p k t", k=KD),
                                     ACT.Copy).then_inc(xT_hi, 1)

            def plain_qk(b, tile):
                f, t = tile
                name = name_of("qk", tile)
                banks.wait_filled(act, b, name)
                src = banks.bank(b, name)[:, 0:QK].rearrange("p (h d) -> p h d", d=DH1)
                if not (isinstance(b, int) and (b + f) * TT + t == 0):
                    act.wait_ge(st_ready, (b + f) * TT + t)
                nc.scalar.activation(qk[:, :, ROPE:DH1], src[:, :, ROPE:DH1], ACT.Copy).then_inc(qk_copied, 1)

            def keep_transposed(b, tile):
                t = tile[1]
                for n, kind in enumerate(("ta", "tb")):
                    name = name_of(kind, tile)
                    banks.wait_filled(act, b, name)
                    banks.freed_by(nc.scalar.activation(
                        qT[:, t % 2, :, 4 * n:4 * n + 4, :].rearrange("p s n q -> p n s q"),
                        banks.bank(b, name)[:].rearrange("p (n s q) -> p n s q", s=2, q=64), ACT.Copy), b, name)
                name = name_of("tk", tile)
                banks.wait_filled(act, b, name)
                bank = banks.bank(b, name)
                nc.scalar.activation(kT[:, PAD + t * P:PAD + (t + 1) * P], bank[:, 0:P], ACT.Copy).then_inc(
                    keys_ready, 1)
                banks.freed_by(nc.scalar.activation(
                    vw[:, 2 * t:2 * t + 2, 0:DH1], bank[:, P:P + 2 * DH1].rearrange("p (w d) -> p w d", d=DH1),
                    ACT.Copy), b, name)

            def exps(b, tile):
                for n in range(NS):
                    banks.wait_kept(act, b, name_of(f"s{n}_", tile))
                    nc.scalar.activation(p[:, n], p[:, n], ACT.Exp, scale=float(DH1) ** -0.5).then_inc(exp_ready, 1)

            def keep_pT(b, tile):
                for n in range(NS):
                    name = name_of(f"p{n}_", tile)
                    banks.wait_filled(act, b, name)
                    banks.freed_by(nc.scalar.activation(pT[:, n], banks.bank(b, name)[:], ACT.Copy), b, name)

            def keep_oT(b, tile):
                name = name_of("oT", tile)
                banks.wait_filled(act, b, name)
                banks.freed_by(nc.scalar.activation(oT[:].rearrange("p k t -> p (k t)"),
                                                    banks.bank(b, name)[:, 0:D], ACT.Copy), b, name)

            def body(b, follows):
                for step in steps(b, follows):
                    for kind, stage in (("qk", plain_qk), ("o", keep_pT), ("ln", hi_of_x), ("y", keep_oT),
                                        ("s", exps), ("qk", keep_transposed)):
                        if kind in step:
                            stage(b, step[kind])

            every_batch(act, body)

        @block.vector
        def _(dve):
            dve.wait_ge(w_hi, 1)
            nc.vector.tensor_tensor(w_s[1][:], w_raw[:], rounded(w_s[0][:]), ALU.subtract).then_inc(w_ready, 1)

            def rotate_and_stack(b, tile):
                f, t = tile
                nth = (b + f) * TT + t + 1
                name = name_of("qk", tile)
                dve.wait_ge(qk_copied, nth)
                src = banks.bank(b, name)[:, 0:QK].rearrange("p (h d) -> p h d", d=DH1)
                half = ROPE // 2

                def table(tab, lo, hi):
                    return tab[:, t, lo:hi].unsqueeze(1).broadcast_to([P, H1 + 1, hi - lo])

                nc.vector.tensor_tensor(qk[:, :, 0:ROPE], src[:, :, 0:ROPE], table(rot_c, 0, ROPE),
                                        ALU.mult)
                nc.vector.tensor_tensor(turned[:, :, 0:half], src[:, :, half:ROPE], table(rot_s, 0, half), ALU.mult)
                ins = nc.vector.tensor_tensor(turned[:, :, half:ROPE], src[:, :, 0:half], table(rot_s, half, ROPE),
                                              ALU.mult)
                banks.freed_by(ins, b, name)
                banks.wait_kept(dve, b, name)
                nc.vector.tensor_tensor(qk[:, :, 0:ROPE], qk[:, :, 0:ROPE], turned[:], ALU.add).then_inc(rotated, 1)
                dve.wait_ge(rotated, nth)
                q = qk[:, 0:H1, :].unsqueeze(2).broadcast_to([P, H1, 2, DH1])
                k = qk[:, H1:H1 + 1, :].broadcast_to([P, 2, DH1])
                nc.vector.tensor_copy(q_st[:, :, 0:2].bitcast(F32R), q)
                for r in (0, 2):
                    ins = nc.vector.tensor_copy(k_st[:, :, r].bitcast(F32R), k)
                ins.then_inc(st_hi, 1)
                dve.wait_ge(st_hi, nth)
                nc.vector.tensor_tensor(q_st[:, :, 2:4], q, q_st[:, :, 0:2], ALU.subtract)
                for r in (1, 3):
                    ins = nc.vector.tensor_tensor(k_st[:, :, r], k, k_st[:, :, r - 1], ALU.subtract)
                ins.then_inc(st_ready, 1)

            def shift_scores(b, tile):
                f, t = tile
                for n in range(NS):
                    nth = ((b + f) * TT + t) * NS + n + 1
                    name = name_of(f"s{n}_", tile)
                    banks.wait_filled(dve, b, name)
                    s = banks.bank(b, name)[:].rearrange("p (m k) -> p m k", k=P)
                    nc.vector.tensor_reduce(top[:, n], s, AX_X, ALU.max).then_inc(top_ready, 1)
                    dve.wait_ge(top_ready, nth)
                    banks.freed_by(nc.vector.tensor_tensor(
                        p[:, n].rearrange("p (m k) -> p m k", k=P), s,
                        top[:, n].unsqueeze(2).broadcast_to([P, 4, P]), ALU.subtract), b, name)

            def norm_o(b, tile):
                t = tile[1]
                name = name_of("o", tile)
                banks.wait_filled(dve, b, name)
                src = banks.bank(b, name)[:, 0:H1 * (DH1 + 1)].rearrange("p (h d) -> p h d", d=DH1 + 1)
                nc.vector.reciprocal(rinv[:], src[:, :, DH1]).then_inc(rinv_ready, 1)
                dve.wait_ge(rinv_ready, b * TT + t + 1)
                banks.freed_by(nc.vector.tensor_tensor(o[:], src[:, :, 0:DH1],
                                                       rinv[:].unsqueeze(2).broadcast_to([P, H1, DH1]), ALU.mult),
                               b, name)

            def lo_of_x(b, tile):
                f, t = tile
                dve.wait_ge(xT_hi, (b + f) * TT + t + 1)
                cols = slice(PAD + t * P, PAD + (t + 1) * P)
                banks.freed_by(nc.vector.tensor_tensor(
                    xT[1][:, :, cols], banks.bank(b, name_of("ln", tile))[:, 0:D].rearrange("p (k t) -> p k t", k=KD),
                    rounded(xT[0][:, :, cols]), ALU.subtract), b, name_of("ln", tile))

            def norm_before(nb):
                norm.wait_inverse(dve, nth_before(nb))
                for i in range(TT):
                    norm.apply(xn[:, i, :], x_tok[:, bass.ds(nb * TT + i, 1), :], i).then_inc(xn_ready, 1)

            def norm_behind(b, follows):
                nth = nth_behind(b, follows, B)
                dve.wait_ge(y_done, b + 1)
                for n in range(2):
                    ins = nc.vector.tensor_tensor(y[:, 2 * n:2 * n + 2, :], y_ps[n][:].rearrange("p (t d) -> p t d", d=D),
                                                  bo[:].unsqueeze(1).broadcast_to([P, 2, D]), ALU.add)
                ins.then_inc(y_freed, 1)
                dve.wait_ge(y_freed, b + 2)
                norm.moments(dve, nth, lambda i: y[:, i, :])
                norm.wait_inverse(dve, nth)
                for i in range(TT):
                    ins = norm.apply(y[:, i, :], y[:, i, :], i)
                ins.then_inc(y_normed, 1)
                dve.wait_ge(y_normed, b + 1)
                x_b = x_tok[:, bass.ds(b * TT, TT), :]
                nc.vector.tensor_tensor(x_b, x_b, y[:], ALU.add).then_inc(x_updated, 1)

            def body(b, follows):
                first = isinstance(b, int) and b < 0
                if first:
                    norm.moments(dve, 0, lambda i: x_tok[:, i, :])
                    norm_before(0)
                for t, step in enumerate(steps(b, follows), 1):
                    if "y" in step:
                        norm_o(b, step["y"])
                    for kind, stage in (("qk", rotate_and_stack), ("ln", lo_of_x)):
                        if kind in step:
                            stage(b, step[kind])
                    if follows and not first and t == 1:
                        norm.moments(dve, nth_before(b + 1), lambda i: x_tok[:, bass.ds((b + 1) * TT + i, 1), :])
                    if "s" in step:
                        shift_scores(b, step["s"])
                    if follows and not first and t == 1:
                        norm_before(b + 1)
                if not first:
                    norm_behind(b, follows)

            every_batch(dve, body)

        @block.tensor
        def _(pe):
            def transpose_x(b, tile):
                f, t = tile
                name = name_of("ln", tile)
                banks.wait_freed(pe, b, name)
                pe.wait_ge(xn_ready, (b + f) * TT + t + 1)
                for k in range(KD):
                    ins = pe.transpose(banks.bank(b, name)[:, k * P:(k + 1) * P], xn[:, t, k * P:(k + 1) * P],
                                       c["ident"][:])
                banks.filled_by(ins)

            def project_qk(b, tile):
                t = tile[1]
                name = name_of("qk", tile)
                banks.wait_freed(pe, b, name)
                if isinstance(b, int) and b < 0:
                    banks.wait_kept(pe, b, name_of("ln", tile))
                for k in range(KD):
                    ins = three_passes(pe, banks.bank(b, name)[:, 0:QK],
                                       [x[:, k, PAD + t * P:PAD + (t + 1) * P] for x in xT],
                                       [w[:, k, 0:QK] for w in w_s], start=(k == 0), stop=(k == KD - 1))
                banks.filled_by(ins)

            def transpose_qk(b, tile):
                f, t = tile
                pe.wait_ge(st_ready, (b + f) * TT + t + 1)
                for n, kind in enumerate(("ta", "tb")):
                    name = name_of(kind, tile)
                    banks.wait_freed(pe, b, name)
                    for m in range(4):
                        two = q_st[:, 8 * n + 2 * m:8 * n + 2 * m + 2].rearrange("p h r d -> p (h r d)")
                        ins = pe.transpose(banks.bank(b, name)[:, m * P:(m + 1) * P], two, c["ident"][:])
                    banks.filled_by(ins)
                name = name_of("tk", tile)
                banks.wait_freed(pe, b, name)
                pe.transpose(banks.bank(b, name)[:, 0:P], k_st[:].rearrange("p h r d -> p (h r d)"), c["ident"][:])
                for w in range(2 * t, 2 * t + 2):
                    col = P + (w - 2 * t) * DH1
                    for k in range(KD):
                        ins = three_passes(pe, banks.bank(b, name)[:, col:col + DH1],
                                           [x[:, k, w * 64:w * 64 + P] for x in xT],
                                           [ww[:, k, QK:QK + DH1] for ww in w_s], start=(k == 0),
                                           stop=(k == KD - 1))
                banks.filled_by(ins)

            def scores(b, tile):
                f, t = tile
                pe.wait_ge(keys_ready, (b + f) * TT + t + 1)
                for n in range(NS):
                    half, odd = n // 2, n % 2
                    w = 2 * t + half
                    name = name_of(f"s{n}_", tile)
                    banks.wait_freed(pe, b, name)
                    rows = slice(64 * odd, 64 * odd + 64)
                    pe.matmul(banks.bank(b, name)[:], c["ident_bf"][:],
                              mask[:, min(w, 1)].rearrange("p m k -> p (m k)"), start=True, stop=False)
                    for m in range(4):
                        ins = pe.matmul(banks.bank(b, name)[:, m * P:(m + 1) * P],
                                        qT[rows, t % 2, half, 2 * m:2 * m + 2, :].rearrange("p n q -> p (n q)"),
                                        kT[rows, w * 64:w * 64 + P], start=False, stop=(m == 3))
                    banks.filled_by(ins)

            def transpose_p(b, tile):
                f, t = tile
                for n in range(NS):
                    name = name_of(f"p{n}_", tile)
                    pe.wait_ge(exp_ready, (b * TT + t) * NS + n + 1)
                    banks.wait_freed(pe, b, name)
                    for m in range(4):
                        ins = pe.transpose(banks.bank(b, name)[:, m * P:(m + 1) * P], p[:, n, m * P:(m + 1) * P],
                                           c["ident"][:])
                    banks.filled_by(ins)

            def attend(b, tile):
                t = tile[1]
                name = name_of("o", tile)
                banks.wait_freed(pe, b, name)
                for n in range(NS):
                    banks.wait_kept(pe, b, name_of(f"p{n}_", tile))
                    for m in range(4):
                        col = (n * 4 + m) * (DH1 + 1)
                        ins = pe.matmul(banks.bank(b, name)[:, col:col + DH1 + 1], pT[:, n, m * P:(m + 1) * P],
                                        vw[:, 2 * t + n // 2, :], start=True, stop=True)
                banks.filled_by(ins)

            def transpose_o(b, tile):
                name = name_of("oT", tile)
                banks.wait_freed(pe, b, name)
                banks.wait_kept(pe, b, name_of("o", tile))
                for k in range(KD):
                    ins = pe.transpose(banks.bank(b, name)[:, k * P:(k + 1) * P],
                                       o[:].rearrange("p h d -> p (h d)")[:, k * P:(k + 1) * P], c["ident"][:])
                banks.filled_by(ins)

            def out_project(b, tile):
                t = tile[1]
                banks.wait_kept(pe, b, name_of("oT", tile))
                if t == 0:
                    pe.wait_ge(y_freed, b + 1)
                for half in range(2):
                    for two in range(2):
                        ins = pe.matmul(y_ps[t // 2][64 * half:64 * half + 64, t % 2 * D:(t % 2 + 1) * D],
                                        oT[:, half, 64 * two:64 * two + 64], wo[:, two, :], start=(two == 0),
                                        stop=(two == 1))
                if t == TT - 1:
                    ins.then_inc(y_done, 1)

            def body(b, follows):
                for step in steps(b, follows):
                    for kind, stage in (("qk", project_qk), ("o", transpose_p), ("ln", transpose_x), ("s", scores),
                                        ("y", transpose_o), ("o", attend), ("y", out_project), ("qk", transpose_qk)):
                        if kind in step:
                            stage(b, step[kind])

            banks.all_free(pe)
            pe.sem_inc(y_freed, 1)
            pe.wait_ge(w_ready, 1)
            pe.wait_ge(mask_ready, 2)
            every_batch(pe, body)


def experts(nc, a, c, x_tok, out):
    E1 = E + 1
    ROWS = E * NT
    first = [f"ln{i}" for i in range(TT)] + ["logits"]
    main = []
    for e in range(E1 + 1):
        main += [f"a{e}", f"b{e}"] * (e < E1) + [f"y{e - 1}_0", f"y{e - 1}_1"] * (e > 0)

    with ExitStack() as ctx:
        def sb(name, shape, dt=F32):
            return ctx.enter_context(nc.sbuf_tensor(name, shape, dt))

        def sem(name):
            return ctx.enter_context(nc.semaphore(name))

        w1_s = [sb(f"m_w1_{s}", [P, KD, E1, 2 * P], F32R) for s in ("hi", "lo")]
        w2_s = [sb(f"m_w2_{s}", [P, E1, D], F32R) for s in ("hi", "lo")]
        xT = [sb(f"m_xT_{s}", [P, KD, B * T], F32R) for s in ("hi", "lo")]
        w_tok = sb("m_w_tok", [P, E, NT])

        with ExitStack() as inner:
            def sbi(name, shape, dt=F32):
                return inner.enter_context(nc.sbuf_tensor(name, shape, dt))

            def semi(name):
                return inner.enter_context(nc.semaphore(name))

            w1 = sbi("m_w1", [P, KD, E1, 2 * P])
            w2 = sbi("m_w2", [P, E1, D])
            gw = sbi("m_gw", [P, KD, E1])
            gw_s = [sbi(f"m_gw_{s}", [P, KD, E1], F32R) for s in ("hi", "lo")]
            bias = sbi("m_bias", [P, E])
            below = sbi("m_below", [P, E, E])
            same, before = sbi("m_same", [P, ROWS]), sbi("m_before", [P, ROWS])
            units, steps = sbi("m_units", [P, DIGITS], I32), sbi("m_steps", [P, DIGITS, WAYS], I32)
            xn = sbi("m_xn", [P, TT, D])
            xT_now = [sbi(f"m_xT_now_{s}", [P, KD, T], F32R) for s in ("hi", "lo")]
            logits = sbi("m_logits", [P, E, NT])
            aff = sbi("m_aff", [P, E, NT])
            more, ties = sbi("m_more", [P, NT, E, E]), sbi("m_ties", [P, NT, E, E])
            rank, off = sbi("m_rank", [P, E, NT]), sbi("m_off", [P, E, NT])
            score = sbi("m_score", [P, E, NT])
            s_row, gt, eq, upto = (sbi(f"m_{s}", [P, P]) for s in ("s_row", "gt", "eq", "upto"))
            zeros = sbi("m_zeros", [P, P])
            found, step = (sbi(f"m_{s}", [P, 1], I32) for s in ("found", "step"))
            cand = sbi("m_cand", [P, WAYS], I32)
            unused = sbi("m_unused", [P, WAYS, P])
            reached = sbi("m_reached", [P, WAYS])
            counts, digit = sbi("m_counts", [P, WAYS]), sbi("m_digit", [P, 1])
            n_gt, n_eq, room = (sbi(f"m_{s}", [P, 1]) for s in ("n_gt", "n_eq", "room"))
            banks = Banks(inner, nc, "n", first, 5)
            sel_ps = [inner.enter_context(nc.psum_tensor(f"sel{n}", [P, 512], F32)) for n in range(3)]
            norm = Norm(inner, nc, c, "n")
            loaded, w_hi, gw_hi, gw_ready = (semi(f"n_{s}") for s in ("loaded", "w_hi", "gw_hi", "gw_ready"))
            zeroed = semi("n_zeroed")
            xn_ready, xT_hi = semi("n_xn_ready"), semi("n_xT_hi_ready")
            exp_ready = semi("n_exp_ready")
            searched = semi("n_search_step")
            chain = semi("n_selection_step")
            score_ready, score_t = semi("n_score_ready"), semi("n_score_transposed")
            counted, summed = semi("n_counted"), semi("n_summed")
            totals_asked, totals = semi("n_totals_asked"), semi("n_totals")
            weights_ready, weights_t = semi("n_weights_ready"), semi("n_weights_transposed")
            block = inner.enter_context(nc.Block())

            @block.sync
            def _(sp):
                for dst, src in ((gw, "L1_ffn_gate_w"), (bias, "L1_ffn_expert_bias"), (below, "c_below"),
                                 (same, "c_same"), (before, "c_before"), (units, "c_units"), (steps, "c_steps"),
                                 (w1, "L1_ffn_w1"), (w2, "L1_ffn_w2")):
                    ap = a[src]
                    if src == "L1_ffn_expert_bias":
                        ap = ap.broadcast_to([P, E])
                    sp.dma_start(dst[:], ap).then_inc(loaded, DMA_INC)

            @block.gpsimd
            def _(pool):
                nc.gpsimd.memset(zeros[:], 0.0).then_inc(zeroed, 1)
                nc.gpsimd.memset(found[:], 0).then_inc(zeroed, 1)
                with pool.Fori(0, B) as b:
                    norm.inverse(pool, b)
                pool.wait_ge(w_hi, KD + 1)
                for k in range(KD):
                    nc.gpsimd.tensor_tensor(w1_s[1][:, k], w1[:, k], rounded(w1_s[0][:, k]), ALU.subtract)
                nc.gpsimd.tensor_tensor(w2_s[1][:], w2[:], rounded(w2_s[0][:]), ALU.subtract)

            @block.scalar
            def _(act):
                act.wait_ge(loaded, 9 * DMA_INC)
                nc.scalar.activation(gw_s[0][:], gw[:], ACT.Copy).then_inc(gw_hi, 1)
                for k in range(KD):
                    nc.scalar.activation(w1_s[0][:, k], w1[:, k], ACT.Copy).then_inc(w_hi, 1)
                nc.scalar.activation(w2_s[0][:], w2[:], ACT.Copy).then_inc(w_hi, 1)
                with act.Fori(0, B) as b:
                    for i in range(TT):
                        banks.wait_filled(act, b, f"ln{i}")
                        src = banks.bank(b, f"ln{i}")[:, 0:D].rearrange("p (k t) -> p k t", k=KD)
                        nc.scalar.activation(xT[0][:, :, bass.ds(b * T + i * P, P)], src, ACT.Copy)
                        nc.scalar.activation(xT_now[0][:, :, i * P:(i + 1) * P], src, ACT.Copy).then_inc(xT_hi, 1)
                banks.wait_kept(act, B - 1, "logits")
                nc.scalar.activation(aff[:], logits[:], ACT.Exp, scale=-1.0).then_inc(exp_ready, 1)

            @block.vector
            def _(dve):
                dve.wait_ge(gw_hi, 1)
                nc.vector.tensor_tensor(gw_s[1][:], gw[:], rounded(gw_s[0][:]), ALU.subtract).then_inc(gw_ready, 1)
                with dve.Fori(0, B) as b:
                    norm.moments(dve, b, lambda i: x_tok[:, bass.ds(b * TT + i, 1), :])
                    norm.wait_inverse(dve, b)
                    for i in range(TT):
                        norm.apply(xn[:, i, :], x_tok[:, bass.ds(b * TT + i, 1), :], i).then_inc(xn_ready, 1)
                    for i in range(TT):
                        dve.wait_ge(xT_hi, b * TT + i + 1)
                        src = banks.bank(b, f"ln{i}")[:, 0:D].rearrange("p (k t) -> p k t", k=KD)
                        now = slice(i * P, (i + 1) * P)
                        nc.vector.tensor_tensor(xT[1][:, :, bass.ds(b * T + i * P, P)], src,
                                                rounded(xT_now[0][:, :, now]), ALU.subtract)
                        banks.freed_by(nc.vector.tensor_tensor(xT_now[1][:, :, now], src,
                                                               rounded(xT_now[0][:, :, now]), ALU.subtract), b, f"ln{i}")
                    banks.wait_filled(dve, b, "logits")
                    ins = nc.vector.tensor_tensor(
                        logits[:, :, bass.ds(b * TT, TT)],
                        banks.bank(b, "logits")[:, 0:TT * E1].rearrange("p (t e) -> p e t", e=E1)[:, 0:E, :],
                        bias[:].unsqueeze(2).broadcast_to([P, E, TT]), ALU.add)
                    banks.freed_by(ins, b, "logits")

                done = [0]

                def then(ins):
                    done[0] += 1
                    ins.then_inc(chain, 1)
                    dve.wait_ge(chain, done[0])

                dve.wait_ge(exp_ready, 1)
                then(nc.vector.tensor_scalar(aff[:], aff[:], 1.0, None, ALU.add))
                then(nc.vector.reciprocal(aff[:], aff[:]))
                rival = aff[:].rearrange("p e t -> p t e").unsqueeze(2).broadcast_to([P, NT, E, E])
                own = aff[:].rearrange("p e t -> p t e").unsqueeze(3).broadcast_to([P, NT, E, E])
                nc.vector.tensor_tensor(more[:], rival, own, ALU.is_gt)
                then(nc.vector.tensor_tensor(ties[:], rival, own, ALU.is_equal))
                lower = below[:].unsqueeze(1).broadcast_to([P, NT, E, E])
                then(nc.vector.tensor_tensor(ties[:], ties[:], lower, ALU.mult))
                then(nc.vector.tensor_tensor(more[:], more[:], ties[:], ALU.add))
                then(nc.vector.tensor_reduce(rank[:].rearrange("p e t -> p t e"), more[:], AX_X, ALU.add))
                then(nc.vector.tensor_scalar(off[:], rank[:], TOP_K - 0.5, -1.0, ALU.is_lt, ALU.add))
                then(nc.vector.scalar_tensor_tensor(out=score[:], in0=off[:], scalar=1.0, in1=aff[:], op0=ALU.add,
                                                    op1=ALU.mult))
                nc.vector.tensor_tensor(score[:], score[:], off[:], ALU.add).then_inc(score_ready, 1)
                dve.wait_ge(score_t, 1)
                then(nc.vector.tensor_copy(s_row[0:ROWS, :], sel_ps[0][0:ROWS, 0:P]))
                dve.wait_ge(zeroed, 2)
                with dve.Fori(0, DIGITS) as n:
                    nc.vector.tensor_tensor(cand[0:ROWS], found[0:ROWS].broadcast_to([ROWS, WAYS]),
                                            steps[0:ROWS, bass.ds(n, 1), :].rearrange("p o w -> p (o w)"),
                                            ALU.bitwise_or).then_inc(searched, 1)
                    dve.wait_ge(searched, n * 4 + 1)
                    for w in range(WAYS):
                        ins = nc.vector.tensor_scalar(unused[0:ROWS, w], s_row[0:ROWS], cand[0:ROWS, w:w + 1].bitcast(F32),
                                                      None, ALU.is_ge, ALU.add, accum_out=counts[0:ROWS, w:w + 1])
                    ins.then_inc(counted, 1)
                    dve.wait_ge(summed, n + 1)
                    nc.vector.tensor_scalar(reached[0:ROWS], sel_ps[1][0:ROWS, 0:WAYS], float(CAPACITY), None,
                                            ALU.is_ge, ALU.add, accum_out=digit[0:ROWS]).then_inc(searched, 1)
                    dve.wait_ge(searched, n * 4 + 2)
                    nc.vector.tensor_tensor(step[0:ROWS], digit[0:ROWS], units[0:ROWS, bass.ds(n, 1)],
                                            ALU.mult).then_inc(searched, 1)
                    dve.wait_ge(searched, n * 4 + 3)
                    nc.vector.tensor_tensor(found[0:ROWS], found[0:ROWS], step[0:ROWS],
                                            ALU.bitwise_or).then_inc(searched, 1)
                    dve.wait_ge(searched, n * 4 + 4)
                bound = found[0:ROWS, 0:1].bitcast(F32)
                nc.vector.tensor_scalar(gt[0:ROWS], s_row[0:ROWS], bound, None, ALU.is_gt, ALU.add,
                                        accum_out=n_gt[0:ROWS])
                nc.vector.tensor_scalar(eq[0:ROWS], s_row[0:ROWS], bound, None, ALU.is_equal, ALU.add,
                                        accum_out=n_eq[0:ROWS]).then_inc(totals_asked, 1)
                dve.wait_ge(totals_asked, 1)
                then(nc.vector.tensor_tensor_scan(upto[0:ROWS], eq[0:ROWS], zeros[0:ROWS], 0.0, ALU.add, ALU.add))
                dve.wait_ge(totals, 1)
                then(nc.vector.tensor_scalar(room[0:ROWS], sel_ps[1][0:ROWS, 0:1], -1.0, float(CAPACITY), ALU.mult,
                                             ALU.add))
                then(nc.vector.scalar_tensor_tensor(out=eq[0:ROWS], in0=upto[0:ROWS], scalar=room[0:ROWS, 0:1],
                                                    in1=eq[0:ROWS], op0=ALU.is_le, op1=ALU.mult))
                then(nc.vector.tensor_tensor(gt[0:ROWS], gt[0:ROWS], eq[0:ROWS], ALU.add))
                nc.vector.tensor_tensor(s_row[0:ROWS], s_row[0:ROWS], gt[0:ROWS], ALU.mult).then_inc(weights_ready, 1)
                dve.wait_ge(weights_t, 1)
                nc.vector.tensor_copy(w_tok[:].rearrange("p e t -> p (e t)"), sel_ps[2][:, 0:ROWS])

            @block.tensor
            def _(pe):
                banks.all_free(pe)
                pe.wait_ge(gw_ready, 1)
                with pe.Fori(0, B) as b:
                    for i in range(TT):
                        banks.wait_freed(pe, b, f"ln{i}")
                        pe.wait_ge(xn_ready, b * TT + i + 1)
                        for k in range(KD):
                            ins = pe.transpose(banks.bank(b, f"ln{i}")[:, k * P:(k + 1) * P],
                                               xn[:, i, k * P:(k + 1) * P], c["ident"][:])
                        banks.filled_by(ins)
                    banks.wait_freed(pe, b, "logits")
                    for i in range(TT):
                        banks.wait_kept(pe, b, f"ln{i}")
                        for k in range(KD):
                            ins = three_passes(pe, banks.bank(b, "logits")[:, i * E1:(i + 1) * E1],
                                               [x[:, k, i * P:(i + 1) * P] for x in xT_now],
                                               [w[:, k, :] for w in gw_s], start=(k == 0), stop=(k == KD - 1))
                    banks.filled_by(ins)
                pe.wait_ge(score_ready, 1)
                pe.transpose(sel_ps[0][0:ROWS, 0:P], score[:].rearrange("p e t -> p (e t)"), c["ident"][:]).then_inc(
                    score_t, 1)
                with pe.Fori(0, DIGITS) as n:
                    pe.wait_ge(counted, n + 1)
                    pe.matmul(sel_ps[1][0:ROWS, 0:WAYS], same[0:ROWS, 0:ROWS], counts[0:ROWS], start=True,
                              stop=True).then_inc(summed, 1)
                pe.wait_ge(totals_asked, 1)
                pe.matmul(sel_ps[1][0:ROWS, 0:1], same[0:ROWS, 0:ROWS], n_gt[0:ROWS, 0:1], start=True, stop=False)
                pe.matmul(sel_ps[1][0:ROWS, 0:1], before[0:ROWS, 0:ROWS], n_eq[0:ROWS, 0:1], start=False,
                          stop=True).then_inc(totals, 1)
                pe.wait_ge(weights_ready, 1)
                pe.transpose(sel_ps[2][:, 0:ROWS], s_row[0:ROWS, :], c["ident"][0:ROWS, 0:ROWS]).then_inc(weights_t, 1)

        acc = sb("m_acc", [P, TT, D])
        gate = sb("m_gate", [P, 2, T])
        h = sb("m_h", [P, 2, T])
        h_s = [sb(f"m_h_{s}", [P, 2, T], F32R) for s in ("hi", "lo")]
        banks = Banks(ctx, nc, "m", main, 8)
        norm = Norm(ctx, nc, c, "m")
        h_hi, h_lo = sem("m_h_hi_ready"), sem("m_h_lo_ready")
        y_normed, x_updated, stored = (sem(f"m_{s}") for s in ("y_normed", "x_updated", "stored"))
        block = ctx.enter_context(nc.Block())

        @block.sync
        def _(sp):
            for b in range(B):
                sp.wait_ge(x_updated, b + 1)
                sp.dma_start(out[b].rearrange("(t p) d -> p t d", p=P), x_tok[:, b * TT:(b + 1) * TT, :]).then_inc(
                    stored, DMA_INC)
            sp.wait_ge(stored, B * DMA_INC)

        @block.gpsimd
        def _(pool):
            with pool.Fori(0, B) as b:
                for e in range(E1):
                    pool.wait_ge(h_hi, b * E1 + e + 1)
                    nc.gpsimd.tensor_tensor(h_s[1][:, e % 2], h[:, e % 2], rounded(h_s[0][:, e % 2]),
                                            ALU.subtract).then_inc(h_lo, 1)
                norm.inverse(pool, b)

        @block.scalar
        def _(act):
            with act.Fori(0, B) as b:
                for e in range(E1):
                    banks.wait_filled(act, b, f"b{e}")
                    banks.freed_by(nc.scalar.activation(gate[:, e % 2], banks.bank(b, f"b{e}")[:], ACT.Silu), b, f"b{e}")
                    banks.wait_kept(act, b, f"a{e}")
                    nc.scalar.activation(h_s[0][:, e % 2], h[:, e % 2], ACT.Copy).then_inc(h_hi, 1)

        @block.vector
        def _(dve):
            def gather(b, e):
                for n in range(2):
                    name = f"y{e}_{n}"
                    banks.wait_filled(dve, b, name)
                    if e:
                        banks.wait_kept(dve, b, f"y{e - 1}_{n}")
                    for j in range(2):
                        i = 2 * n + j
                        y = banks.bank(b, name)[:, j * D:(j + 1) * D]
                        if e == 0:
                            ins = nc.vector.tensor_copy(acc[:, i, :], y)
                        else:
                            ins = nc.vector.scalar_tensor_tensor(
                                out=acc[:, i, :], in0=y, scalar=w_tok[:, e - 1, bass.ds(b * TT + i, 1)],
                                in1=acc[:, i, :], op0=ALU.mult, op1=ALU.add)
                    banks.freed_by(ins, b, name)

            with dve.Fori(0, B) as b:
                for e in range(E1):
                    banks.wait_filled(dve, b, f"a{e}")
                    banks.wait_kept(dve, b, f"b{e}")
                    if e >= 2:
                        dve.wait_ge(h_lo, b * E1 + e - 1)
                    banks.freed_by(nc.vector.tensor_tensor(h[:, e % 2], banks.bank(b, f"a{e}")[:], gate[:, e % 2],
                                                           ALU.mult), b, f"a{e}")
                    if e:
                        gather(b, e - 1)
                gather(b, E1 - 1)
                for n in range(2):
                    banks.wait_kept(dve, b, f"y{E1 - 1}_{n}")
                norm.moments(dve, b, lambda i: acc[:, i, :])
                norm.wait_inverse(dve, b)
                for i in range(TT):
                    ins = norm.apply(acc[:, i, :], acc[:, i, :], i)
                ins.then_inc(y_normed, 1)
                dve.wait_ge(y_normed, b + 1)
                x_b = x_tok[:, bass.ds(b * TT, TT), :]
                nc.vector.tensor_tensor(x_b, x_b, acc[:], ALU.add).then_inc(x_updated, 1)
                dve.wait_ge(x_updated, b + 1)

        @block.tensor
        def _(pe):
            def project_down(b, e):
                pe.wait_ge(h_lo, b * E1 + e + 1)
                for n in range(2):
                    name = f"y{e}_{n}"
                    banks.wait_freed(pe, b, name)
                    for j in range(2):
                        i = 2 * n + j
                        ins = three_passes(pe, banks.bank(b, name)[:, j * D:(j + 1) * D],
                                           [x[:, e % 2, i * P:(i + 1) * P] for x in h_s],
                                           [w[:, e, :] for w in w2_s], start=True, stop=True)
                    banks.filled_by(ins)

            banks.all_free(pe)
            with pe.Fori(0, B) as b:
                for e in range(E1):
                    for name, half in ((f"a{e}", 0), (f"b{e}", 1)):
                        banks.wait_freed(pe, b, name)
                        for k in range(KD):
                            ins = three_passes(pe, banks.bank(b, name)[:],
                                               [w[:, k, e, half * P:(half + 1) * P] for w in w1_s],
                                               [x[:, k, bass.ds(b * T, T)] for x in xT], start=(k == 0),
                                               stop=(k == KD - 1))
                        banks.filled_by(ins)
                    if e:
                        project_down(b, e - 1)
                project_down(b, E1 - 1)


def layers(nc, a, out):
    with ExitStack() as ctx:
        c = {}
        x_tok = ctx.enter_context(nc.sbuf_tensor("x_tok", [P, NT, D], F32))
        c["ident"] = ctx.enter_context(nc.sbuf_tensor("ident", [P, P], F32))
        c["ident_bf"] = ctx.enter_context(nc.sbuf_tensor("ident_bf", [P, P], BF16))
        c["causal"] = ctx.enter_context(nc.sbuf_tensor("causal", [P, P], F32))
        c["causal_bf"] = ctx.enter_context(nc.sbuf_tensor("causal_bf", [P, P], BF16))
        c["minus_half"] = ctx.enter_context(nc.sbuf_tensor("minus_half", [P, TT], F32))
        const_loaded = ctx.enter_context(nc.semaphore("const_loaded"))
        const_ready = ctx.enter_context(nc.semaphore("const_ready"))
        with nc.Block() as block:
            @block.sync
            def _(sp):
                sp.dma_start(c["ident"][:], a["c_ident"]).then_inc(const_loaded, DMA_INC)
                sp.dma_start(c["causal"][:], a["c_causal"]).then_inc(const_loaded, DMA_INC)
            @block.gpsimd
            def _(pool):
                nc.gpsimd.memset(c["minus_half"][:], -0.5).then_inc(const_ready, 1)
            @block.vector
            def _(dve):
                dve.wait_ge(const_loaded, 2 * DMA_INC)
                nc.vector.tensor_copy(c["ident_bf"][:], c["ident"][:]).then_inc(const_ready, 1)
                nc.vector.tensor_copy(c["causal_bf"][:], c["causal"][:]).then_inc(const_ready, 1)
        attention0(nc, a, c, x_tok)
        ffn0(nc, a, c, x_tok)
        attention1(nc, a, c, x_tok)
        experts(nc, a, c, x_tok, out)


_INS = ['L0_attn_x', 'L0_attn_Wq', 'L0_attn_bq', 'L0_attn_Wk', 'L0_attn_bk', 'L0_attn_Wv', 'L0_attn_bv', 'L0_attn_Wo',
        'L0_attn_bo', 'L0_ffn_SU_ug', 'L0_ffn_SU_dp', 'L0_ffn_Wscale_ug', 'L0_ffn_Wscale_dp', 'L0_ffn_W_up',
        'L0_ffn_W_gate', 'L0_ffn_W_down', 'L1_attn_Wq', 'L1_attn_Wk', 'L1_attn_Wv', 'L1_attn_Wo', 'L1_attn_bo',
        'L1_ffn_gate_w', 'L1_ffn_expert_bias', 'L1_ffn_shared_w1', 'L1_ffn_shared_w2', 'L1_ffn_routed_w1',
        'L1_ffn_routed_w2']


def kernel(**inputs):
    import concourse.bacc as _bacc
    from concourse.bass_utils import run_bass_kernel_spmd as _run

    nc = _bacc.Bacc("TRN2", target_bir_lowering=False, num_devices=1)
    arrays, args = {}, {}
    given = {name: np.asarray(inputs[name]) for name in _INS}
    for name in ("L0_attn_bq", "L0_attn_bk", "L0_attn_bv"):
        given[name] = given[name].reshape(H, DH).T
    for name in ("L0_attn_bo", "L0_ffn_Wscale_dp", "L1_attn_bo", "L1_ffn_expert_bias"):
        given[name] = given[name].reshape(1, -1)
    for name in ("L0_ffn_SU_ug", "L0_ffn_SU_dp"):
        given[name] = given[name].reshape(-1, P).T
    scales = given.pop("L0_ffn_Wscale_ug").reshape(2, -1, P)
    given["L0_ffn_Wscale_up"], given["L0_ffn_Wscale_gate"] = scales[0].T, scales[1].T
    w1 = np.concatenate([given.pop("L1_ffn_shared_w1"), given.pop("L1_ffn_routed_w1")])
    given["L1_ffn_w1"] = w1.reshape(E + 1, KD, P, D).transpose(2, 1, 0, 3)
    w2 = np.concatenate([given.pop("L1_ffn_shared_w2"), given.pop("L1_ffn_routed_w2")])
    given["L1_ffn_w2"] = w2.transpose(1, 0, 2)
    gate = np.pad(given["L1_ffn_gate_w"], ((0, 0), (0, 1)))
    given["L1_ffn_gate_w"] = gate.reshape(KD, P, E + 1).transpose(1, 0, 2)
    given["L1_attn_Wo"] = given["L1_attn_Wo"].reshape(4, 2, 2, DH1, D).transpose(1, 2, 0, 3, 4).reshape(D, D)
    for name in ("L0_ffn_W_up", "L0_ffn_W_gate", "L0_ffn_W_down"):
        given[name] = given[name].T
    for name, a in (given | shape_constants()).items():
        a = np.ascontiguousarray(a)
        arrays[f"in_{name}"] = a
        args[name] = nc.dram_tensor(f"in_{name}", a.shape, mybir.dt.from_np(a.dtype), kind="ExternalInput").ap()
    out = nc.dram_tensor("out_x", (B, T, D), F32, kind="ExternalOutput").ap()
    layers(nc, args, out)
    r = _run(nc, [arrays], core_ids=[0])
    return r.results[0]["out_x"]
```

```python
from contextlib import ExitStack

import numpy as np

import concourse.bass as bass
from concourse import mybir
from concourse.alu_op_type import AluOpType as ALU

ACT = mybir.ActivationFunctionType
AX_X = mybir.AxisListType.X
F32 = mybir.dt.float32
F32R = mybir.dt.float32r
BF16 = mybir.dt.bfloat16
I32 = mybir.dt.int32

P = 128
B, T, D = 4, 512, 256
TT, KD = T // P, D // P
NT = B * TT
INTER = 1024
H, DH = 16, 128
HD = H * DH
H1, DH1 = 16, 16
WINDOW, ROPE, ROPE_BASE = 64, 8, 10000.0
E, TOP_K = 7, 2
CAPACITY = B * T // E
DIGITS, DIGIT = 10, 3
WAYS = 2 ** DIGIT - 1
UNROLL = 5
LN_EPS = 1e-5
DMA_INC = 16
CHUNK = 256
NCHUNK = HD // CHUNK
RAW = 4

S_BANK = {0: 0, 2: 0, 1: 1, 3: 2}
S_COL = {0: 0, 2: P, 1: 0, 3: 0}
P_COL = {0: 0, 2: P, 1: 4 * P, 3: 6 * P}
SOFTMAX_ORDER = (0, 2, 1, 3)
T_FILLS = ((0,), (1, 3), (2,))
PT_COL = {0: 0, 1: 4 * P, 3: 7 * P, 2: 8 * P}
PT_ALL = 10 * P


def shape_constants():
    ident = np.eye(P, dtype=np.float32)
    causal = np.where(np.arange(P)[None, :] > np.arange(P)[:, None], -1e30, 0.0).astype(np.float32)
    signs = [[(-1.0) ** bin(i & j).count("1") for j in range(P)] for i in range(P)]
    freq = np.exp(-np.log(np.float32(ROPE_BASE)) * (np.arange(0, ROPE, 2, dtype=np.float32) / ROPE))
    theta = np.arange(T, dtype=np.float32)[:, None] * freq[None, :].astype(np.float32)
    cos, sin = np.cos(theta), np.sin(theta)
    tiled = [np.concatenate(x, 1).reshape(TT, P, ROPE).transpose(1, 0, 2) for x in ((cos, cos), (-sin, sin))]
    query, key = np.arange(P)[:, None] % WINDOW, np.arange(P)[None, :]
    seen = (key <= WINDOW + query) & (key > query)
    window = np.stack([np.where(seen & (key >= WINDOW), 0.0, -1e30), np.where(seen, 0.0, -1e30)], 1)
    below = np.tril(np.ones((E, E)), -1)
    expert = np.arange(P) // NT
    same = (expert[:, None] == expert[None, :]) & (expert[:, None] < E)
    units = 1 << (DIGIT * np.arange(DIGITS - 1, -1, -1))
    before = same & (np.arange(P)[:, None] < np.arange(P)[None, :])
    return {"c_ident": ident, "c_causal": causal, "c_hadamard": np.array(signs, np.float32),
            "c_cos": tiled[0].astype(np.float32), "c_sin": tiled[1].astype(np.float32),
            "c_window": window.astype(np.float32), "c_below": np.tile(below, (P, 1, 1)).astype(np.float32),
            "c_same": same[:, :E * NT].astype(np.float32), "c_before": before[:, :E * NT].astype(np.float32),
            "c_units": np.tile(units.astype(np.int32), (P, 1)),
            "c_steps": np.tile((units[:, None] * np.arange(1, WAYS + 1)).astype(np.int32), (P, 1, 1))}


def rounded(ap):
    return ap.bitcast(F32)


class Ring:

    def __init__(self, names, banks, before=(), last=None, rounds=None):
        assert len(names) % banks == 0
        self.banks, self.fills, self.rounds = banks, len(names), rounds
        self.start = len(before)
        self.before = {name: n for n, name in enumerate(before)}
        self.names = {name: n for n, name in enumerate(names)}
        self.last = {name: n for n, name in enumerate(last)} if last else self.names

    def bank(self, b, name):
        if isinstance(b, int) and b < 0:
            return self.before[name] % self.banks
        return (self.start + self.table(b)[name]) % self.banks

    def table(self, b):
        return self.last if isinstance(b, int) and b + 1 == self.rounds else self.names

    def order(self, b, name):
        if isinstance(b, int) and b < 0:
            return self.before[name]
        return b * self.fills + (self.start + self.table(b)[name])

    def earlier(self, b, name):
        if isinstance(b, int) and b < 0:
            return self.before[name] // self.banks
        return b * (self.fills // self.banks) + (self.start + self.table(b)[name]) // self.banks


class Banks:

    def __init__(self, ctx, nc, label, names, count, **more):
        self.ring = Ring(names, count, **more)
        self.psum = [ctx.enter_context(nc.psum_tensor(f"{label}{n}", [P, 512], F32)) for n in range(count)]
        self.filled = ctx.enter_context(nc.semaphore(f"{label}_filled"))
        self.freed = [ctx.enter_context(nc.semaphore(f"{label}_freed{n}")) for n in range(count)]

    def bank(self, b, name):
        return self.psum[self.ring.bank(b, name)]

    def wait_filled(self, eng, b, name):
        eng.wait_ge(self.filled, self.ring.order(b, name) + 1)

    def wait_freed(self, eng, b, name):
        eng.wait_ge(self.freed[self.ring.bank(b, name)], self.ring.earlier(b, name) + 1)

    def wait_kept(self, eng, b, name):
        eng.wait_ge(self.freed[self.ring.bank(b, name)], self.ring.earlier(b, name) + 2)

    def all_free(self, pe):
        for freed in self.freed:
            pe.sem_inc(freed, 1)

    def filled_by(self, ins):
        ins.then_inc(self.filled, 1)

    def freed_by(self, ins, b, name):
        ins.then_inc(self.freed[self.ring.bank(b, name)], 1)


def three_passes(pe, out, lhs, rhs, start, stop, **kw):
    (lh, ll), (rh, rl) = lhs, rhs
    pe.matmul(out, lh, rh, start=start, stop=False, **kw)
    pe.matmul(out, lh, rl, start=False, stop=False, **kw)
    return pe.matmul(out, ll, rh, start=False, stop=stop, **kw)


class Norm:

    def __init__(self, ctx, nc, c, label, tiles=TT):
        self.nc, self.c, self.tiles = nc, c, tiles

        def sb(name, shape):
            return ctx.enter_context(nc.sbuf_tensor(f"{label}_{name}", shape, F32))

        self.st, self.mv = sb("st", [P, tiles, 6]), sb("mv", [P, tiles, 2])
        self.ve, self.rstd = sb("ve", [P, tiles]), sb("rstd", [P, tiles])
        self.var_ready = ctx.enter_context(nc.semaphore(f"{label}_var_ready"))
        self.rstd_ready = ctx.enter_context(nc.semaphore(f"{label}_rstd_ready"))

    def moments(self, dve, source):
        nc = self.nc
        for i in range(self.tiles):
            nc.vector.bn_stats(self.st[:, i, :], source(i))
        dve.drain()
        for i in range(self.tiles):
            nc.vector.bn_aggr(self.mv[:, i, :], self.st[:, i, :])
        dve.drain()
        nc.vector.tensor_scalar(self.ve[:], self.mv[:, :, 1], LN_EPS, None, ALU.add).then_inc(self.var_ready, 1)

    def wait_inverse(self, dve, nth):
        dve.wait_ge(self.rstd_ready, nth + 1)

    def inverse(self, pool, nth):
        pool.wait_ge(self.var_ready, nth + 1)
        self.nc.gpsimd.tensor_tensor(self.rstd[:], self.ve[:], self.c["minus_half"][:, 0:self.tiles], ALU.pow).then_inc(
            self.rstd_ready, 1)

    def apply(self, out, source, i):
        return self.nc.vector.tensor_scalar(out, source, self.mv[:, i, 0:1], self.rstd[:, i:i + 1], ALU.subtract,
                                            ALU.mult)


def nth_before(b):
    return 0 if isinstance(b, int) and b == 0 else b * 2 - 1


def nth_behind(b, follows, batches):
    return b * 2 + 2 if follows else 2 * batches - 1


def view(c, col, *shape):
    size = int(np.prod(shape))
    names = " ".join("xyz"[:len(shape)])
    return c["landing"][:, col:col + size].rearrange(f"p ({names}) -> p {names}",
                                                     **dict(zip("xyz", shape))) if len(shape) > 1 else c["landing"][
        :, col:col + size]


def ffn0_landing(c):
    return view(c, 0, KD, 2 * INTER), view(c, 2 * KD * INTER, INTER // P, D)


def load_ffn0(sp, a, c):
    wT, dT = ffn0_landing(c)
    for n, name in enumerate(("L0_ffn_W_up", "L0_ffn_W_gate")):
        sp.dma_start(wT[:, :, n * INTER:(n + 1) * INTER],
                     a[name].rearrange("(k p) n -> p k n", p=P)).then_inc(c["ffn0_ug_loaded"], DMA_INC)
    sp.dma_start(dT, a["L0_ffn_W_down"].rearrange("(k p) n -> p k n", p=P)).then_inc(c["ffn0_down_loaded"], DMA_INC)


def attention1_landing(c):
    shapes = ((KD, D + 2 * DH1), (KD, D), (D,), (TT, ROPE), (TT, ROPE), (2, P))
    cols = np.cumsum([0] + [int(np.prod(x)) for x in shapes])
    return [view(c, int(col), *shape) for col, shape in zip(cols, shapes)]


def load_attention1(sp, a, c):
    w_raw, wo, bo, rot_c, rot_s, mask_raw = attention1_landing(c)
    qkv = ((0, D, "L1_attn_Wq"), (D, DH1, "L1_attn_Wk"), (D + DH1, DH1, "L1_attn_Wv"))
    moves = [(w_raw[:, :, col:col + w], a[name].rearrange("(k p) n -> p k n", p=P)) for col, w, name in qkv]
    moves += [(wo, a["L1_attn_Wo"].rearrange("(k p) n -> p k n", p=P)), (bo, a["L1_attn_bo"].broadcast_to([P, D])),
              (rot_c, a["c_cos"]), (rot_s, a["c_sin"]), (mask_raw, a["c_window"])]
    for dst, src in moves:
        sp.dma_start(dst, src).then_inc(c["attention1_loaded"], DMA_INC)


def experts_landing(c):
    return view(c, T * H // 4, KD, E + 1, 2 * P), view(c, T * H // 4 + KD * (E + 1) * 2 * P, E + 1, D)


def load_experts(sp, a, c):
    for dst, name in zip(experts_landing(c), ("L1_ffn_w1", "L1_ffn_w2")):
        sp.dma_start(dst, a[name]).then_inc(c["experts_loaded"], DMA_INC)


def every_batch(eng, body):
    body(-1, True)
    with eng.Fori(0, B - 1) as b:
        body(b, True)
    body(B - 1, False)


def attention0(nc, a, c, x_tok):
    HG = 2

    def v_fills(h):
        if h == 0:
            return [(0, 0), (0, 1)]
        return [((h + 1) // HG, (h + 1) % HG)] * (h + 1 < H)

    prepare = [f"ln{k}" for k in range(KD)] + [f"q{n}" for n in range(H)] + ["k0"]
    fills, last = [], []
    for names, follows in ((fills, True), (last, False)):
        for h in range(H):
            tail = follows and h + 1 == H
            names += [f"ln{k}" for k in range(KD)] * tail
            names += [f"k{h + 1}"] * (h + 1 < H) + [f"o{h - 1}"] * (h > 0)
            names += [f"v{g}_{n}" for g, n in v_fills(h)]
            names += ["q0", "q1"] * tail + [f"t{h}_{n}" for n in range(3)] + ["q2", "q3"] * tail
        names += [f"o{H - 1}"]
        names += ([f"q{n}" for n in range(4, H)] + ["k0"]) * follows
    RAW, SLOTS = 2, 3
    HALF = HD // 2

    with ExitStack() as ctx:
        def sb(name, shape, dt=F32):
            return ctx.enter_context(nc.sbuf_tensor(name, shape, dt))

        def sem(name):
            return ctx.enter_context(nc.semaphore(name))

        wq_raw = sb("wq_raw", [P, RAW, KD, CHUNK])
        wq_s = [sb(f"wq_{s}", [P, SLOTS, KD, CHUNK], F32R) for s in ("hi", "lo")]
        wk_s = [sb(f"wk_{s}", [P, KD, HD], F32R) for s in ("hi", "lo")]
        wv_s = [sb(f"wv_{s}", [P, KD, HD], F32R) for s in ("hi", "lo")]
        wo = sb("wo", [P, H, D])
        xT = [sb(f"xT_{s}", [P, KD, T], F32R) for s in ("hi", "lo")]
        qT = view(c, 0, T, H)
        qs = [sb(f"qs_{s}", [P, T], F32R) for s in ("hi", "lo")]
        kT = [sb(f"kT_{s}", [P, T], F32R) for s in ("hi", "lo")]
        v = [sb(f"v_{s}", [P, 2, TT, HG * DH], F32R) for s in ("hi", "lo")]
        p = sb("p", [P, PT_ALL])
        pT = [sb(f"pT_{s}", [P, PT_ALL], F32R) for s in ("hi", "lo")]
        oT = sb("oT", [P, T])
        xn = sb("xn", [P, TT, D])
        y = sb("y", [P, TT, D])
        bq, bk, bv = (sb(n, [P, H]) for n in ("bq", "bk", "bv"))
        bqs = sb("bqs", [P, H])
        bo = sb("bo", [P, D])
        negm = sb("negm", [P, TT])
        rsum = sb("rsum", [P, TT])
        rinv = sb("rinv", [P, TT])
        banks = Banks(ctx, nc, "ring", fills, 3, before=prepare, last=last, rounds=B)
        s_ps = [ctx.enter_context(nc.psum_tensor(f"scores{n}", [P, 512], F32)) for n in range(3)]
        y_ps = [ctx.enter_context(nc.psum_tensor(f"y_ps{n}", [P, 512], F32)) for n in range(2)]
        norm = Norm(ctx, nc, c, "a")

        wo_flat, y_flat = wo[:].rearrange("p h d -> p (h d)"), y[:].rearrange("p t d -> p (t d)")
        landing = [wo_flat[:, n * HALF:(n + 1) * HALF] for n in range(4)] + [y_flat, p[:, 0:HALF]]
        pieces = [(w, k, half) for w in range(2) for k in range(KD) for half in range(2)]
        wq_loaded = [sem(f"wq_loaded{n}") for n in range(RAW)]
        wkv_loaded = [sem(f"wkv_loaded{n}") for n in range(len(pieces))]
        wq_hi, wq_lo = sem("wq_hi_ready"), sem("wq_lo_ready")
        wkv_hi, wkv_lo = sem("wkv_hi_ready"), sem("wkv_lo_ready")
        x_loaded, rows_loaded, wo_loaded = sem("x_loaded"), sem("rows_loaded"), sem("wo_loaded")
        bqs_ready = sem("bqs_ready")
        xn_ready, xT_hi = sem("xn_ready"), sem("xT_hi_ready")
        qs_hi, qs_lo = sem("qs_hi_ready"), sem("qs_lo_ready")
        k_hi, v_hi = sem("k_hi_ready"), sem("v_hi_ready")
        scored = [sem(f"scored{n}") for n in range(3)]
        max_ready, exp_ready, rinv_ready, p_ready = (sem(s) for s in ("max_ready", "exp_ready", "rinv_ready",
                                                                      "p_ready"))
        pT_hi = sem("pT_hi_ready")
        y_done, y_freed, y_normed, x_updated = (sem(s) for s in ("y_done", "y_freed", "y_normed", "x_updated"))

        def q_of(h):
            return qT[:, h * (T // H):(h + 1) * (T // H), :].rearrange("p t c -> p (t c)")

        block = ctx.enter_context(nc.Block())

        @block.sync
        def _(sp):
            def load_chunks(b):
                for n in range(NCHUNK):
                    if not (isinstance(b, int) and n < RAW):
                        sp.wait_ge(wq_lo, (b + 1) * NCHUNK + n - RAW + 1)
                    sp.dma_start(wq_raw[:, n % RAW], a["L0_attn_Wq"][:, n * CHUNK:(n + 1) * CHUNK].rearrange(
                        "(k p) n -> p k n", p=P)).then_inc(wq_loaded[n % RAW], DMA_INC)
                    if isinstance(b, int) and n >= 1:
                        load_pieces(*{1: (0, 2), 2: (2, 4), 3: (4, 6), 4: (6, 7), 5: (7, 8)}.get(n, (8, 8)))

            def load_pieces(lo, hi):
                for m in range(lo, hi):
                    w, k, half = pieces[m]
                    if m >= len(landing):
                        sp.wait_ge(wkv_lo, m - len(landing) + 1)
                    sp.dma_start(landing[m % len(landing)],
                                 a[("L0_attn_Wk", "L0_attn_Wv")[w]][k * P:(k + 1) * P,
                                                                    half * HALF:(half + 1) * HALF]).then_inc(
                        wkv_loaded[m], DMA_INC)

            sp.dma_start(x_tok[:, 0:TT, :], a["L0_attn_x"][0].rearrange("(t p) d -> p t d", p=P)).then_inc(
                x_loaded, DMA_INC)
            for name, dst in (("bq", bq), ("bk", bk), ("bv", bv)):
                sp.dma_start(dst[:], a[f"L0_attn_{name}"]).then_inc(rows_loaded, DMA_INC)
            sp.dma_start(bo[:], a["L0_attn_bo"].broadcast_to([P, D])).then_inc(rows_loaded, DMA_INC)
            load_chunks(-1)
            for b in range(1, B):
                sp.dma_start(x_tok[:, b * TT:(b + 1) * TT, :],
                             a["L0_attn_x"][b].rearrange("(t p) d -> p t d", p=P)).then_inc(x_loaded, DMA_INC)
            sp.wait_ge(wkv_lo, len(pieces))
            sp.dma_start(wo[:], a["L0_attn_Wo"].rearrange("(h d) n -> d h n", d=DH)).then_inc(wo_loaded, DMA_INC)
            with sp.Fori(0, B - 1) as b:
                load_chunks(b)
            sp.wait_ge(qs_lo, B * H)
            load_ffn0(sp, a, c)

        @block.gpsimd
        def _(pool):
            def lo_of_chunk(b, n):
                pool.wait_ge(wq_hi, (b + 1) * NCHUNK + n + 1)
                nc.gpsimd.tensor_tensor(wq_s[1][:, n % SLOTS], wq_raw[:, n % RAW], rounded(wq_s[0][:, n % SLOTS]),
                                        ALU.subtract).then_inc(wq_lo, 1)

            def lo_of_q(nb, h):
                pool.wait_ge(qs_hi, nb * H + h + 1)
                nc.gpsimd.tensor_tensor(qs[1][:], q_of(h), rounded(qs[0][:]), ALU.subtract).then_inc(qs_lo, 1)

            def body(b, follows):
                first = isinstance(b, int) and b < 0
                for h in range(H if not first else 0):
                    if h + 1 < H:
                        lo_of_q(b, h + 1)
                    if follows and h == H - 4:
                        norm.inverse(pool, nth_before(b + 1))
                    if follows and H - 5 <= h < H - 5 + SLOTS:
                        lo_of_chunk(b, h - (H - 5))
                if first:
                    norm.inverse(pool, 0)
                    for n in range(SLOTS):
                        lo_of_chunk(b, n)
                if follows:
                    lo_of_chunk(b, 3)
                    lo_of_chunk(b, 4)
                if not first:
                    norm.inverse(pool, nth_behind(b, follows, B))
                if follows:
                    for n in range(5, NCHUNK):
                        lo_of_chunk(b, n)
                    lo_of_q(b + 1, 0)

            every_batch(pool, body)

        @block.scalar
        def _(act):
            def hi_of_x(b, k):
                banks.wait_filled(act, b, f"ln{k}")
                nc.scalar.activation(xT[0][:, k, :], banks.bank(b, f"ln{k}")[:], ACT.Copy).then_inc(xT_hi, 1)

            def hi_of_chunk(b, n):
                act.wait_ge(wq_loaded[n % RAW], (b + 1) * (NCHUNK // RAW * DMA_INC) + (n // RAW + 1) * DMA_INC)
                nc.scalar.activation(wq_s[0][:, n % SLOTS], wq_raw[:, n % RAW], ACT.Copy).then_inc(wq_hi, 1)

            def store_q(b, n):
                banks.wait_filled(act, b, f"q{n}")
                banks.freed_by(nc.scalar.activation(qT[:, :, n], banks.bank(b, f"q{n}")[:], ACT.Identity,
                                                    bias=bqs[:, n:n + 1], scale=float(DH) ** -0.5), b, f"q{n}")

            def hi_of_q(b, h):
                if h == 0:
                    for n in range(H - 3, H):
                        banks.wait_kept(act, b, f"q{n}")
                else:
                    act.wait_ge(scored[2], b * H + h)
                nc.scalar.activation(qs[0][:], q_of(h), ACT.Copy).then_inc(qs_hi, 1)

            def hi_of_k(b, h):
                banks.wait_filled(act, b, f"k{h}")
                nc.scalar.activation(kT[0][:], banks.bank(b, f"k{h}")[:], ACT.Identity,
                                     bias=bk[:, h:h + 1]).then_inc(k_hi, 1)

            def hi_of_v(b, g, n):
                banks.wait_filled(act, b, f"v{g}_{n}")
                nc.scalar.activation(v[0][:, g % 2, 2 * n:2 * n + 2].rearrange("p t d -> p (t d)"),
                                     banks.bank(b, f"v{g}_{n}")[:], ACT.Copy).then_inc(v_hi, 1)

            def softmax_exp(b, h):
                for n, i in enumerate(SOFTMAX_ORDER):
                    act.wait_ge(max_ready, b * H * TT + h * TT + max(n + 1, 2))
                    w = (i + 1) * P
                    ins = nc.scalar.activation(p[:, P_COL[i]:P_COL[i] + w],
                                               s_ps[S_BANK[i]][:, S_COL[i]:S_COL[i] + w], ACT.Exp,
                                               bias=negm[:, i:i + 1], accum_out=rsum[:, i:i + 1])
                    ins.then_inc(exp_ready, 1)

            def hi_of_pT(b, h):
                for n in range(3):
                    banks.wait_filled(act, b, f"t{h}_{n}")
                    col, w = PT_COL[T_FILLS[n][0]], (512, 512, 256)[n]
                    nc.scalar.activation(pT[0][:, col:col + w], banks.bank(b, f"t{h}_{n}")[:, 0:w],
                                         ACT.Copy).then_inc(pT_hi, 1)

            def store_o(b, h):
                banks.wait_filled(act, b, f"o{h}")
                banks.freed_by(nc.scalar.activation(oT[:], banks.bank(b, f"o{h}")[:], ACT.Identity,
                                                    bias=bv[:, h:h + 1]), b, f"o{h}")

            def body(b, follows):
                first = isinstance(b, int) and b < 0
                for h in range(H if not first else 0):
                    tail = follows and h + 1 == H
                    if tail:
                        hi_of_x(b, 0)
                        hi_of_x(b, 1)
                    softmax_exp(b, h)
                    if h + 1 < H:
                        hi_of_q(b, h + 1)
                        hi_of_k(b, h + 1)
                    if h:
                        store_o(b, h - 1)
                    for g, n in v_fills(h):
                        hi_of_v(b, g, n)
                    if tail:
                        store_q(b, 0)
                        store_q(b, 1)
                    hi_of_pT(b, h)
                    if follows and H - 5 <= h < H - 5 + SLOTS:
                        hi_of_chunk(b, h - (H - 5))
                if first:
                    hi_of_chunk(b, 0)
                    hi_of_chunk(b, 1)
                    hi_of_x(b, 0)
                    hi_of_x(b, 1)
                    hi_of_chunk(b, 2)
                    act.wait_ge(bqs_ready, 1)
                    store_q(b, 0)
                    store_q(b, 1)
                if follows:
                    hi_of_chunk(b, 3)
                    store_q(b, 2)
                    store_q(b, 3)
                    hi_of_chunk(b, 4)
                if not first:
                    store_o(b, H - 1)
                if follows:
                    for n in range(4, H):
                        store_q(b, n)
                        if n in (5, 7, 9):
                            hi_of_chunk(b, (n + 5) // 2)
                    hi_of_q(b, 0)
                    hi_of_k(b, 0)

            every_batch(act, body)

        @block.vector
        def _(dve):
            def lo_of(b, name, out, hi, hi_sem, nth, bias=None):
                dve.wait_ge(hi_sem, nth)
                src = banks.bank(b, name)[:, 0:out.shape[-1]]
                if bias is None:
                    ins = nc.vector.tensor_tensor(out, src, rounded(hi), ALU.subtract)
                else:
                    ins = nc.vector.scalar_tensor_tensor(out=out, in0=src, scalar=bias, in1=rounded(hi),
                                                         op0=ALU.add, op1=ALU.subtract)
                banks.freed_by(ins, b, name)

            def softmax_max(b, h):
                for i in SOFTMAX_ORDER:
                    if i != 2:
                        dve.wait_ge(scored[S_BANK[i]], b * H + h + 1)
                    nc.vector.tensor_reduce(negm[:, i:i + 1], s_ps[S_BANK[i]][:, S_COL[i]:S_COL[i] + (i + 1) * P],
                                            AX_X, ALU.max, negate=True).then_inc(max_ready, 1)

            def softmax_norm(b, h):
                dve.wait_ge(exp_ready, b * H * TT + (h + 1) * TT)
                nc.vector.reciprocal(rinv[:], rsum[:]).then_inc(rinv_ready, 1)
                dve.wait_ge(rinv_ready, b * H + h + 1)
                for i in SOFTMAX_ORDER:
                    cols = p[:, P_COL[i]:P_COL[i] + (i + 1) * P]
                    nc.vector.tensor_scalar(cols, cols, rinv[:, i:i + 1], None, ALU.mult).then_inc(p_ready, 1)

            def lo_of_x(b, k):
                lo_of(b, f"ln{k}", xT[1][:, k, :], xT[0][:, k, :], xT_hi, (b + 1) * KD + k + 1)

            def lo_of_k(b, h, nb):
                lo_of(b, f"k{h}", kT[1][:], kT[0][:], k_hi, nb * H + h + 1, bias=bk[:, h:h + 1])

            def lo_of_v(b, g, n):
                out, hi = (x[:, g % 2, 2 * n:2 * n + 2].rearrange("p t d -> p (t d)") for x in (v[1], v[0]))
                lo_of(b, f"v{g}_{n}", out, hi, v_hi, b * H + HG * g + n + 1)

            def norm_before(b):
                nb = b + 1
                norm.wait_inverse(dve, nth_before(nb))
                for i in range(TT):
                    norm.apply(xn[:, i, :], x_tok[:, bass.ds(nb * TT + i, 1), :], i).then_inc(xn_ready, 1)

            def norm_behind(b, follows):
                dve.wait_ge(y_done, b + 1)
                for n in range(2):
                    ins = nc.vector.tensor_tensor(y[:, 2 * n:2 * n + 2, :],
                                                  y_ps[n][:].rearrange("p (t d) -> p t d", d=D),
                                                  bo[:].unsqueeze(1).broadcast_to([P, 2, D]), ALU.add)
                ins.then_inc(y_freed, 1)
                dve.wait_ge(y_freed, b + 1)
                norm.moments(dve, lambda i: y[:, i, :])
                norm.wait_inverse(dve, nth_behind(b, follows, B))
                for i in range(TT):
                    ins = norm.apply(y[:, i, :], y[:, i, :], i)
                ins.then_inc(y_normed, 1)
                dve.wait_ge(y_normed, b + 1)
                x_b = x_tok[:, bass.ds(b * TT, TT), :]
                nc.vector.tensor_tensor(x_b, x_b, y[:], ALU.add).then_inc(x_updated, 1)

            def body(b, follows):
                first = isinstance(b, int) and b < 0
                for h in range(H if not first else 0):
                    softmax_max(b, h)
                    if follows and h + 1 == H:
                        lo_of_x(b, 0)
                        lo_of_x(b, 1)
                    if h + 1 < H:
                        lo_of_k(b, h + 1, b)
                    softmax_norm(b, h)
                    for g, n in v_fills(h):
                        lo_of_v(b, g, n)
                    for n in range(3):
                        col, w = PT_COL[T_FILLS[n][0]], (512, 512, 256)[n]
                        lo_of(b, f"t{h}_{n}", pT[1][:, col:col + w], pT[0][:, col:col + w], pT_hi,
                              b * 3 * H + h * 3 + n + 1)
                    if follows and h == H - 4:
                        norm.moments(dve, lambda i: x_tok[:, bass.ds((b + 1) * TT + i, 1), :])
                    if follows and h == H - 3:
                        norm_before(b)
                if not first:
                    norm_behind(b, follows)
                if first:
                    dve.wait_ge(x_loaded, DMA_INC)
                    norm.moments(dve, lambda i: x_tok[:, i, :])
                    norm_before(b)
                    dve.wait_ge(rows_loaded, 4 * DMA_INC)
                    nc.vector.tensor_scalar(bqs[:], bq[:], float(DH) ** -0.5, None, ALU.mult).then_inc(bqs_ready, 1)
                    lo_of_x(b, 0)
                    lo_of_x(b, 1)
                    for m, (w, k, half) in enumerate(pieces):
                        hi, lo = (x[:, k, half * HALF:(half + 1) * HALF] for x in (wk_s, wv_s)[w])
                        dve.wait_ge(wkv_loaded[m], DMA_INC)
                        nc.vector.tensor_copy(hi, landing[m % len(landing)]).then_inc(wkv_hi, 1)
                        dve.wait_ge(wkv_hi, m + 1)
                        nc.vector.tensor_tensor(lo, landing[m % len(landing)], rounded(hi), ALU.subtract).then_inc(
                            wkv_lo, 1)
                    dve.wait_ge(x_loaded, B * DMA_INC)
                if follows:
                    lo_of_k(b, 0, b + 1)

            every_batch(dve, body)

        @block.tensor
        def _(pe):
            def project(out, k_lhs, k_rhs):
                for k in range(KD):
                    ins = three_passes(pe, out, k_lhs(k), k_rhs(k), start=(k == 0), stop=(k == KD - 1))
                return ins

            def fill_ln(b, k):
                banks.wait_freed(pe, b, f"ln{k}")
                for i in range(TT):
                    if k == 0:
                        pe.wait_ge(xn_ready, (b + 1) * TT + i + 1)
                    ins = pe.transpose(banks.bank(b, f"ln{k}")[:, i * P:(i + 1) * P],
                                       xn[:, i, k * P:(k + 1) * P], c["ident"][:])
                banks.filled_by(ins)

            def fill_q(b, n):
                if n == 0:
                    for k in range(KD):
                        banks.wait_kept(pe, b, f"ln{k}")
                if n % 2 == 0:
                    pe.wait_ge(wq_lo, (b + 1) * NCHUNK + n // 2 + 1)
                banks.wait_freed(pe, b, f"q{n}")
                col = n % 2 * DH
                banks.filled_by(project(banks.bank(b, f"q{n}")[:],
                                        lambda k: [w[:, n // 2 % SLOTS, k, col:col + DH] for w in wq_s],
                                        lambda k: [x[:, k, :] for x in xT]))

            def fill_k(b, h):
                banks.wait_freed(pe, b, f"k{h}")
                banks.filled_by(project(banks.bank(b, f"k{h}")[:],
                                        lambda k: [w[:, k, h * DH:(h + 1) * DH] for w in wk_s],
                                        lambda k: [x[:, k, :] for x in xT]))

            def fill_v(b, g, n):
                banks.wait_freed(pe, b, f"v{g}_{n}")
                w = HG * DH
                for j in range(2):
                    t = 2 * n + j
                    ins = project(banks.bank(b, f"v{g}_{n}")[:, j * w:(j + 1) * w],
                                  lambda k: [x[:, k, t * P:(t + 1) * P] for x in xT],
                                  lambda k: [x[:, k, g * w:(g + 1) * w] for x in wv_s])
                banks.filled_by(ins)

            def scores(b, h):
                pe.wait_ge(qs_lo, b * H + h + 1)
                if h:
                    banks.wait_kept(pe, b, f"k{h}")
                for i in SOFTMAX_ORDER:
                    w = (i + 1) * P
                    out = s_ps[S_BANK[i]][:, S_COL[i]:S_COL[i] + w]
                    three_passes(pe, out, [q[:, i * P:(i + 1) * P] for q in qs], [k[:, 0:w] for k in kT],
                                 start=(i != 2), stop=False)
                    if i == 2:
                        ins = pe.matmul(s_ps[0][:].rearrange("p (t k) -> p t k", k=P)[:, 0:TT:TT - 1, :],
                                        c["ident_bf"][:], c["causal_bf"][:].unsqueeze(1).broadcast_to([P, 2, P]),
                                        start=False, stop=True)
                    elif i:
                        ins = pe.matmul(out[:, i * P:w], c["ident_bf"][:], c["causal_bf"][:], start=False, stop=True)
                    if i:
                        ins.then_inc(scored[S_BANK[i]], 1)

            def transpose_p(b, h):
                pe.wait_ge(p_ready, b * H * TT + (h + 1) * TT)
                for n, tiles in enumerate(T_FILLS):
                    name = f"t{h}_{n}"
                    banks.wait_freed(pe, b, name)
                    base = PT_COL[tiles[0]]
                    for j in tiles:
                        for i in range(j, TT):
                            col = PT_COL[j] - base + (i - j) * P
                            src = P_COL[i] + j * P
                            ins = pe.transpose(banks.bank(b, name)[:, col:col + P], p[:, src:src + P], c["ident"][:])
                    banks.filled_by(ins)

            def fill_o(b, h):
                name = f"o{h}"
                banks.wait_freed(pe, b, name)
                for n in range(3):
                    banks.wait_kept(pe, b, f"t{h}_{n}")
                for j in range(TT):
                    w = T - j * P
                    ins = three_passes(pe, banks.bank(b, name)[:, j * P:T],
                                       [x[:, h // HG % 2, j, h % HG * DH:(h % HG + 1) * DH] for x in v],
                                       [x[:, PT_COL[j]:PT_COL[j] + w] for x in pT], start=(j == 0),
                                       stop=(j == TT - 1))
                banks.filled_by(ins)

            def out_project(b, h):
                if h == 0:
                    pe.wait_ge(norm.var_ready, b * 2 + 1)
                    pe.wait_ge(wo_loaded, DMA_INC)
                banks.wait_kept(pe, b, f"o{h}")
                for i in range(TT):
                    ins = pe.matmul(y_ps[i // 2][:, i % 2 * D:(i % 2 + 1) * D], oT[:, i * P:(i + 1) * P],
                                    wo[:, h, :], start=(h == 0 and i % 2 == 0), stop=(h == H - 1),
                                    skip_group_check=True)
                if h == H - 1:
                    ins.then_inc(y_done, 1)

            def body(b, follows):
                first = isinstance(b, int) and b < 0
                for h in range(H if not first else 0):
                    tail = follows and h + 1 == H
                    scores(b, h)
                    if tail:
                        fill_ln(b, 0)
                        fill_ln(b, 1)
                    if h + 1 < H:
                        fill_k(b, h + 1)
                    if h:
                        fill_o(b, h - 1)
                    for g, n in v_fills(h):
                        fill_v(b, g, n)
                    if tail:
                        fill_q(b, 0)
                    if h:
                        out_project(b, h - 1)
                    if tail:
                        fill_q(b, 1)
                    transpose_p(b, h)
                if first:
                    fill_ln(b, 0)
                    fill_ln(b, 1)
                    fill_q(b, 0)
                    fill_q(b, 1)
                if follows:
                    fill_q(b, 2)
                    fill_q(b, 3)
                if not first:
                    fill_o(b, H - 1)
                if follows:
                    fill_q(b, 4)
                if not first:
                    out_project(b, H - 1)
                if follows:
                    for n in range(5, H):
                        fill_q(b, n)
                    if first:
                        pe.wait_ge(wkv_lo, len(pieces))
                    fill_k(b, 0)
                    banks.wait_kept(pe, b, "k0")

            banks.all_free(pe)
            every_batch(pe, body)


def ffn0(nc, a, c, x_tok):
    NF = INTER // P
    LAG = 2
    ahead = [f"ln+{k}" for k in range(KD)] + ["up+0", "gate+0", "up+1", "gate+1"]
    fills, last = [], []
    for names, follows in ((fills, True), (last, False)):
        for n in range(LAG, NF):
            names += [f"up{n}", f"gate{n}"] + ahead[:KD] * (follows and n == NF - 2)
        names += ahead[KD:] * follows

    with ExitStack() as ctx:
        def sb(name, shape, dt=F32):
            return ctx.enter_context(nc.sbuf_tensor(name, shape, dt))

        def sem(name):
            return ctx.enter_context(nc.semaphore(name))

        eff = [sb(f"f_eff_{s}", [P, KD, 2 * INTER], F32R) for s in ("hi", "lo")]
        down = [sb(f"f_down_{s}", [P, NF, D], F32R) for s in ("hi", "lo")]
        xn = sb("f_xn", [P, TT, D])
        norm = Norm(ctx, nc, c, "f")
        xn_ready = sem("f_xn_ready")
        with ExitStack() as inner:
            def sbi(name, shape, dt=F32):
                return inner.enter_context(nc.sbuf_tensor(name, shape, dt))

            def semi(name):
                return inner.enter_context(nc.semaphore(name))

            hada = sbi("hada", [P, P])
            hada_r = [sbi(f"hada_{s}", [P, P], F32R) for s in ("pos", "neg")]
            turned = [sbi(f"f_turned{n}", [P, NF, D]) for n in range(2)]
            wT, dT = ffn0_landing(c)
            wT_s = [sbi(f"f_wT_{s}", [P, KD, 2 * INTER], F32R) for s in ("hi", "lo")]
            dT_s = [sbi(f"f_dT_{s}", [P, NF, D], F32R) for s in ("hi", "lo")]
            d_eff = sbi("f_d_eff", [P, NF, D])
            su_ug, su_dp = sbi("su_ug", [P, KD]), sbi("su_dp", [P, NF])
            su_ug_n, su_dp_n = sbi("su_ug_n", [P, KD]), sbi("su_dp_n", [P, NF])
            sc_dp = sbi("sc_dp", [P, D])
            ug_fills = [f"w{k}_{n}" for n in range(4) for k in range(KD)]
            banks = Banks(inner, nc, "fw", ug_fills + [f"d{n}" for n in range(NF)], 8)
            s_loaded = semi("s_loaded")
            w_loaded, d_loaded = c["ffn0_ug_loaded"], c["ffn0_down_loaded"]
            hada_ready, signs_ready = semi("hada_ready"), semi("signs_ready")
            w_hi, w_lo, d_hi, d_lo = semi("w_hi"), semi("w_lo"), semi("d_hi"), semi("d_lo")
            eff_hi, d_turned = semi("eff_hi"), semi("d_turned")
            down_hi = semi("down_hi")
            block = inner.enter_context(nc.Block())

            @block.sync
            def _(sp):
                sp.dma_start(hada[:], a["c_hadamard"]).then_inc(s_loaded, DMA_INC)
                sp.dma_start(su_ug[:], a["L0_ffn_SU_ug"]).then_inc(s_loaded, DMA_INC)
                sp.dma_start(su_dp[:], a["L0_ffn_SU_dp"]).then_inc(s_loaded, DMA_INC)
                sp.dma_start(sc_dp[:], a["L0_ffn_Wscale_dp"].broadcast_to([P, D])).then_inc(s_loaded, DMA_INC)

            @block.scalar
            def _(act):
                act.wait_ge(w_loaded, 2 * DMA_INC)
                nc.scalar.activation(wT_s[0][:, 1], wT[:, 1], ACT.Copy).then_inc(w_hi, 1)
                act.wait_ge(s_loaded, 4 * DMA_INC)
                nc.scalar.activation(hada_r[0][:], hada[:], ACT.Copy).then_inc(hada_ready, 1)
                nc.scalar.activation(hada_r[1][:], hada[:], ACT.Copy, scale=-1.0).then_inc(hada_ready, 1)
                act.wait_ge(signs_ready, 2)
                for n in range(4):
                    for k in range(KD):
                        name = f"w{k}_{n}"
                        banks.wait_filled(act, 0, name)
                        nc.scalar.activation(eff[0][:, k, n * 512:(n + 1) * 512], banks.bank(0, name)[:], ACT.Copy,
                                             scale=su_ug_n[:, k:k + 1]).then_inc(eff_hi, 1)
                for n in range(NF):
                    if n == 0:
                        act.wait_ge(d_turned, 6)
                        nc.scalar.activation(dT_s[0][:], turned[0][:], ACT.Copy).then_inc(d_hi, 1)
                    banks.wait_kept(act, 0, f"d{n}")
                    nc.scalar.activation(down[0][:, n], d_eff[:, n], ACT.Copy).then_inc(down_hi, 1)

            @block.gpsimd
            def _(pool):
                pool.wait_ge(d_loaded, DMA_INC)
                src = dT
                for stage in range(3):
                    dst = turned[stage % 2]
                    if stage:
                        pool.wait_ge(d_turned, 2 * stage)
                    x, y_ = (ap.rearrange("p (g two h) d -> p g two (h d)", two=2, h=2 ** stage)
                             for ap in (src, dst[:]))
                    nc.gpsimd.tensor_tensor(y_[:, :, 0], x[:, :, 0], x[:, :, 1], ALU.add).then_inc(d_turned, 1)
                    nc.gpsimd.tensor_tensor(y_[:, :, 1], x[:, :, 0], x[:, :, 1], ALU.subtract).then_inc(d_turned, 1)
                    src = dst[:]
                norm.inverse(pool, 0)
                for n in range(NF):
                    pool.wait_ge(down_hi, n + 1)
                    nc.gpsimd.tensor_tensor(down[1][:, n], d_eff[:, n], rounded(down[0][:, n]), ALU.subtract)

            @block.vector
            def _(dve):
                dve.wait_ge(w_loaded, 2 * DMA_INC)
                nc.vector.tensor_copy(wT_s[0][:, 0], wT[:, 0]).then_inc(w_lo, 1)
                dve.wait_ge(w_lo, 1)
                nc.vector.tensor_tensor(wT_s[1][:, 0], wT[:, 0], rounded(wT_s[0][:, 0]), ALU.subtract).then_inc(w_lo, 1)
                dve.wait_ge(w_hi, 1)
                nc.vector.tensor_tensor(wT_s[1][:, 1], wT[:, 1], rounded(wT_s[0][:, 1]), ALU.subtract).then_inc(w_lo, 1)
                norm.moments(dve, lambda i: x_tok[:, i, :])
                dve.wait_ge(s_loaded, 4 * DMA_INC)
                nc.vector.tensor_scalar(su_ug_n[:], su_ug[:], float(D) ** -0.5, None, ALU.mult).then_inc(
                    signs_ready, 1)
                nc.vector.tensor_scalar(su_dp_n[:], su_dp[:], float(INTER) ** -0.5, None, ALU.mult).then_inc(
                    signs_ready, 1)
                dve.wait_ge(signs_ready, 2)
                for n in range(4):
                    for k in range(KD):
                        name = f"w{k}_{n}"
                        dve.wait_ge(eff_hi, n * KD + k + 1)
                        banks.freed_by(nc.vector.scalar_tensor_tensor(
                            out=eff[1][:, k, n * 512:(n + 1) * 512], in0=banks.bank(0, name)[:],
                            scalar=su_ug_n[:, k:k + 1], in1=rounded(eff[0][:, k, n * 512:(n + 1) * 512]),
                            op0=ALU.mult, op1=ALU.subtract), 0, name)
                dve.wait_ge(d_hi, 1)
                nc.vector.tensor_tensor(dT_s[1][:], turned[0][:], rounded(dT_s[0][:]), ALU.subtract).then_inc(d_lo, 1)
                norm.wait_inverse(dve, 0)
                for i in range(TT):
                    norm.apply(xn[:, i, :], x_tok[:, i, :], i).then_inc(xn_ready, 1)
                for n in range(NF):
                    banks.wait_filled(dve, 0, f"d{n}")
                    banks.freed_by(nc.vector.scalar_tensor_tensor(
                        out=d_eff[:, n], in0=banks.bank(0, f"d{n}")[:, 0:D], scalar=su_dp_n[:, n:n + 1], in1=sc_dp[:],
                        op0=ALU.mult, op1=ALU.mult), 0, f"d{n}")

            @block.tensor
            def _(pe):
                def transformed(name, out, sources, row, tiles):
                    banks.wait_freed(pe, 0, name)
                    for j in range(tiles):
                        sign = hada_r[bin(row & j).count("1") % 2]
                        for n, half in enumerate(sources):
                            ins = pe.matmul(out, sign[:], half(j), start=(j == 0 and n == 0),
                                            stop=(j == tiles - 1 and n == 1))
                    banks.filled_by(ins)

                banks.all_free(pe)
                pe.wait_ge(hada_ready, 2)
                pe.wait_ge(w_lo, 3)
                for n in range(4):
                    for k in range(KD):
                        name = f"w{k}_{n}"
                        transformed(name, banks.bank(0, name)[:],
                                    [lambda j, w=w: w[:, j, n * 512:(n + 1) * 512] for w in wT_s], k, KD)
                pe.wait_ge(d_lo, 1)
                for n in range(NF):
                    name = f"d{n}"
                    transformed(name, banks.bank(0, name)[:, 0:D], [lambda j, w=w: w[:, n, :] for w in dT_s], 0, 1)

        xT = [sb(f"f_xT_{s}", [P, KD, B * T], F32R) for s in ("hi", "lo")]
        y = sb("f_y", [P, TT, D])
        gate = sb("f_gate", [P, 2, T])
        h = sb("f_h", [P, 2, T])
        h_s = [sb(f"f_h_{s}", [P, 2 * LAG, T], F32R) for s in ("hi", "lo")]
        su, sg = sb("f_scale_up", [P, NF]), sb("f_scale_gate", [P, NF])
        banks = Banks(ctx, nc, "f", fills, 6, before=ahead, last=last, rounds=B)
        y_ps = [ctx.enter_context(nc.psum_tensor(f"f_y_ps{n}", [P, 512], F32)) for n in range(2)]
        scales = sem("f_scales_loaded")
        xT_hi = sem("f_xT_hi_ready")
        h_hi, h_lo = sem("f_h_hi_ready"), sem("f_h_lo_ready")
        y_done, y_freed, y_normed = sem("f_y_done"), sem("f_y_freed"), sem("f_y_normed")

        def tiles(b, follows):
            own = [] if isinstance(b, int) and b < 0 else [(0, n) for n in range(LAG, NF)]
            return own + [(1, n) for n in range(LAG)] * follows

        def name_of(kind, tile):
            return f"{kind}{'+' * tile[0]}{tile[1]}"

        block = ctx.enter_context(nc.Block())

        @block.sync
        def _(sp):
            sp.dma_start(su[:], a["L0_ffn_Wscale_up"]).then_inc(scales, DMA_INC)
            sp.dma_start(sg[:], a["L0_ffn_Wscale_gate"]).then_inc(scales, DMA_INC)
            load_attention1(sp, a, c)

        @block.gpsimd
        def _(pool):
            def body(b, follows):
                first = isinstance(b, int) and b < 0
                for f, n in tiles(b, follows):
                    pool.wait_ge(h_hi, (b + f) * NF + n + 1)
                    nc.gpsimd.tensor_tensor(h_s[1][:, n % (2 * LAG)], h[:, n % 2], rounded(h_s[0][:, n % (2 * LAG)]),
                                            ALU.subtract).then_inc(h_lo, 1)
                    if follows and not f and n == 3:
                        norm.inverse(pool, nth_before(b + 1))
                if not first:
                    norm.inverse(pool, nth_behind(b, follows, B))

            every_batch(pool, body)

        @block.scalar
        def _(act):
            def hi_of_x(b):
                for k in range(KD):
                    banks.wait_filled(act, b, f"ln+{k}")
                    nc.scalar.activation(xT[0][:, k, bass.ds((b + 1) * T, T)], banks.bank(b, f"ln+{k}")[:],
                                         ACT.Copy).then_inc(xT_hi, 1)

            def body(b, follows):
                first = isinstance(b, int) and b < 0
                if first:
                    hi_of_x(b)
                for f, n in tiles(b, follows):
                    up, gt = name_of("up", (f, n)), name_of("gate", (f, n))
                    banks.wait_filled(act, b, gt)
                    banks.freed_by(nc.scalar.activation(gate[:, n % 2], banks.bank(b, gt)[:], ACT.Silu,
                                                        scale=sg[:, n:n + 1]), b, gt)
                    banks.wait_kept(act, b, up)
                    nc.scalar.activation(h_s[0][:, n % (2 * LAG)], h[:, n % 2], ACT.Copy).then_inc(h_hi, 1)
                    if follows and not f and n == NF - 2:
                        hi_of_x(b)
                if not first:
                    act.wait_ge(y_done, b + 1)
                    for n in range(2):
                        ins = nc.scalar.activation(y[:, 2 * n:2 * n + 2, :].rearrange("p t d -> p (t d)"), y_ps[n][:],
                                                   ACT.Copy)
                    ins.then_inc(y_freed, 1)

            act.wait_ge(scales, 2 * DMA_INC)
            every_batch(act, body)

        @block.vector
        def _(dve):
            def norm_before(nb):
                norm.wait_inverse(dve, nth_before(nb))
                for i in range(TT):
                    norm.apply(xn[:, i, :], x_tok[:, bass.ds(nb * TT + i, 1), :], i).then_inc(xn_ready, 1)

            def lo_of_x(b):
                cols = bass.ds((b + 1) * T, T)
                for k in range(KD):
                    dve.wait_ge(xT_hi, (b + 1) * KD + k + 1)
                    banks.freed_by(nc.vector.tensor_tensor(xT[1][:, k, cols], banks.bank(b, f"ln+{k}")[:],
                                                           rounded(xT[0][:, k, cols]), ALU.subtract), b, f"ln+{k}")

            def norm_behind(b, follows):
                nth = nth_behind(b, follows, B)
                dve.wait_ge(y_freed, b + 2)
                norm.moments(dve, lambda i: y[:, i, :])
                norm.wait_inverse(dve, nth)
                for i in range(TT):
                    ins = norm.apply(y[:, i, :], y[:, i, :], i)
                ins.then_inc(y_normed, 1)
                dve.wait_ge(y_normed, b + 1)
                x_b = x_tok[:, bass.ds(b * TT, TT), :]
                nc.vector.tensor_tensor(x_b, x_b, y[:], ALU.add)

            def body(b, follows):
                first = isinstance(b, int) and b < 0
                if first:
                    lo_of_x(b)
                for f, n in tiles(b, follows):
                    up, gt = name_of("up", (f, n)), name_of("gate", (f, n))
                    banks.wait_filled(dve, b, up)
                    banks.wait_kept(dve, b, gt)
                    before = (b + f) * NF + n - 1
                    if not isinstance(b, int) or before >= 1:
                        dve.wait_ge(h_lo, before)
                    ins = nc.vector.scalar_tensor_tensor(out=h[:, n % 2], in0=banks.bank(b, up)[:],
                                                         scalar=su[:, n:n + 1], in1=gate[:, n % 2], op0=ALU.mult,
                                                         op1=ALU.mult)
                    banks.freed_by(ins, b, up)
                    if follows and not f and n == 3:
                        norm.moments(dve, lambda i: x_tok[:, bass.ds((b + 1) * TT + i, 1), :])
                    if follows and not f and n == 4:
                        norm_before(b + 1)
                    if follows and not f and n == NF - 2:
                        lo_of_x(b)
                if not first:
                    norm_behind(b, follows)

            dve.wait_ge(scales, 2 * DMA_INC)
            every_batch(dve, body)

        @block.tensor
        def _(pe):
            def transpose_x(b):
                for k in range(KD):
                    banks.wait_freed(pe, b, f"ln+{k}")
                    for i in range(TT):
                        if k == 0:
                            pe.wait_ge(xn_ready, (b + 1) * TT + i + 1)
                        ins = pe.transpose(banks.bank(b, f"ln+{k}")[:, i * P:(i + 1) * P],
                                           xn[:, i, k * P:(k + 1) * P], c["ident"][:])
                    banks.filled_by(ins)

            def project_down(nb, n):
                pe.wait_ge(h_lo, nb * NF + n + 1)
                for i in range(TT):
                    ins = three_passes(pe, y_ps[i // 2][:, i % 2 * D:(i % 2 + 1) * D],
                                       [x[:, n % (2 * LAG), i * P:(i + 1) * P] for x in h_s], [w[:, n, :] for w in down],
                                       start=(n == 0 and i % 2 == 0), stop=(n == NF - 1), skip_group_check=True)
                return ins

            def body(b, follows):
                first = isinstance(b, int) and b < 0
                if first:
                    transpose_x(b)
                for f, n in tiles(b, follows):
                    if f and n == 0:
                        for k in range(KD):
                            banks.wait_kept(pe, b, f"ln+{k}")
                    for kind, col in (("up", n * P), ("gate", INTER + n * P)):
                        name = name_of(kind, (f, n))
                        banks.wait_freed(pe, b, name)
                        for k in range(KD):
                            ins = three_passes(pe, banks.bank(b, name)[:], [w[:, k, col:col + P] for w in eff],
                                               [x[:, k, bass.ds((b + f) * T, T)] for x in xT], start=(k == 0),
                                               stop=(k == KD - 1))
                        banks.filled_by(ins)
                    if follows and not f and n == NF - 2:
                        transpose_x(b)
                    if n == LAG:
                        pe.wait_ge(y_freed, b + 1)
                    if not f:
                        project_down(b, n - LAG)
                    elif not first:
                        ins = project_down(b, NF - LAG + n)
                if not follows:
                    for n in range(NF - LAG, NF):
                        ins = project_down(b, n)
                if not first:
                    ins.then_inc(y_done, 1)

            banks.all_free(pe)
            pe.sem_inc(y_freed, 1)
            every_batch(pe, body)


def attention1(nc, a, c, x_tok):
    PAD = WINDOW
    NS, NB = 4, H1 // 2

    def name_of(kind, tile):
        return f"{kind}{'+' * tile[0]}{tile[1]}"

    def steps(b, follows):
        if isinstance(b, int) and b < 0:
            return [dict(ln=(1, 0)), dict(ln=(1, 1), qk=(1, 0)), dict(ln=(1, 2), qk=(1, 1), s=(1, 0)),
                    dict(ln=(1, 3), qk=(1, 2), s=(1, 1), o=(1, 0))]
        out = []
        for t in range(2, TT + 2):
            tiles = [(0, n) if n < TT else (1, n - TT) for n in (t + 2, t + 1, t, t - 1, t - 2)]
            out.append({kind: tile for kind, tile in zip(("ln", "qk", "s", "o", "y"), tiles)
                        if follows or not tile[0]})
        return out

    def fills_of(b, follows):
        names = []
        for step in steps(b, follows):
            for kind, stage in (("qk", ("qk",)), ("p", ("p0_", "p1_", "p2_", "p3_")),
                                ("s", ("s0_", "s1_", "s2_", "s3_")), ("y", ("oT",)), ("o", ("o",)), ("ln", ("ln",)),
                                ("qk", ("ta", "tb", "tk"))):
                tile = step.get("o" if kind == "p" else kind)
                names += [name_of(n, tile) for n in stage] if tile else []
        return names

    with ExitStack() as ctx:
        def sb(name, shape, dt=F32):
            return ctx.enter_context(nc.sbuf_tensor(name, shape, dt))

        def sem(name):
            return ctx.enter_context(nc.semaphore(name))

        QK = D + DH1
        w_raw, wo, bo, rot_c, rot_s, mask_raw = attention1_landing(c)
        w_s = [sb(f"g_w_{s}", [P, KD, QK + DH1], F32R) for s in ("hi", "lo")]
        mask = sb("g_mask", [P, 2, NS, P], BF16)
        xT = [sb(f"g_xT_{s}", [P, KD, PAD + T], F32R) for s in ("hi", "lo")]
        xn, y = sb("g_xn", [P, TT, D]), sb("g_y", [P, TT, D])
        qk = sb("g_qk", [P, H1 + 1, DH1])
        turned = sb("g_turned", [P, H1 + 1, ROPE])
        q_st = sb("g_q_st", [P, H1, 4, DH1])
        k_st = sb("g_k_st", [P, 2, 4, DH1])
        qT = sb("g_qT", [P, 2, 2, NB, 64], F32R)
        kT = sb("g_kT", [P, PAD + T], F32R)
        vw = sb("g_vw", [P, 2 * TT, DH1 + 1])
        p = sb("g_p", [P, NS, 4 * P])
        pT = sb("g_pT", [P, NS, 4 * P])
        top = sb("g_top", [P, NS, 4])
        o = sb("g_o", [P, H1, DH1])
        oT = sb("g_oT", [P, KD, P])
        rinv = sb("g_rinv", [P, H1])
        banks = Banks(ctx, nc, "g", fills_of(0, True), 6, before=fills_of(-1, True), last=fills_of(B - 1, False),
                      rounds=B)
        y_ps = [ctx.enter_context(nc.psum_tensor(f"g_y_ps{n}", [P, 512], F32)) for n in range(2)]
        norm, norm_y = Norm(ctx, nc, c, "g"), Norm(ctx, nc, c, "gy")
        loaded = c["attention1_loaded"]
        w_ready, w_hi, mask_ready, pads = (sem(f"g_{s}") for s in ("w_ready", "w_hi", "mask_ready", "pads_ready"))
        xn_ready, xT_hi = sem("g_xn_ready"), sem("g_xT_hi_ready")
        rotated, qk_copied, keys_ready = sem("g_rotated"), sem("g_qk_copied"), sem("g_keys_ready")
        st_hi, st_ready = sem("g_st_hi_ready"), sem("g_st_ready")
        top_ready, exp_ready = sem("g_top_ready"), sem("g_exp_ready")
        rinv_ready = sem("g_rinv_ready")
        y_done, y_freed, y_normed, x_updated = (sem(f"g_{s}") for s in ("y_done", "y_freed", "y_normed", "x_updated"))
        block = ctx.enter_context(nc.Block())

        @block.sync
        def _(sp):
            load_experts(sp, a, c)

        @block.gpsimd
        def _(pool):
            nc.gpsimd.memset(kT[:, 0:PAD].bitcast(F32), 0.0).then_inc(pads, 1)
            for x in xT:
                nc.gpsimd.memset(x[:, :, 0:PAD].bitcast(F32), 0.0).then_inc(pads, 1)
            nc.gpsimd.memset(vw[:], 1.0).then_inc(pads, 1)

            def body(b, follows):
                if follows:
                    norm.inverse(pool, b + 1)
                if not isinstance(b, int) or b >= 0:
                    norm_y.inverse(pool, b)
                if follows and (not isinstance(b, int) or b >= 0):
                    pool.drain()
                    for i in range(TT):
                        ins = nc.gpsimd.tensor_scalar(y[:, i, :], y[:, i, :], norm_y.mv[:, i, 0:1],
                                                      norm_y.rstd[:, i:i + 1], ALU.subtract, ALU.mult)
                    ins.then_inc(y_normed, 1)
                    pool.wait_ge(y_normed, b + 1)
                    x_b = x_tok[:, bass.ds(b * TT, TT), :]
                    nc.gpsimd.tensor_tensor(x_b, x_b, y[:], ALU.add).then_inc(x_updated, 1)

            every_batch(pool, body)

        @block.scalar
        def _(act):
            act.wait_ge(loaded, 8 * DMA_INC)
            nc.scalar.activation(w_s[0][:], w_raw, ACT.Copy).then_inc(w_hi, 1)
            for v in range(2):
                nc.scalar.activation(mask[:, v], mask_raw[:, v].unsqueeze(1).broadcast_to([P, NS, P]),
                                     ACT.Copy).then_inc(mask_ready, 1)
            act.wait_ge(pads, 4)

            def hi_of_x(b, tile):
                f, t = tile
                banks.wait_filled(act, b, name_of("ln", tile))
                nc.scalar.activation(xT[0][:, :, PAD + t * P:PAD + (t + 1) * P],
                                     banks.bank(b, name_of("ln", tile))[:, 0:D].rearrange("p (k t) -> p k t", k=KD),
                                     ACT.Copy).then_inc(xT_hi, 1)

            def plain_qk(b, tile):
                f, t = tile
                name = name_of("qk", tile)
                banks.wait_filled(act, b, name)
                src = banks.bank(b, name)[:, 0:QK].rearrange("p (h d) -> p h d", d=DH1)
                if not (isinstance(b, int) and (b + f) * TT + t == 0):
                    act.wait_ge(st_ready, (b + f) * TT + t)
                nc.scalar.activation(qk[:, :, ROPE:DH1], src[:, :, ROPE:DH1], ACT.Copy).then_inc(qk_copied, 1)

            def keep_transposed(b, tile):
                t = tile[1]
                for n, kind in enumerate(("ta", "tb")):
                    name = name_of(kind, tile)
                    banks.wait_filled(act, b, name)
                    banks.freed_by(nc.scalar.activation(
                        qT[:, t % 2, :, 4 * n:4 * n + 4, :].rearrange("p s n q -> p n s q"),
                        banks.bank(b, name)[:].rearrange("p (n s q) -> p n s q", s=2, q=64), ACT.Copy), b, name)
                name = name_of("tk", tile)
                banks.wait_filled(act, b, name)
                bank = banks.bank(b, name)
                nc.scalar.activation(kT[:, PAD + t * P:PAD + (t + 1) * P], bank[:, 0:P], ACT.Copy).then_inc(
                    keys_ready, 1)
                banks.freed_by(nc.scalar.activation(
                    vw[:, 2 * t:2 * t + 2, 0:DH1], bank[:, P:P + 2 * DH1].rearrange("p (w d) -> p w d", d=DH1),
                    ACT.Copy), b, name)

            def exps(b, tile):
                for n in range(NS):
                    banks.wait_kept(act, b, name_of(f"s{n}_", tile))
                    nc.scalar.activation(p[:, n], p[:, n], ACT.Exp, scale=float(DH1) ** -0.5).then_inc(exp_ready, 1)

            def keep_pT(b, tile):
                for n in range(NS):
                    name = name_of(f"p{n}_", tile)
                    banks.wait_filled(act, b, name)
                    banks.freed_by(nc.scalar.activation(pT[:, n], banks.bank(b, name)[:], ACT.Copy), b, name)

            def keep_oT(b, tile):
                name = name_of("oT", tile)
                banks.wait_filled(act, b, name)
                banks.freed_by(nc.scalar.activation(oT[:].rearrange("p k t -> p (k t)"),
                                                    banks.bank(b, name)[:, 0:D], ACT.Copy), b, name)

            def body(b, follows):
                for step in steps(b, follows):
                    for kind, stage in (("qk", plain_qk), ("o", keep_pT), ("y", keep_oT), ("s", exps),
                                        ("ln", hi_of_x), ("qk", keep_transposed)):
                        if kind in step:
                            stage(b, step[kind])

            every_batch(act, body)

        @block.vector
        def _(dve):
            dve.wait_ge(w_hi, 1)
            nc.vector.tensor_tensor(w_s[1][:], w_raw, rounded(w_s[0][:]), ALU.subtract).then_inc(w_ready, 1)

            def rotate_and_stack(b, tile):
                f, t = tile
                nth = (b + f) * TT + t + 1
                name = name_of("qk", tile)
                dve.wait_ge(qk_copied, nth)
                src = banks.bank(b, name)[:, 0:QK].rearrange("p (h d) -> p h d", d=DH1)
                half = ROPE // 2

                def table(tab, lo, hi):
                    return tab[:, t, lo:hi].unsqueeze(1).broadcast_to([P, H1 + 1, hi - lo])

                nc.vector.tensor_tensor(qk[:, :, 0:ROPE], src[:, :, 0:ROPE], table(rot_c, 0, ROPE),
                                        ALU.mult)
                nc.vector.tensor_tensor(turned[:, :, 0:half], src[:, :, half:ROPE], table(rot_s, 0, half), ALU.mult)
                ins = nc.vector.tensor_tensor(turned[:, :, half:ROPE], src[:, :, 0:half], table(rot_s, half, ROPE),
                                              ALU.mult)
                banks.freed_by(ins, b, name)
                banks.wait_kept(dve, b, name)
                nc.vector.tensor_tensor(qk[:, :, 0:ROPE], qk[:, :, 0:ROPE], turned[:], ALU.add).then_inc(rotated, 1)
                dve.wait_ge(rotated, nth)
                q = qk[:, 0:H1, :].unsqueeze(2).broadcast_to([P, H1, 2, DH1])
                k = qk[:, H1:H1 + 1, :].broadcast_to([P, 2, DH1])
                nc.vector.tensor_copy(q_st[:, :, 0:2].bitcast(F32R), q)
                for r in (0, 2):
                    ins = nc.vector.tensor_copy(k_st[:, :, r].bitcast(F32R), k)
                ins.then_inc(st_hi, 1)
                dve.wait_ge(st_hi, nth)
                nc.vector.tensor_tensor(q_st[:, :, 2:4], q, q_st[:, :, 0:2], ALU.subtract)
                for r in (1, 3):
                    ins = nc.vector.tensor_tensor(k_st[:, :, r], k, k_st[:, :, r - 1], ALU.subtract)
                ins.then_inc(st_ready, 1)

            def shift_scores(b, tile):
                f, t = tile
                for n in range(NS):
                    nth = ((b + f) * TT + t) * NS + n + 1
                    name = name_of(f"s{n}_", tile)
                    banks.wait_filled(dve, b, name)
                    s = banks.bank(b, name)[:].rearrange("p (m k) -> p m k", k=P)
                    nc.vector.tensor_reduce(top[:, n], s, AX_X, ALU.max).then_inc(top_ready, 1)
                    dve.wait_ge(top_ready, nth)
                    banks.freed_by(nc.vector.tensor_tensor(
                        p[:, n].rearrange("p (m k) -> p m k", k=P), s,
                        top[:, n].unsqueeze(2).broadcast_to([P, 4, P]), ALU.subtract), b, name)

            def norm_o(b, tile):
                f, t = tile
                name = name_of("o", tile)
                banks.wait_filled(dve, b, name)
                src = banks.bank(b, name)[:, 0:H1 * (DH1 + 1)].rearrange("p (h d) -> p h d", d=DH1 + 1)
                nc.vector.reciprocal(rinv[:], src[:, :, DH1]).then_inc(rinv_ready, 1)
                dve.wait_ge(rinv_ready, (b + f) * TT + t + 1)
                banks.freed_by(nc.vector.tensor_tensor(o[:], src[:, :, 0:DH1],
                                                       rinv[:].unsqueeze(2).broadcast_to([P, H1, DH1]), ALU.mult),
                               b, name)

            def lo_of_x(b, tile):
                f, t = tile
                dve.wait_ge(xT_hi, (b + f) * TT + t + 1)
                cols = slice(PAD + t * P, PAD + (t + 1) * P)
                banks.freed_by(nc.vector.tensor_tensor(
                    xT[1][:, :, cols], banks.bank(b, name_of("ln", tile))[:, 0:D].rearrange("p (k t) -> p k t", k=KD),
                    rounded(xT[0][:, :, cols]), ALU.subtract), b, name_of("ln", tile))

            def norm_before(nb):
                norm.wait_inverse(dve, nb)
                for i in range(TT):
                    norm.apply(xn[:, i, :], x_tok[:, bass.ds(nb * TT + i, 1), :], i).then_inc(xn_ready, 1)

            def moments_behind(b, follows):
                dve.wait_ge(y_done, b + 1)
                if not follows:
                    dve.wait_ge(x_updated, b)
                for n in range(2):
                    ins = nc.vector.tensor_tensor(y[:, 2 * n:2 * n + 2, :], y_ps[n][:].rearrange("p (t d) -> p t d", d=D),
                                                  bo.unsqueeze(1).broadcast_to([P, 2, D]), ALU.add)
                ins.then_inc(y_freed, 1)
                dve.wait_ge(y_freed, b + 2)
                norm_y.moments(dve, lambda i: y[:, i, :])
                if not follows:
                    norm_y.wait_inverse(dve, b)
                    for i in range(TT):
                        ins = norm_y.apply(y[:, i, :], y[:, i, :], i)
                    ins.then_inc(y_normed, 1)
                    dve.wait_ge(y_normed, b + 1)
                    x_b = x_tok[:, bass.ds(b * TT, TT), :]
                    nc.vector.tensor_tensor(x_b, x_b, y[:], ALU.add).then_inc(x_updated, 1)

            def body(b, follows):
                first = isinstance(b, int) and b < 0
                if first:
                    norm.moments(dve, lambda i: x_tok[:, i, :])
                    norm_before(0)
                elif follows:
                    norm.moments(dve, lambda i: x_tok[:, bass.ds((b + 1) * TT + i, 1), :])
                for n, step in enumerate(steps(b, follows)):
                    if "qk" in step:
                        rotate_and_stack(b, step["qk"])
                    if follows and not first and n == 0:
                        norm_before(b + 1)
                    for kind, stage in (("s", shift_scores), ("o", norm_o), ("ln", lo_of_x)):
                        if kind in step:
                            stage(b, step[kind])
                if not first:
                    moments_behind(b, follows)

            every_batch(dve, body)

        @block.tensor
        def _(pe):
            def transpose_x(b, tile):
                f, t = tile
                name = name_of("ln", tile)
                banks.wait_freed(pe, b, name)
                pe.wait_ge(xn_ready, (b + f) * TT + t + 1)
                for k in range(KD):
                    ins = pe.transpose(banks.bank(b, name)[:, k * P:(k + 1) * P], xn[:, t, k * P:(k + 1) * P],
                                       c["ident"][:])
                banks.filled_by(ins)

            def project_qk(b, tile):
                t = tile[1]
                name = name_of("qk", tile)
                banks.wait_freed(pe, b, name)
                if tile[0]:
                    banks.wait_kept(pe, b, name_of("ln", tile))
                for k in range(KD):
                    ins = three_passes(pe, banks.bank(b, name)[:, 0:QK],
                                       [x[:, k, PAD + t * P:PAD + (t + 1) * P] for x in xT],
                                       [w[:, k, 0:QK] for w in w_s], start=(k == 0), stop=(k == KD - 1))
                banks.filled_by(ins)

            def transpose_qk(b, tile):
                f, t = tile
                pe.wait_ge(st_ready, (b + f) * TT + t + 1)
                for n, kind in enumerate(("ta", "tb")):
                    name = name_of(kind, tile)
                    banks.wait_freed(pe, b, name)
                    for m in range(4):
                        two = q_st[:, 8 * n + 2 * m:8 * n + 2 * m + 2].rearrange("p h r d -> p (h r d)")
                        ins = pe.transpose(banks.bank(b, name)[:, m * P:(m + 1) * P], two, c["ident"][:])
                    banks.filled_by(ins)
                name = name_of("tk", tile)
                banks.wait_freed(pe, b, name)
                pe.transpose(banks.bank(b, name)[:, 0:P], k_st[:].rearrange("p h r d -> p (h r d)"), c["ident"][:])
                for w in range(2 * t, 2 * t + 2):
                    col = P + (w - 2 * t) * DH1
                    for k in range(KD):
                        ins = three_passes(pe, banks.bank(b, name)[:, col:col + DH1],
                                           [x[:, k, w * 64:w * 64 + P] for x in xT],
                                           [ww[:, k, QK:QK + DH1] for ww in w_s], start=(k == 0),
                                           stop=(k == KD - 1))
                banks.filled_by(ins)

            def scores(b, tile):
                f, t = tile
                pe.wait_ge(keys_ready, (b + f) * TT + t + 1)
                for n in range(NS):
                    half, odd = n // 2, n % 2
                    w = 2 * t + half
                    name = name_of(f"s{n}_", tile)
                    banks.wait_freed(pe, b, name)
                    rows = slice(64 * odd, 64 * odd + 64)
                    pe.matmul(banks.bank(b, name)[:], c["ident_bf"][:],
                              mask[:, min(w, 1)].rearrange("p m k -> p (m k)"), start=True, stop=False)
                    for m in range(4):
                        ins = pe.matmul(banks.bank(b, name)[:, m * P:(m + 1) * P],
                                        qT[rows, t % 2, half, 2 * m:2 * m + 2, :].rearrange("p n q -> p (n q)"),
                                        kT[rows, w * 64:w * 64 + P], start=False, stop=(m == 3))
                    banks.filled_by(ins)

            def transpose_p(b, tile):
                f, t = tile
                for n in range(NS):
                    name = name_of(f"p{n}_", tile)
                    pe.wait_ge(exp_ready, ((b + f) * TT + t) * NS + n + 1)
                    banks.wait_freed(pe, b, name)
                    for m in range(4):
                        ins = pe.transpose(banks.bank(b, name)[:, m * P:(m + 1) * P], p[:, n, m * P:(m + 1) * P],
                                           c["ident"][:])
                    banks.filled_by(ins)

            def attend(b, tile):
                t = tile[1]
                name = name_of("o", tile)
                banks.wait_freed(pe, b, name)
                for n in range(NS):
                    banks.wait_kept(pe, b, name_of(f"p{n}_", tile))
                    for m in range(4):
                        col = (n * 4 + m) * (DH1 + 1)
                        ins = pe.matmul(banks.bank(b, name)[:, col:col + DH1 + 1], pT[:, n, m * P:(m + 1) * P],
                                        vw[:, 2 * t + n // 2, :], start=True, stop=True)
                banks.filled_by(ins)

            def transpose_o(b, tile):
                t = tile[1]
                name = name_of("oT", tile)
                banks.wait_freed(pe, b, name)
                if t:
                    banks.wait_kept(pe, b, name_of("o", tile))
                for k in range(KD):
                    ins = pe.transpose(banks.bank(b, name)[:, k * P:(k + 1) * P],
                                       o[:].rearrange("p h d -> p (h d)")[:, k * P:(k + 1) * P], c["ident"][:])
                banks.filled_by(ins)

            def out_project(b, tile):
                t = tile[1]
                banks.wait_kept(pe, b, name_of("oT", tile))
                if t == 0:
                    pe.wait_ge(y_freed, b + 1)
                for half in range(2):
                    for two in range(2):
                        ins = pe.matmul(y_ps[t // 2][64 * half:64 * half + 64, t % 2 * D:(t % 2 + 1) * D],
                                        oT[:, half, 64 * two:64 * two + 64], wo[:, two, :], start=(two == 0),
                                        stop=(two == 1))
                if t == TT - 1:
                    ins.then_inc(y_done, 1)

            def body(b, follows):
                for step in steps(b, follows):
                    for kind, stage in (("qk", project_qk), ("o", transpose_p), ("s", scores), ("y", transpose_o),
                                        ("o", attend), ("y", out_project), ("ln", transpose_x),
                                        ("qk", transpose_qk)):
                        if kind in step:
                            stage(b, step[kind])
                if follows:
                    banks.wait_kept(pe, b, name_of("ln", (1, TT - 1)))
                    banks.wait_kept(pe, b, name_of("o", (1, 0)))

            banks.all_free(pe)
            pe.sem_inc(y_freed, 1)
            pe.wait_ge(w_ready, 1)
            pe.wait_ge(mask_ready, 2)
            every_batch(pe, body)


def experts(nc, a, c, x_tok, out):
    E1 = E + 1
    ROWS = E * NT
    LAG = 2
    ahead = ["a+0", "b+0", "a+1", "b+1"]
    fills, last = [], []
    for names, follows in ((fills, True), (last, False)):
        for e in range(LAG, E1):
            names += [f"a{e}", f"b{e}", f"y{e - LAG}_0", f"y{e - LAG}_1"]
        for e in range(LAG):
            names += ahead[2 * e:2 * e + 2] * follows + [f"y{E1 - LAG + e}_0", f"y{E1 - LAG + e}_1"]

    with ExitStack() as ctx:
        def sb(name, shape, dt=F32):
            return ctx.enter_context(nc.sbuf_tensor(name, shape, dt))

        def sem(name):
            return ctx.enter_context(nc.semaphore(name))

        w1_s = [sb(f"m_w1_{s}", [P, KD, E1, 2 * P], F32R) for s in ("hi", "lo")]
        w2_s = [sb(f"m_w2_{s}", [P, E1, D], F32R) for s in ("hi", "lo")]
        xT = [sb(f"m_xT_{s}", [P, KD, B * T], F32R) for s in ("hi", "lo")]
        w_tok = sb("m_w_tok", [P, E, NT])

        with ExitStack() as inner:
            def sbi(name, shape, dt=F32):
                return inner.enter_context(nc.sbuf_tensor(name, shape, dt))

            def semi(name):
                return inner.enter_context(nc.semaphore(name))

            w1, w2 = experts_landing(c)
            gw = sbi("m_gw", [P, KD, E1])
            gw_s = [sbi(f"m_gw_{s}", [P, KD, E1], F32R) for s in ("hi", "lo")]
            bias = sbi("m_bias", [E1, 1])
            below = sbi("m_below", [P, E, E])
            same, before = sbi("m_same", [P, ROWS]), sbi("m_before", [P, ROWS])
            units, steps = sbi("m_units", [P, DIGITS], I32), sbi("m_steps", [P, DIGITS, WAYS], I32)
            xn = sbi("m_xn", [P, NT, D])
            logits_t = sbi("m_logits_t", [P, T])
            logits = sbi("m_logits", [P, E, NT])
            aff = sbi("m_aff", [P, E, NT])
            more, ties = sbi("m_more", [P, NT, E, E]), sbi("m_ties", [P, NT, E, E])
            rank, off = sbi("m_rank", [P, E, NT]), sbi("m_off", [P, E, NT])
            score = sbi("m_score", [P, E, NT])
            s_row, gt, eq, upto = (sbi(f"m_{s}", [P, P]) for s in ("s_row", "gt", "eq", "upto"))
            zeros = sbi("m_zeros", [P, P])
            found, step = (sbi(f"m_{s}", [P, 1], I32) for s in ("found", "step"))
            cand = sbi("m_cand", [P, WAYS], I32)
            unused = sbi("m_unused", [P, WAYS, P])
            reached = sbi("m_reached", [P, WAYS])
            counts, digit = sbi("m_counts", [P, WAYS]), sbi("m_digit", [P, 1])
            n_gt, n_eq, room = (sbi(f"m_{s}", [P, 1]) for s in ("n_gt", "n_eq", "room"))
            banks = Banks(inner, nc, "n", ["lt", "ln+0", "ln+1", "logits"], 4, before=["ln+0", "ln+1"],
                          last=["lt", "logits"], rounds=B)
            sel_ps = [inner.enter_context(nc.psum_tensor(f"sel{n}", [P, 512], F32)) for n in range(3)]
            norm = Norm(inner, nc, c, "n", NT)
            loaded, w_hi, gw_hi, gw_ready = (semi(f"n_{s}") for s in ("loaded", "w_hi", "gw_hi", "gw_ready"))
            zeroed = semi("n_zeroed")
            xn_ready, xT_hi = semi("n_xn_ready"), semi("n_xT_hi_ready")
            exp_ready = semi("n_exp_ready")
            searched = semi("n_search_step")
            chain = semi("n_selection_step")
            score_ready, score_t = semi("n_score_ready"), semi("n_score_transposed")
            counted, summed = semi("n_counted"), semi("n_summed")
            totals_asked, totals = semi("n_totals_asked"), semi("n_totals")
            weights_ready, weights_t = semi("n_weights_ready"), semi("n_weights_transposed")
            block = inner.enter_context(nc.Block())

            @block.sync
            def _(sp):
                for dst, src in ((gw, "L1_ffn_gate_w"), (bias, "L1_ffn_expert_bias"), (below, "c_below"),
                                 (same, "c_same"), (before, "c_before"), (units, "c_units"), (steps, "c_steps")):
                    ap = a[src]
                    sp.dma_start(dst[:], ap).then_inc(loaded, DMA_INC)

            @block.gpsimd
            def _(pool):
                nc.gpsimd.memset(logits_t[:], 0.0).then_inc(zeroed, 1)
                nc.gpsimd.memset(zeros[:], 0.0).then_inc(zeroed, 1)
                nc.gpsimd.memset(found[:], 0).then_inc(zeroed, 1)
                norm.inverse(pool, 0)
                pool.wait_ge(w_hi, KD + 1)
                for k in range(KD):
                    nc.gpsimd.tensor_tensor(w1_s[1][:, k], w1[:, k], rounded(w1_s[0][:, k]), ALU.subtract)
                nc.gpsimd.tensor_tensor(w2_s[1][:], w2, rounded(w2_s[0][:]), ALU.subtract)

            @block.scalar
            def _(act):
                act.wait_ge(loaded, 7 * DMA_INC)
                nc.scalar.activation(gw_s[0][:], gw[:], ACT.Copy).then_inc(gw_hi, 1)

                act.wait_ge(zeroed, 1)

                def body(b, follows):
                    if b >= 0:
                        banks.wait_filled(act, b, "lt")
                        banks.freed_by(nc.scalar.activation(logits_t[0:E1, :], banks.bank(b, "lt")[0:E1, :], ACT.Identity,
                                                            bias=bias[:, 0:1]), b, "lt")
                    for k in range(KD if follows else 0):
                        banks.wait_filled(act, b, f"ln+{k}")
                        nc.scalar.activation(xT[0][:, k, bass.ds((b + 1) * T, T)], banks.bank(b, f"ln+{k}")[:],
                                             ACT.Copy).then_inc(xT_hi, 1)

                for b in range(-1, B):
                    body(b, b + 1 < B)
                banks.wait_kept(act, B - 1, "logits")
                nc.scalar.activation(aff[:], logits[:], ACT.Exp, scale=-1.0).then_inc(exp_ready, 1)
                act.wait_ge(c["experts_loaded"], 2 * DMA_INC)
                for k in range(KD):
                    nc.scalar.activation(w1_s[0][:, k], w1[:, k], ACT.Copy).then_inc(w_hi, 1)
                nc.scalar.activation(w2_s[0][:], w2, ACT.Copy).then_inc(w_hi, 1)

            @block.vector
            def _(dve):
                norm.moments(dve, lambda i: x_tok[:, i, :])
                norm.wait_inverse(dve, 0)
                for i in range(NT):
                    norm.apply(xn[:, i, :], x_tok[:, i, :], i).then_inc(xn_ready, 1)
                    if i == TT - 1:
                        dve.wait_ge(gw_hi, 1)
                        nc.vector.tensor_tensor(gw_s[1][:], gw[:], rounded(gw_s[0][:]), ALU.subtract).then_inc(
                            gw_ready, 1)

                def body(b, follows):
                    first = b < 0
                    if not first:
                        banks.wait_filled(dve, b, "logits")
                        src = banks.bank(b, "logits")[:].rearrange("p (t e) -> p e t", e=P)[:, 0:E, :]
                        banks.freed_by(nc.vector.tensor_copy(logits[:, :, bass.ds(b * TT, TT)], src), b, "logits")
                    for k in range(KD if follows else 0):
                        cols = bass.ds((b + 1) * T, T)
                        dve.wait_ge(xT_hi, (b + 1) * KD + k + 1)
                        banks.freed_by(nc.vector.tensor_tensor(xT[1][:, k, cols], banks.bank(b, f"ln+{k}")[:],
                                                               rounded(xT[0][:, k, cols]), ALU.subtract),
                                       b, f"ln+{k}")

                for b in range(-1, B):
                    body(b, b + 1 < B)
                done = [0]

                def then(ins):
                    done[0] += 1
                    ins.then_inc(chain, 1)
                    dve.wait_ge(chain, done[0])

                dve.wait_ge(exp_ready, 1)
                then(nc.vector.tensor_scalar(aff[:], aff[:], 1.0, None, ALU.add))
                then(nc.vector.reciprocal(aff[:], aff[:]))
                rival = aff[:].rearrange("p e t -> p t e").unsqueeze(2).broadcast_to([P, NT, E, E])
                own = aff[:].rearrange("p e t -> p t e").unsqueeze(3).broadcast_to([P, NT, E, E])
                nc.vector.tensor_tensor(more[:], rival, own, ALU.is_gt)
                then(nc.vector.tensor_tensor(ties[:], rival, own, ALU.is_equal))
                lower = below[:].unsqueeze(1).broadcast_to([P, NT, E, E])
                then(nc.vector.tensor_tensor(ties[:], ties[:], lower, ALU.mult))
                then(nc.vector.tensor_tensor(more[:], more[:], ties[:], ALU.add))
                then(nc.vector.tensor_reduce(rank[:].rearrange("p e t -> p t e"), more[:], AX_X, ALU.add))
                then(nc.vector.tensor_scalar(off[:], rank[:], TOP_K - 0.5, -1.0, ALU.is_lt, ALU.add))
                then(nc.vector.scalar_tensor_tensor(out=score[:], in0=off[:], scalar=1.0, in1=aff[:], op0=ALU.add,
                                                    op1=ALU.mult))
                nc.vector.tensor_tensor(score[:], score[:], off[:], ALU.add).then_inc(score_ready, 1)
                dve.wait_ge(score_t, 1)
                then(nc.vector.tensor_copy(s_row[0:ROWS, :], sel_ps[0][0:ROWS, 0:P]))
                dve.wait_ge(zeroed, 3)
                def search_digit(n):
                    nc.vector.tensor_tensor(cand[0:ROWS], found[0:ROWS].broadcast_to([ROWS, WAYS]),
                                            steps[0:ROWS, bass.ds(n, 1), :].rearrange("p o w -> p (o w)"),
                                            ALU.bitwise_or).then_inc(searched, 1)
                    dve.wait_ge(searched, n * 4 + 1)
                    for w in range(WAYS):
                        ins = nc.vector.tensor_scalar(unused[0:ROWS, w], s_row[0:ROWS], cand[0:ROWS, w:w + 1].bitcast(F32),
                                                      None, ALU.is_ge, ALU.add, accum_out=counts[0:ROWS, w:w + 1])
                    ins.then_inc(counted, 1)
                    dve.wait_ge(summed, n + 1)
                    nc.vector.tensor_scalar(reached[0:ROWS], sel_ps[1][0:ROWS, 0:WAYS], float(CAPACITY), None,
                                            ALU.is_ge, ALU.add, accum_out=digit[0:ROWS]).then_inc(searched, 1)
                    dve.wait_ge(searched, n * 4 + 2)
                    nc.vector.tensor_tensor(step[0:ROWS], digit[0:ROWS], units[0:ROWS, bass.ds(n, 1)],
                                            ALU.mult).then_inc(searched, 1)
                    dve.wait_ge(searched, n * 4 + 3)
                    nc.vector.tensor_tensor(found[0:ROWS], found[0:ROWS], step[0:ROWS],
                                            ALU.bitwise_or).then_inc(searched, 1)
                    dve.wait_ge(searched, n * 4 + 4)
                with dve.Fori(0, DIGITS // UNROLL) as turn:
                    for k in range(UNROLL):
                        search_digit(turn * UNROLL + k)
                bound = found[0:ROWS, 0:1].bitcast(F32)
                nc.vector.tensor_scalar(gt[0:ROWS], s_row[0:ROWS], bound, None, ALU.is_gt, ALU.add,
                                        accum_out=n_gt[0:ROWS])
                nc.vector.tensor_scalar(eq[0:ROWS], s_row[0:ROWS], bound, None, ALU.is_equal, ALU.add,
                                        accum_out=n_eq[0:ROWS]).then_inc(totals_asked, 1)
                dve.wait_ge(totals_asked, 1)
                then(nc.vector.tensor_tensor_scan(upto[0:ROWS], eq[0:ROWS], zeros[0:ROWS], 0.0, ALU.add, ALU.add))
                dve.wait_ge(totals, 1)
                then(nc.vector.tensor_scalar(room[0:ROWS], sel_ps[1][0:ROWS, 0:1], -1.0, float(CAPACITY), ALU.mult,
                                             ALU.add))
                then(nc.vector.scalar_tensor_tensor(out=eq[0:ROWS], in0=upto[0:ROWS], scalar=room[0:ROWS, 0:1],
                                                    in1=eq[0:ROWS], op0=ALU.is_le, op1=ALU.mult))
                then(nc.vector.tensor_tensor(gt[0:ROWS], gt[0:ROWS], eq[0:ROWS], ALU.add))
                nc.vector.tensor_tensor(s_row[0:ROWS], s_row[0:ROWS], gt[0:ROWS], ALU.mult).then_inc(weights_ready, 1)
                dve.wait_ge(weights_t, 1)
                nc.vector.tensor_copy(w_tok[:].rearrange("p e t -> p (e t)"), sel_ps[2][:, 0:ROWS])

            @block.tensor
            def _(pe):
                banks.all_free(pe)

                def body(b, follows):
                    first = b < 0
                    if not first:
                        banks.wait_freed(pe, b, "lt")
                        if b == 0:
                            pe.wait_ge(gw_ready, 1)
                        for k in range(KD):
                            ins = three_passes(pe, banks.bank(b, "lt")[0:E1, :], [w[:, k, :] for w in gw_s],
                                               [x[:, k, bass.ds(b * T, T)] for x in xT], start=(k == 0),
                                               stop=(k == KD - 1))
                        banks.filled_by(ins)
                    for k in range(KD if follows else 0):
                        banks.wait_freed(pe, b, f"ln+{k}")
                        for i in range(TT):
                            if k == 0:
                                pe.wait_ge(xn_ready, (b + 1) * TT + i + 1)
                            ins = pe.transpose(banks.bank(b, f"ln+{k}")[:, i * P:(i + 1) * P],
                                               xn[:, (b + 1) * TT + i, k * P:(k + 1) * P], c["ident"][:])
                        banks.filled_by(ins)
                    if not first:
                        banks.wait_freed(pe, b, "logits")
                        banks.wait_kept(pe, b, "lt")
                        for i in range(TT):
                            ins = pe.transpose(banks.bank(b, "logits")[:, i * P:(i + 1) * P],
                                               logits_t[:, i * P:(i + 1) * P], c["ident"][:])
                        banks.filled_by(ins)
                    for k in range(KD if follows else 0):
                        banks.wait_kept(pe, b, f"ln+{k}")

                for b in range(-1, B):
                    body(b, b + 1 < B)
                pe.wait_ge(score_ready, 1)
                pe.transpose(sel_ps[0][0:ROWS, 0:P], score[:].rearrange("p e t -> p (e t)"), c["ident"][:]).then_inc(
                    score_t, 1)
                with pe.Fori(0, DIGITS // UNROLL) as turn:
                    for k in range(UNROLL):
                        pe.wait_ge(counted, turn * UNROLL + k + 1)
                        pe.matmul(sel_ps[1][0:ROWS, 0:WAYS], same[0:ROWS, 0:ROWS], counts[0:ROWS], start=True,
                                  stop=True).then_inc(summed, 1)
                pe.wait_ge(totals_asked, 1)
                pe.matmul(sel_ps[1][0:ROWS, 0:1], same[0:ROWS, 0:ROWS], n_gt[0:ROWS, 0:1], start=True, stop=False)
                pe.matmul(sel_ps[1][0:ROWS, 0:1], before[0:ROWS, 0:ROWS], n_eq[0:ROWS, 0:1], start=False,
                          stop=True).then_inc(totals, 1)
                pe.wait_ge(weights_ready, 1)
                pe.transpose(sel_ps[2][:, 0:ROWS], s_row[0:ROWS, :], c["ident"][0:ROWS, 0:ROWS]).then_inc(weights_t, 1)

        acc = sb("m_acc", [P, TT, D])
        gate = sb("m_gate", [P, 2, T])
        h = sb("m_h", [P, 2, T])
        h_s = [sb(f"m_h_{s}", [P, 2 * LAG, T], F32R) for s in ("hi", "lo")]
        banks = Banks(ctx, nc, "m", fills, 8, before=ahead, last=last, rounds=B)
        norm = Norm(ctx, nc, c, "m")
        h_hi, h_lo = sem("m_h_hi_ready"), sem("m_h_lo_ready")
        y_normed, x_updated, stored = (sem(f"m_{s}") for s in ("y_normed", "x_updated", "stored"))

        def turns(b, follows):
            own = [] if isinstance(b, int) and b < 0 else [(0, e) for e in range(LAG, E1)]
            return own + [(1, e) for e in range(LAG)] * follows

        def name_of(kind, turn):
            return f"{kind}{'+' * turn[0]}{turn[1]}"

        block = ctx.enter_context(nc.Block())

        @block.sync
        def _(sp):
            for b in range(B):
                sp.wait_ge(x_updated, b + 1)
                sp.dma_start(out[b].rearrange("(t p) d -> p t d", p=P), x_tok[:, b * TT:(b + 1) * TT, :]).then_inc(
                    stored, DMA_INC)
            sp.wait_ge(stored, B * DMA_INC)

        @block.gpsimd
        def _(pool):
            def body(b, follows):
                for f, e in turns(b, follows):
                    pool.wait_ge(h_hi, (b + f) * E1 + e + 1)
                    nc.gpsimd.tensor_tensor(h_s[1][:, e % (2 * LAG)], h[:, e % 2], rounded(h_s[0][:, e % (2 * LAG)]),
                                            ALU.subtract).then_inc(h_lo, 1)
                if not isinstance(b, int) or b >= 0:
                    norm.inverse(pool, b)

            every_batch(pool, body)

        @block.scalar
        def _(act):
            def body(b, follows):
                for turn in turns(b, follows):
                    e, name = turn[1], name_of("b", turn)
                    banks.wait_filled(act, b, name)
                    banks.freed_by(nc.scalar.activation(gate[:, e % 2], banks.bank(b, name)[:], ACT.Silu), b, name)
                    banks.wait_kept(act, b, name_of("a", turn))
                    nc.scalar.activation(h_s[0][:, e % (2 * LAG)], h[:, e % 2], ACT.Copy).then_inc(h_hi, 1)

            every_batch(act, body)

        @block.vector
        def _(dve):
            def gather(b, e):
                for n in range(2):
                    name = f"y{e}_{n}"
                    banks.wait_filled(dve, b, name)
                    if e:
                        banks.wait_kept(dve, b, f"y{e - 1}_{n}")
                    for j in range(2):
                        i = 2 * n + j
                        y = banks.bank(b, name)[:, j * D:(j + 1) * D]
                        if e == 0:
                            ins = nc.vector.tensor_copy(acc[:, i, :], y)
                        else:
                            ins = nc.vector.scalar_tensor_tensor(
                                out=acc[:, i, :], in0=y, scalar=w_tok[:, e - 1, bass.ds(b * TT + i, 1)],
                                in1=acc[:, i, :], op0=ALU.mult, op1=ALU.add)
                    banks.freed_by(ins, b, name)

            def body(b, follows):
                for f, e in turns(b, follows):
                    up, gt = name_of("a", (f, e)), name_of("b", (f, e))
                    banks.wait_filled(dve, b, up)
                    banks.wait_kept(dve, b, gt)
                    before = (b + f) * E1 + e - 1
                    if not isinstance(b, int) or before >= 1:
                        dve.wait_ge(h_lo, before)
                    banks.freed_by(nc.vector.tensor_tensor(h[:, e % 2], banks.bank(b, up)[:], gate[:, e % 2],
                                                           ALU.mult), b, up)
                    if not f:
                        gather(b, e - LAG)
                    elif not isinstance(b, int) or b >= 0:
                        gather(b, E1 - LAG + e)
                if not follows:
                    for e in range(E1 - LAG, E1):
                        gather(b, e)
                if not isinstance(b, int) or b >= 0:
                    for n in range(2):
                        banks.wait_kept(dve, b, f"y{E1 - 1}_{n}")
                    norm.moments(dve, lambda i: acc[:, i, :])
                    norm.wait_inverse(dve, b)
                    for i in range(TT):
                        ins = norm.apply(acc[:, i, :], acc[:, i, :], i)
                    ins.then_inc(y_normed, 1)
                    dve.wait_ge(y_normed, b + 1)
                    x_b = x_tok[:, bass.ds(b * TT, TT), :]
                    nc.vector.tensor_tensor(x_b, x_b, acc[:], ALU.add).then_inc(x_updated, 1)
                    dve.wait_ge(x_updated, b + 1)

            every_batch(dve, body)

        @block.tensor
        def _(pe):
            def project_down(b, e):
                pe.wait_ge(h_lo, b * E1 + e + 1)
                for n in range(2):
                    name = f"y{e}_{n}"
                    banks.wait_freed(pe, b, name)
                    for j in range(2):
                        i = 2 * n + j
                        ins = three_passes(pe, banks.bank(b, name)[:, j * D:(j + 1) * D],
                                           [x[:, e % (2 * LAG), i * P:(i + 1) * P] for x in h_s],
                                           [w[:, e, :] for w in w2_s], start=True, stop=True)
                    banks.filled_by(ins)

            def body(b, follows):
                for f, e in turns(b, follows):
                    for kind, half in (("a", 0), ("b", 1)):
                        name = name_of(kind, (f, e))
                        banks.wait_freed(pe, b, name)
                        for k in range(KD):
                            ins = three_passes(pe, banks.bank(b, name)[:],
                                               [w[:, k, e, half * P:(half + 1) * P] for w in w1_s],
                                               [x[:, k, bass.ds((b + f) * T, T)] for x in xT], start=(k == 0),
                                               stop=(k == KD - 1))
                        banks.filled_by(ins)
                    if not f:
                        project_down(b, e - LAG)
                    elif not isinstance(b, int) or b >= 0:
                        project_down(b, E1 - LAG + e)
                if not follows:
                    for e in range(E1 - LAG, E1):
                        project_down(b, e)

            banks.all_free(pe)
            every_batch(pe, body)


def layers(nc, a, out):
    with ExitStack() as ctx:
        c = {}
        x_tok = ctx.enter_context(nc.sbuf_tensor("x_tok", [P, NT, D], F32))
        c["ident"] = ctx.enter_context(nc.sbuf_tensor("ident", [P, P], F32))
        c["ident_bf"] = ctx.enter_context(nc.sbuf_tensor("ident_bf", [P, P], BF16))
        c["causal"] = ctx.enter_context(nc.sbuf_tensor("causal", [P, P], F32))
        c["causal_bf"] = ctx.enter_context(nc.sbuf_tensor("causal_bf", [P, P], BF16))
        c["minus_half"] = ctx.enter_context(nc.sbuf_tensor("minus_half", [P, NT], F32))
        c["landing"] = ctx.enter_context(nc.sbuf_tensor("landing", [P, T * H], F32))
        for name in ("ffn0_ug", "ffn0_down", "attention1", "experts"):
            c[f"{name}_loaded"] = ctx.enter_context(nc.semaphore(f"{name}_loaded"))
        const_loaded = ctx.enter_context(nc.semaphore("const_loaded"))
        const_ready = ctx.enter_context(nc.semaphore("const_ready"))
        with nc.Block() as block:
            @block.sync
            def _(sp):
                sp.dma_start(c["ident"][:], a["c_ident"]).then_inc(const_loaded, DMA_INC)
                sp.dma_start(c["causal"][:], a["c_causal"]).then_inc(const_loaded, DMA_INC)
            @block.gpsimd
            def _(pool):
                nc.gpsimd.memset(c["minus_half"][:], -0.5).then_inc(const_ready, 1)
            @block.vector
            def _(dve):
                dve.wait_ge(const_loaded, 2 * DMA_INC)
                nc.vector.tensor_copy(c["ident_bf"][:], c["ident"][:]).then_inc(const_ready, 1)
                nc.vector.tensor_copy(c["causal_bf"][:], c["causal"][:]).then_inc(const_ready, 1)
        attention0(nc, a, c, x_tok)
        ffn0(nc, a, c, x_tok)
        attention1(nc, a, c, x_tok)
        experts(nc, a, c, x_tok, out)


_INS = ['L0_attn_x', 'L0_attn_Wq', 'L0_attn_bq', 'L0_attn_Wk', 'L0_attn_bk', 'L0_attn_Wv', 'L0_attn_bv', 'L0_attn_Wo',
        'L0_attn_bo', 'L0_ffn_SU_ug', 'L0_ffn_SU_dp', 'L0_ffn_Wscale_ug', 'L0_ffn_Wscale_dp', 'L0_ffn_W_up',
        'L0_ffn_W_gate', 'L0_ffn_W_down', 'L1_attn_Wq', 'L1_attn_Wk', 'L1_attn_Wv', 'L1_attn_Wo', 'L1_attn_bo',
        'L1_ffn_gate_w', 'L1_ffn_expert_bias', 'L1_ffn_shared_w1', 'L1_ffn_shared_w2', 'L1_ffn_routed_w1',
        'L1_ffn_routed_w2']


def kernel(**inputs):
    import concourse.bacc as _bacc
    from concourse.bass_utils import run_bass_kernel_spmd as _run

    nc = _bacc.Bacc("TRN2", target_bir_lowering=False, num_devices=1)
    arrays, args = {}, {}
    given = {name: np.asarray(inputs[name]) for name in _INS}
    for name in ("L0_attn_bq", "L0_attn_bk", "L0_attn_bv"):
        given[name] = given[name].reshape(H, DH).T
    for name in ("L0_attn_bo", "L0_ffn_Wscale_dp", "L1_attn_bo"):
        given[name] = given[name].reshape(1, -1)
    for name in ("L0_ffn_SU_ug", "L0_ffn_SU_dp"):
        given[name] = given[name].reshape(-1, P).T
    scales = given.pop("L0_ffn_Wscale_ug").reshape(2, -1, P)
    given["L0_ffn_Wscale_up"], given["L0_ffn_Wscale_gate"] = scales[0].T, scales[1].T
    w1 = np.concatenate([given.pop("L1_ffn_shared_w1"), given.pop("L1_ffn_routed_w1")])
    given["L1_ffn_w1"] = w1.reshape(E + 1, KD, P, D).transpose(2, 1, 0, 3)
    w2 = np.concatenate([given.pop("L1_ffn_shared_w2"), given.pop("L1_ffn_routed_w2")])
    given["L1_ffn_w2"] = w2.transpose(1, 0, 2)
    given["L1_ffn_expert_bias"] = np.pad(given["L1_ffn_expert_bias"], (0, 1)).reshape(-1, 1)
    gate = np.pad(given["L1_ffn_gate_w"], ((0, 0), (0, 1)))
    given["L1_ffn_gate_w"] = gate.reshape(KD, P, E + 1).transpose(1, 0, 2)
    given["L1_attn_Wo"] = given["L1_attn_Wo"].reshape(4, 2, 2, DH1, D).transpose(1, 2, 0, 3, 4).reshape(D, D)
    for name in ("L0_ffn_W_up", "L0_ffn_W_gate", "L0_ffn_W_down"):
        given[name] = given[name].T
    for name, a in (given | shape_constants()).items():
        a = np.ascontiguousarray(a)
        arrays[f"in_{name}"] = a
        args[name] = nc.dram_tensor(f"in_{name}", a.shape, mybir.dt.from_np(a.dtype), kind="ExternalInput").ap()
    out = nc.dram_tensor("out_x", (B, T, D), F32, kind="ExternalOutput").ap()
    layers(nc, args, out)
    r = _run(nc, [arrays], core_ids=[0])
    return r.results[0]["out_x"]
```

```python
from contextlib import ExitStack

import numpy as np

import concourse.bass as bass
from concourse import mybir
from concourse.alu_op_type import AluOpType as ALU

ACT = mybir.ActivationFunctionType
AX_X = mybir.AxisListType.X
F32 = mybir.dt.float32
F32R = mybir.dt.float32r
BF16 = mybir.dt.bfloat16
I32 = mybir.dt.int32

P = 128
B, T, D = 4, 512, 256
TT, KD = T // P, D // P
NT = B * TT
INTER = 1024
H, DH = 16, 128
HD = H * DH
H1, DH1 = 16, 16
WINDOW, ROPE, ROPE_BASE = 64, 8, 10000.0
E, TOP_K = 7, 2
CAPACITY = B * T // E
DIGITS, DIGIT = 10, 3
WAYS = 2 ** DIGIT - 1
UNROLL = 5
LN_EPS = 1e-5
DMA_INC = 16
CHUNK = 256
NCHUNK = HD // CHUNK

S_BANK = {0: 0, 2: 0, 1: 1, 3: 2}
S_COL = {0: 0, 2: P, 1: 0, 3: 0}
P_COL = {0: 0, 2: P, 1: 4 * P, 3: 6 * P}
SOFTMAX_ORDER = (0, 2, 1, 3)
T_FILLS = ((0,), (1, 3), (2,))
T_WIDTHS = (512, 512, 256)
PT_COL = {0: 0, 1: 4 * P, 3: 7 * P, 2: 8 * P}
PT_ALL = 10 * P


def shape_constants():
    ident = np.eye(P, dtype=np.float32)
    causal = np.where(np.arange(P)[None, :] > np.arange(P)[:, None], -1e30, 0.0).astype(np.float32)
    signs = [[(-1.0) ** bin(i & j).count("1") for j in range(P)] for i in range(P)]
    freq = np.exp(-np.log(np.float32(ROPE_BASE)) * (np.arange(0, ROPE, 2, dtype=np.float32) / ROPE))
    theta = np.arange(T, dtype=np.float32)[:, None] * freq[None, :].astype(np.float32)
    cos, sin = np.cos(theta), np.sin(theta)
    tiled = [np.concatenate(x, 1).reshape(TT, P, ROPE).transpose(1, 0, 2) for x in ((cos, cos), (-sin, sin))]
    query, key = np.arange(P)[:, None] % WINDOW, np.arange(P)[None, :]
    seen = (key <= WINDOW + query) & (key > query)
    window = np.stack([np.where(seen & (key >= WINDOW), 0.0, -1e30), np.where(seen, 0.0, -1e30)], 1)
    below = np.tril(np.ones((E, E)), -1)
    expert = np.arange(P) // NT
    same = (expert[:, None] == expert[None, :]) & (expert[:, None] < E)
    units = 1 << (DIGIT * np.arange(DIGITS - 1, -1, -1))
    before = same & (np.arange(P)[:, None] < np.arange(P)[None, :])
    return {"c_ident": ident, "c_causal": causal, "c_hadamard": np.array(signs, np.float32),
            "c_cos": tiled[0].astype(np.float32), "c_sin": tiled[1].astype(np.float32),
            "c_window": window.astype(np.float32), "c_below": np.tile(below, (P, 1, 1)).astype(np.float32),
            "c_same": same[:, :E * NT].astype(np.float32), "c_before": before[:, :E * NT].astype(np.float32),
            "c_units": np.tile(units.astype(np.int32), (P, 1)),
            "c_steps": np.tile((units[:, None] * np.arange(1, WAYS + 1)).astype(np.int32), (P, 1, 1))}


def rounded(ap):
    return ap.bitcast(F32)


class Ring:

    def __init__(self, names, banks, before=(), last=None, rounds=None):
        assert len(names) % banks == 0
        self.banks, self.fills, self.rounds = banks, len(names), rounds
        self.start = len(before)
        self.before = {name: n for n, name in enumerate(before)}
        self.names = {name: n for n, name in enumerate(names)}
        self.last = {name: n for n, name in enumerate(last)} if last else self.names

    def bank(self, b, name):
        if isinstance(b, int) and b < 0:
            return self.before[name] % self.banks
        return (self.start + self.table(b)[name]) % self.banks

    def table(self, b):
        return self.last if isinstance(b, int) and b + 1 == self.rounds else self.names

    def order(self, b, name):
        if isinstance(b, int) and b < 0:
            return self.before[name]
        return b * self.fills + (self.start + self.table(b)[name])

    def earlier(self, b, name):
        if isinstance(b, int) and b < 0:
            return self.before[name] // self.banks
        return b * (self.fills // self.banks) + (self.start + self.table(b)[name]) // self.banks


class Banks:

    def __init__(self, ctx, nc, label, names, psum, **more):
        if isinstance(psum, int):
            psum = [ctx.enter_context(nc.psum_tensor(f"{label}{n}", [P, 512], F32)) for n in range(psum)]
        self.psum, count = psum, len(psum)
        self.ring = Ring(names, count, **more)
        self.filled = ctx.enter_context(nc.semaphore(f"{label}_filled"))
        self.freed = [ctx.enter_context(nc.semaphore(f"{label}_freed{n}")) for n in range(count)]

    def bank(self, b, name):
        return self.psum[self.ring.bank(b, name)]

    def wait_filled(self, eng, b, name):
        eng.wait_ge(self.filled, self.ring.order(b, name) + 1)

    def wait_freed(self, eng, b, name):
        eng.wait_ge(self.freed[self.ring.bank(b, name)], self.ring.earlier(b, name) + 1)

    def wait_kept(self, eng, b, name):
        eng.wait_ge(self.freed[self.ring.bank(b, name)], self.ring.earlier(b, name) + 2)

    def all_free(self, pe):
        for freed in self.freed:
            pe.sem_inc(freed, 1)

    def filled_by(self, ins):
        ins.then_inc(self.filled, 1)

    def freed_by(self, ins, b, name):
        ins.then_inc(self.freed[self.ring.bank(b, name)], 1)


def three_passes(pe, out, lhs, rhs, start, stop, **kw):
    (lh, ll), (rh, rl) = lhs, rhs
    pe.matmul(out, lh, rh, start=start, stop=False, **kw)
    pe.matmul(out, lh, rl, start=False, stop=False, **kw)
    return pe.matmul(out, ll, rh, start=False, stop=stop, **kw)


class Norm:

    def __init__(self, ctx, nc, c, label, tiles=TT):
        self.nc, self.c = nc, c

        def sb(name, shape):
            return ctx.enter_context(nc.sbuf_tensor(f"{label}_{name}", shape, F32))

        self.st, self.mv = sb("st", [P, tiles, 6]), sb("mv", [P, tiles, 2])
        self.ve, self.rstd = sb("ve", [P, tiles]), sb("rstd", [P, tiles])
        self.var_ready = ctx.enter_context(nc.semaphore(f"{label}_var_ready"))
        self.rstd_ready = ctx.enter_context(nc.semaphore(f"{label}_rstd_ready"))

    def moments(self, dve, source, first=0):
        nc, tiles = self.nc, range(first, first + TT)
        for i in tiles:
            nc.vector.bn_stats(self.st[:, i, :], source(i))
        dve.drain()
        for i in tiles:
            nc.vector.bn_aggr(self.mv[:, i, :], self.st[:, i, :])
        dve.drain()
        nc.vector.tensor_scalar(self.ve[:, first:first + TT], self.mv[:, first:first + TT, 1], LN_EPS, None,
                                ALU.add).then_inc(self.var_ready, 1)

    def wait_inverse(self, dve, nth):
        dve.wait_ge(self.rstd_ready, nth + 1)

    def inverse(self, pool, nth, first=0):
        pool.wait_ge(self.var_ready, nth + 1)
        self.nc.gpsimd.tensor_tensor(self.rstd[:, first:first + TT], self.ve[:, first:first + TT],
                                     self.c["minus_half"][:], ALU.pow).then_inc(self.rstd_ready, 1)

    def apply(self, out, source, i):
        return self.nc.vector.tensor_scalar(out, source, self.mv[:, i, 0:1], self.rstd[:, i:i + 1], ALU.subtract,
                                            ALU.mult)


def nth_before(b):
    return 0 if isinstance(b, int) and b == 0 else b * 2 - 1


def nth_behind(b, follows, batches):
    return b * 2 + 2 if follows else 2 * batches - 1


def view(c, col, *shape):
    part = c["landing"][:, col:col + int(np.prod(shape))]
    if len(shape) == 1:
        return part
    names = " ".join("xyz"[:len(shape)])
    return part.rearrange(f"p ({names}) -> p {names}", **dict(zip("xyz", shape)))


def ffn0_landing(c):
    tiles = INTER // P
    return view(c, 0, tiles, D), view(c, tiles * D, tiles, D), view(c, 2 * tiles * D, KD, 2 * INTER)


def load_ffn0(sp, a, c, queries_out, last):
    dT, _, wT = ffn0_landing(c)
    down_heads = INTER // P * D // T
    sp.wait_ge(queries_out, last * H + down_heads)
    sp.dma_start(dT, a["L0_ffn_W_down"].rearrange("(k p) n -> p k n", p=P)).then_inc(c["ffn0_down_loaded"], DMA_INC)
    sp.wait_ge(queries_out, (last + 1) * H)
    for n, name in enumerate(("L0_ffn_W_up", "L0_ffn_W_gate")):
        sp.dma_start(wT[:, :, n * INTER:(n + 1) * INTER],
                     a[name].rearrange("(k p) n -> p k n", p=P)).then_inc(c["ffn0_ug_loaded"], DMA_INC)


def turn_down_weights(nc, pool, c, stage):
    dT, room, _ = ffn0_landing(c)
    src, dst = ((dT, room), (room, dT))[stage % 2]
    if stage == 0:
        pool.wait_ge(c["ffn0_down_loaded"], DMA_INC)
    else:
        pool.wait_ge(c["down_turned"], 2 * stage)
    x, y = (ap.rearrange("p (g two h) d -> p g two (h d)", two=2, h=2 ** stage) for ap in (src, dst))
    nc.gpsimd.tensor_tensor(y[:, :, 0], x[:, :, 0], x[:, :, 1], ALU.add).then_inc(c["down_turned"], 1)
    nc.gpsimd.tensor_tensor(y[:, :, 1], x[:, :, 0], x[:, :, 1], ALU.subtract).then_inc(c["down_turned"], 1)


def attention1_landing(c):
    shapes = ((KD, D + 2 * DH1), (KD, D), (D,), (TT, ROPE), (TT, ROPE), (2, P))
    cols = np.cumsum([0] + [int(np.prod(x)) for x in shapes])
    return [view(c, int(col), *shape) for col, shape in zip(cols, shapes)]


def load_attention1(sp, a, c):
    w_raw, wo, bo, rot_c, rot_s, mask_raw = attention1_landing(c)
    qkv = ((0, D, "L1_attn_Wq"), (D, DH1, "L1_attn_Wk"), (D + DH1, DH1, "L1_attn_Wv"))
    moves = [(w_raw[:, :, col:col + w], a[name].rearrange("(k p) n -> p k n", p=P)) for col, w, name in qkv]
    moves += [(wo, a["L1_attn_Wo"].rearrange("(k p) n -> p k n", p=P)), (bo, a["L1_attn_bo"].broadcast_to([P, D])),
              (rot_c, a["c_cos"]), (rot_s, a["c_sin"]), (mask_raw, a["c_window"])]
    for dst, src in moves:
        sp.dma_start(dst, src).then_inc(c["attention1_loaded"], DMA_INC)


def experts_landing(c):
    return view(c, T * H // 4, KD, E + 1, 2 * P), view(c, T * H // 4 + KD * (E + 1) * 2 * P, E + 1, D)


def load_experts(sp, a, c):
    for dst, name in zip(experts_landing(c), ("L1_ffn_w1", "L1_ffn_w2")):
        sp.dma_start(dst, a[name]).then_inc(c["experts_loaded"], DMA_INC)


def batches(eng, body):
    with eng.Fori(0, B - 1) as b:
        body(b, True)
    body(B - 1, False)


def every_batch(eng, body):
    body(-1, True)
    batches(eng, body)


def attention0(nc, a, c, x_tok):
    HG = 2

    def v_fills(h):
        if h == 0:
            return [(0, 0), (0, 1)]
        return [((h + 1) // HG, (h + 1) % HG)] * (h + 1 < H)

    prepare = [f"ln{k}" for k in range(KD)] + [f"q{n}" for n in range(H)] + ["k0"]
    fills, last = [], []
    for names, follows in ((fills, True), (last, False)):
        for h in range(H):
            tail = follows and h + 1 == H
            names += [f"ln{k}" for k in range(KD)] * tail
            names += [f"k{h + 1}"] * (h + 1 < H) + [f"o{h - 1}"] * (h > 0)
            names += [f"v{g}_{n}" for g, n in v_fills(h)]
            names += ["q0", "q1"] * tail + [f"t{h}_{n}" for n in range(3)] + ["q2", "q3"] * tail
        names += [f"o{H - 1}"]
        names += ([f"q{n}" for n in range(4, H)] + ["k0"]) * follows
    RAW, SLOTS = 2, 3
    HALF = HD // 2
    TURNS = range(H // 2, H // 2 + 3)

    with ExitStack() as ctx:
        def sb(name, shape, dt=F32):
            return ctx.enter_context(nc.sbuf_tensor(name, shape, dt))

        def sem(name):
            return ctx.enter_context(nc.semaphore(name))

        wq_raw = sb("wq_raw", [P, RAW, KD, CHUNK])
        wq_s = [sb(f"wq_{s}", [P, SLOTS, KD, CHUNK], F32R) for s in ("hi", "lo")]
        wk_s = [sb(f"wk_{s}", [P, KD, HD], F32R) for s in ("hi", "lo")]
        wv_s = [sb(f"wv_{s}", [P, KD, HD], F32R) for s in ("hi", "lo")]
        wo = sb("wo", [P, H, D])
        xT = [sb(f"xT_{s}", [P, KD, T], F32R) for s in ("hi", "lo")]
        qT = view(c, 0, T, H)
        qs = [sb(f"qs_{s}", [P, T], F32R) for s in ("hi", "lo")]
        kT = [sb(f"kT_{s}", [P, T], F32R) for s in ("hi", "lo")]
        v = [sb(f"v_{s}", [P, 2, TT, HG * DH], F32R) for s in ("hi", "lo")]
        p = sb("p", [P, PT_ALL])
        pT = [sb(f"pT_{s}", [P, PT_ALL], F32R) for s in ("hi", "lo")]
        oT = sb("oT", [P, T])
        xn = sb("xn", [P, TT, D])
        y = sb("y", [P, TT, D])
        bq, bk, bv = (sb(n, [P, H]) for n in ("bq", "bk", "bv"))
        bqs = sb("bqs", [P, H])
        bo = sb("bo", [P, D])
        negm = sb("negm", [P, TT])
        rsum = sb("rsum", [P, TT])
        rinv = sb("rinv", [P, TT])
        banks = Banks(ctx, nc, "ring", fills, 3, before=prepare, last=last, rounds=B)
        s_ps = [ctx.enter_context(nc.psum_tensor(f"scores{n}", [P, 512], F32)) for n in range(3)]
        y_ps = [ctx.enter_context(nc.psum_tensor(f"y_ps{n}", [P, 512], F32)) for n in range(2)]
        norm = Norm(ctx, nc, c, "a")

        wo_flat, y_flat = wo[:].rearrange("p h d -> p (h d)"), y[:].rearrange("p t d -> p (t d)")
        landing = [wo_flat[:, n * HALF:(n + 1) * HALF] for n in range(4)] + [y_flat, p[:, 0:HALF]]
        pieces = [(w, k, half) for w in range(2) for k in range(KD) for half in range(2)]
        wq_loaded = [sem(f"wq_loaded{n}") for n in range(RAW)]
        wkv_loaded = [sem(f"wkv_loaded{n}") for n in range(len(pieces))]
        wq_hi, wq_lo = sem("wq_hi_ready"), sem("wq_lo_ready")
        wkv_hi, wkv_lo = sem("wkv_hi_ready"), sem("wkv_lo_ready")
        x_loaded, rows_loaded, wo_loaded = c["x_loaded"], sem("rows_loaded"), sem("wo_loaded")
        bqs_ready = sem("bqs_ready")
        xn_ready, xT_hi = sem("xn_ready"), sem("xT_hi_ready")
        qs_hi, qs_lo = sem("qs_hi_ready"), sem("qs_lo_ready")
        k_hi, v_hi = sem("k_hi_ready"), sem("v_hi_ready")
        scored = [sem(f"scored{n}") for n in range(3)]
        max_ready, exp_ready, rinv_ready, p_ready = (sem(s) for s in ("max_ready", "exp_ready", "rinv_ready",
                                                                      "p_ready"))
        pT_hi = sem("pT_hi_ready")
        y_done, y_freed, y_normed = (sem(s) for s in ("y_done", "y_freed", "y_normed"))

        def q_of(h):
            return qT[:, h * (T // H):(h + 1) * (T // H), :].rearrange("p t c -> p (t c)")

        block = ctx.enter_context(nc.Block())

        @block.sync
        def _(sp):
            def load_chunks(b):
                for n in range(NCHUNK):
                    if not (isinstance(b, int) and n < RAW):
                        sp.wait_ge(wq_lo, (b + 1) * NCHUNK + n - RAW + 1)
                    sp.dma_start(wq_raw[:, n % RAW], a["L0_attn_Wq"][:, n * CHUNK:(n + 1) * CHUNK].rearrange(
                        "(k p) n -> p k n", p=P)).then_inc(wq_loaded[n % RAW], DMA_INC)
                    if isinstance(b, int) and n >= 1:
                        load_pieces(*{1: (0, 2), 2: (2, 4), 3: (4, 6), 4: (6, 7), 5: (7, 8)}.get(n, (8, 8)))

            def load_pieces(lo, hi):
                for m in range(lo, hi):
                    w, k, half = pieces[m]
                    if m >= len(landing):
                        sp.wait_ge(wkv_lo, m - len(landing) + 1)
                    sp.dma_start(landing[m % len(landing)],
                                 a[("L0_attn_Wk", "L0_attn_Wv")[w]][k * P:(k + 1) * P,
                                                                    half * HALF:(half + 1) * HALF]).then_inc(
                        wkv_loaded[m], DMA_INC)

            for name, dst in (("bq", bq), ("bk", bk), ("bv", bv)):
                sp.dma_start(dst[:], a[f"L0_attn_{name}"]).then_inc(rows_loaded, DMA_INC)
            sp.dma_start(bo[:], a["L0_attn_bo"].broadcast_to([P, D])).then_inc(rows_loaded, DMA_INC)
            load_chunks(-1)
            for b in range(1, B):
                sp.dma_start(x_tok[:, b * TT:(b + 1) * TT, :],
                             a["L0_attn_x"][b].rearrange("(t p) d -> p t d", p=P)).then_inc(x_loaded, DMA_INC)
            sp.wait_ge(wkv_lo, len(pieces))
            sp.dma_start(wo[:], a["L0_attn_Wo"].rearrange("(h d) n -> d h n", d=DH)).then_inc(wo_loaded, DMA_INC)
            with sp.Fori(0, B - 1) as b:
                load_chunks(b)
            load_ffn0(sp, a, c, qs_lo, B - 1)

        @block.gpsimd
        def _(pool):
            def lo_of_chunk(b, n):
                pool.wait_ge(wq_hi, (b + 1) * NCHUNK + n + 1)
                nc.gpsimd.tensor_tensor(wq_s[1][:, n % SLOTS], wq_raw[:, n % RAW], rounded(wq_s[0][:, n % SLOTS]),
                                        ALU.subtract).then_inc(wq_lo, 1)

            def lo_of_q(nb, h):
                pool.wait_ge(qs_hi, nb * H + h + 1)
                nc.gpsimd.tensor_tensor(qs[1][:], q_of(h), rounded(qs[0][:]), ALU.subtract).then_inc(qs_lo, 1)

            def body(b, follows):
                first = isinstance(b, int) and b < 0
                for h in range(H if not first else 0):
                    if h + 1 < H:
                        lo_of_q(b, h + 1)
                    if not follows and h in TURNS:
                        if h == TURNS[0]:
                            pool.wait_ge(qs_lo, b * H + h)
                        turn_down_weights(nc, pool, c, h - TURNS[0])
                    if follows and h == H - 4:
                        norm.inverse(pool, nth_before(b + 1))
                    if follows and H - 5 <= h < H - 5 + SLOTS:
                        lo_of_chunk(b, h - (H - 5))
                if first:
                    norm.inverse(pool, 0)
                    for n in range(SLOTS):
                        lo_of_chunk(b, n)
                if follows:
                    lo_of_chunk(b, 3)
                    lo_of_chunk(b, 4)
                if not first:
                    norm.inverse(pool, nth_behind(b, follows, B))
                if follows:
                    for n in range(5, NCHUNK):
                        lo_of_chunk(b, n)
                    lo_of_q(b + 1, 0)

            every_batch(pool, body)

        @block.scalar
        def _(act):
            def hi_of_x(b, k):
                banks.wait_filled(act, b, f"ln{k}")
                nc.scalar.activation(xT[0][:, k, :], banks.bank(b, f"ln{k}")[:], ACT.Copy).then_inc(xT_hi, 1)

            def hi_of_chunk(b, n):
                act.wait_ge(wq_loaded[n % RAW], (b + 1) * (NCHUNK // RAW * DMA_INC) + (n // RAW + 1) * DMA_INC)
                nc.scalar.activation(wq_s[0][:, n % SLOTS], wq_raw[:, n % RAW], ACT.Copy).then_inc(wq_hi, 1)

            def store_q(b, n):
                banks.wait_filled(act, b, f"q{n}")
                banks.freed_by(nc.scalar.activation(qT[:, :, n], banks.bank(b, f"q{n}")[:], ACT.Identity,
                                                    bias=bqs[:, n:n + 1], scale=float(DH) ** -0.5), b, f"q{n}")

            def hi_of_q(b, h):
                if h == 0:
                    for n in range(H - 3, H):
                        banks.wait_kept(act, b, f"q{n}")
                else:
                    act.wait_ge(scored[2], b * H + h)
                nc.scalar.activation(qs[0][:], q_of(h), ACT.Copy).then_inc(qs_hi, 1)

            def hi_of_k(b, h):
                banks.wait_filled(act, b, f"k{h}")
                nc.scalar.activation(kT[0][:], banks.bank(b, f"k{h}")[:], ACT.Identity,
                                     bias=bk[:, h:h + 1]).then_inc(k_hi, 1)

            def hi_of_v(b, g, n):
                banks.wait_filled(act, b, f"v{g}_{n}")
                nc.scalar.activation(v[0][:, g % 2, 2 * n:2 * n + 2].rearrange("p t d -> p (t d)"),
                                     banks.bank(b, f"v{g}_{n}")[:], ACT.Copy).then_inc(v_hi, 1)

            def softmax_exp(b, h):
                for n, i in enumerate(SOFTMAX_ORDER):
                    act.wait_ge(max_ready, b * H * TT + h * TT + max(n + 1, 2))
                    w = (i + 1) * P
                    ins = nc.scalar.activation(p[:, P_COL[i]:P_COL[i] + w],
                                               s_ps[S_BANK[i]][:, S_COL[i]:S_COL[i] + w], ACT.Exp,
                                               bias=negm[:, i:i + 1], accum_out=rsum[:, i:i + 1])
                    ins.then_inc(exp_ready, 1)

            def hi_of_pT(b, h):
                for n in range(3):
                    banks.wait_filled(act, b, f"t{h}_{n}")
                    col, w = PT_COL[T_FILLS[n][0]], T_WIDTHS[n]
                    nc.scalar.activation(pT[0][:, col:col + w], banks.bank(b, f"t{h}_{n}")[:, 0:w],
                                         ACT.Copy).then_inc(pT_hi, 1)

            def store_o(b, h):
                banks.wait_filled(act, b, f"o{h}")
                banks.freed_by(nc.scalar.activation(oT[:], banks.bank(b, f"o{h}")[:], ACT.Identity,
                                                    bias=bv[:, h:h + 1]), b, f"o{h}")

            def body(b, follows):
                first = isinstance(b, int) and b < 0
                for h in range(H if not first else 0):
                    tail = follows and h + 1 == H
                    if tail:
                        hi_of_x(b, 0)
                        hi_of_x(b, 1)
                    softmax_exp(b, h)
                    if h + 1 < H:
                        hi_of_q(b, h + 1)
                        hi_of_k(b, h + 1)
                    if h:
                        store_o(b, h - 1)
                    for g, n in v_fills(h):
                        hi_of_v(b, g, n)
                    if tail:
                        store_q(b, 0)
                        store_q(b, 1)
                    hi_of_pT(b, h)
                    if follows and H - 5 <= h < H - 5 + SLOTS:
                        hi_of_chunk(b, h - (H - 5))
                if first:
                    hi_of_chunk(b, 0)
                    hi_of_chunk(b, 1)
                    hi_of_x(b, 0)
                    hi_of_x(b, 1)
                    hi_of_chunk(b, 2)
                    act.wait_ge(bqs_ready, 1)
                    store_q(b, 0)
                    store_q(b, 1)
                if follows:
                    hi_of_chunk(b, 3)
                    store_q(b, 2)
                    store_q(b, 3)
                    hi_of_chunk(b, 4)
                if not first:
                    store_o(b, H - 1)
                if follows:
                    for n in range(4, H):
                        store_q(b, n)
                        if n in (5, 7, 9):
                            hi_of_chunk(b, (n + 5) // 2)
                    hi_of_q(b, 0)
                    hi_of_k(b, 0)

            every_batch(act, body)

        @block.vector
        def _(dve):
            def lo_of(b, name, out, hi, hi_sem, nth, bias=None):
                dve.wait_ge(hi_sem, nth)
                src = banks.bank(b, name)[:, 0:out.shape[-1]]
                if bias is None:
                    ins = nc.vector.tensor_tensor(out, src, rounded(hi), ALU.subtract)
                else:
                    ins = nc.vector.scalar_tensor_tensor(out=out, in0=src, scalar=bias, in1=rounded(hi),
                                                         op0=ALU.add, op1=ALU.subtract)
                banks.freed_by(ins, b, name)

            def softmax_max(b, h):
                for i in SOFTMAX_ORDER:
                    if i != 2:
                        dve.wait_ge(scored[S_BANK[i]], b * H + h + 1)
                    nc.vector.tensor_reduce(negm[:, i:i + 1], s_ps[S_BANK[i]][:, S_COL[i]:S_COL[i] + (i + 1) * P],
                                            AX_X, ALU.max, negate=True).then_inc(max_ready, 1)

            def softmax_norm(b, h):
                dve.wait_ge(exp_ready, b * H * TT + (h + 1) * TT)
                nc.vector.reciprocal(rinv[:], rsum[:]).then_inc(rinv_ready, 1)
                dve.wait_ge(rinv_ready, b * H + h + 1)
                for i in SOFTMAX_ORDER:
                    cols = p[:, P_COL[i]:P_COL[i] + (i + 1) * P]
                    nc.vector.tensor_scalar(cols, cols, rinv[:, i:i + 1], None, ALU.mult).then_inc(p_ready, 1)

            def lo_of_x(b, k):
                lo_of(b, f"ln{k}", xT[1][:, k, :], xT[0][:, k, :], xT_hi, (b + 1) * KD + k + 1)

            def lo_of_k(b, h, nb):
                lo_of(b, f"k{h}", kT[1][:], kT[0][:], k_hi, nb * H + h + 1, bias=bk[:, h:h + 1])

            def lo_of_v(b, g, n):
                out, hi = (x[:, g % 2, 2 * n:2 * n + 2].rearrange("p t d -> p (t d)") for x in (v[1], v[0]))
                lo_of(b, f"v{g}_{n}", out, hi, v_hi, b * H + HG * g + n + 1)

            def norm_before(b):
                nb = b + 1
                norm.wait_inverse(dve, nth_before(nb))
                for i in range(TT):
                    norm.apply(xn[:, i, :], x_tok[:, bass.ds(nb * TT + i, 1), :], i).then_inc(xn_ready, 1)

            def norm_behind(b, follows):
                dve.wait_ge(y_done, b + 1)
                for n in range(2):
                    ins = nc.vector.tensor_tensor(y[:, 2 * n:2 * n + 2, :],
                                                  y_ps[n][:].rearrange("p (t d) -> p t d", d=D),
                                                  bo[:].unsqueeze(1).broadcast_to([P, 2, D]), ALU.add)
                ins.then_inc(y_freed, 1)
                dve.wait_ge(y_freed, b + 1)
                norm.moments(dve, lambda i: y[:, i, :])
                norm.wait_inverse(dve, nth_behind(b, follows, B))
                for i in range(TT):
                    ins = norm.apply(y[:, i, :], y[:, i, :], i)
                ins.then_inc(y_normed, 1)
                dve.wait_ge(y_normed, b + 1)
                x_b = x_tok[:, bass.ds(b * TT, TT), :]
                nc.vector.tensor_tensor(x_b, x_b, y[:], ALU.add)

            def body(b, follows):
                first = isinstance(b, int) and b < 0
                for h in range(H if not first else 0):
                    softmax_max(b, h)
                    if follows and h + 1 == H:
                        lo_of_x(b, 0)
                        lo_of_x(b, 1)
                    if h + 1 < H:
                        lo_of_k(b, h + 1, b)
                    softmax_norm(b, h)
                    for g, n in v_fills(h):
                        lo_of_v(b, g, n)
                    for n in range(3):
                        col, w = PT_COL[T_FILLS[n][0]], T_WIDTHS[n]
                        lo_of(b, f"t{h}_{n}", pT[1][:, col:col + w], pT[0][:, col:col + w], pT_hi,
                              b * 3 * H + h * 3 + n + 1)
                    if follows and h == H - 4:
                        norm.moments(dve, lambda i: x_tok[:, bass.ds((b + 1) * TT + i, 1), :])
                    if follows and h == H - 3:
                        norm_before(b)
                if not first:
                    norm_behind(b, follows)
                if first:
                    dve.wait_ge(x_loaded, DMA_INC)
                    norm.moments(dve, lambda i: x_tok[:, i, :])
                    norm_before(b)
                    dve.wait_ge(rows_loaded, 4 * DMA_INC)
                    nc.vector.tensor_scalar(bqs[:], bq[:], float(DH) ** -0.5, None, ALU.mult).then_inc(bqs_ready, 1)
                    lo_of_x(b, 0)
                    lo_of_x(b, 1)
                    for m, (w, k, half) in enumerate(pieces):
                        hi, lo = (x[:, k, half * HALF:(half + 1) * HALF] for x in (wk_s, wv_s)[w])
                        dve.wait_ge(wkv_loaded[m], DMA_INC)
                        nc.vector.tensor_copy(hi, landing[m % len(landing)]).then_inc(wkv_hi, 1)
                        dve.wait_ge(wkv_hi, m + 1)
                        nc.vector.tensor_tensor(lo, landing[m % len(landing)], rounded(hi), ALU.subtract).then_inc(
                            wkv_lo, 1)
                    dve.wait_ge(x_loaded, B * DMA_INC)
                if follows:
                    lo_of_k(b, 0, b + 1)

            every_batch(dve, body)

        @block.tensor
        def _(pe):
            def project(out, k_lhs, k_rhs):
                for k in range(KD):
                    ins = three_passes(pe, out, k_lhs(k), k_rhs(k), start=(k == 0), stop=(k == KD - 1))
                return ins

            def fill_ln(b, k):
                banks.wait_freed(pe, b, f"ln{k}")
                for i in range(TT):
                    if k == 0:
                        pe.wait_ge(xn_ready, (b + 1) * TT + i + 1)
                    ins = pe.transpose(banks.bank(b, f"ln{k}")[:, i * P:(i + 1) * P],
                                       xn[:, i, k * P:(k + 1) * P], c["ident"][:])
                banks.filled_by(ins)

            def fill_q(b, n):
                if n == 0:
                    for k in range(KD):
                        banks.wait_kept(pe, b, f"ln{k}")
                if n % 2 == 0:
                    pe.wait_ge(wq_lo, (b + 1) * NCHUNK + n // 2 + 1)
                banks.wait_freed(pe, b, f"q{n}")
                col = n % 2 * DH
                banks.filled_by(project(banks.bank(b, f"q{n}")[:],
                                        lambda k: [w[:, n // 2 % SLOTS, k, col:col + DH] for w in wq_s],
                                        lambda k: [x[:, k, :] for x in xT]))

            def fill_k(b, h):
                banks.wait_freed(pe, b, f"k{h}")
                banks.filled_by(project(banks.bank(b, f"k{h}")[:],
                                        lambda k: [w[:, k, h * DH:(h + 1) * DH] for w in wk_s],
                                        lambda k: [x[:, k, :] for x in xT]))

            def fill_v(b, g, n):
                banks.wait_freed(pe, b, f"v{g}_{n}")
                w = HG * DH
                for j in range(2):
                    t = 2 * n + j
                    ins = project(banks.bank(b, f"v{g}_{n}")[:, j * w:(j + 1) * w],
                                  lambda k: [x[:, k, t * P:(t + 1) * P] for x in xT],
                                  lambda k: [x[:, k, g * w:(g + 1) * w] for x in wv_s])
                banks.filled_by(ins)

            def scores(b, h):
                pe.wait_ge(qs_lo, b * H + h + 1)
                if h:
                    banks.wait_kept(pe, b, f"k{h}")
                for i in SOFTMAX_ORDER:
                    w = (i + 1) * P
                    out = s_ps[S_BANK[i]][:, S_COL[i]:S_COL[i] + w]
                    three_passes(pe, out, [q[:, i * P:(i + 1) * P] for q in qs], [k[:, 0:w] for k in kT],
                                 start=(i != 2), stop=False)
                    if i == 2:
                        ins = pe.matmul(s_ps[0][:].rearrange("p (t k) -> p t k", k=P)[:, 0:TT:TT - 1, :],
                                        c["ident_bf"][:], c["causal_bf"][:].unsqueeze(1).broadcast_to([P, 2, P]),
                                        start=False, stop=True)
                    elif i:
                        ins = pe.matmul(out[:, i * P:w], c["ident_bf"][:], c["causal_bf"][:], start=False, stop=True)
                    if i:
                        ins.then_inc(scored[S_BANK[i]], 1)

            def transpose_p(b, h):
                pe.wait_ge(p_ready, b * H * TT + (h + 1) * TT)
                for n, tiles in enumerate(T_FILLS):
                    name = f"t{h}_{n}"
                    banks.wait_freed(pe, b, name)
                    base = PT_COL[tiles[0]]
                    for j in tiles:
                        for i in range(j, TT):
                            col = PT_COL[j] - base + (i - j) * P
                            src = P_COL[i] + j * P
                            ins = pe.transpose(banks.bank(b, name)[:, col:col + P], p[:, src:src + P], c["ident"][:])
                    banks.filled_by(ins)

            def fill_o(b, h):
                name = f"o{h}"
                banks.wait_freed(pe, b, name)
                for n in range(3):
                    banks.wait_kept(pe, b, f"t{h}_{n}")
                for j in range(TT):
                    w = T - j * P
                    ins = three_passes(pe, banks.bank(b, name)[:, j * P:T],
                                       [x[:, h // HG % 2, j, h % HG * DH:(h % HG + 1) * DH] for x in v],
                                       [x[:, PT_COL[j]:PT_COL[j] + w] for x in pT], start=(j == 0),
                                       stop=(j == TT - 1))
                banks.filled_by(ins)

            def out_project(b, h):
                if h == 0:
                    pe.wait_ge(norm.var_ready, b * 2 + 1)
                    pe.wait_ge(wo_loaded, DMA_INC)
                banks.wait_kept(pe, b, f"o{h}")
                for i in range(TT):
                    ins = pe.matmul(y_ps[i // 2][:, i % 2 * D:(i % 2 + 1) * D], oT[:, i * P:(i + 1) * P],
                                    wo[:, h, :], start=(h == 0 and i % 2 == 0), stop=(h == H - 1),
                                    skip_group_check=True)
                if h == H - 1:
                    ins.then_inc(y_done, 1)

            def body(b, follows):
                first = isinstance(b, int) and b < 0
                for h in range(H if not first else 0):
                    tail = follows and h + 1 == H
                    scores(b, h)
                    if tail:
                        fill_ln(b, 0)
                        fill_ln(b, 1)
                    if h + 1 < H:
                        fill_k(b, h + 1)
                    if h:
                        fill_o(b, h - 1)
                    for g, n in v_fills(h):
                        fill_v(b, g, n)
                    if tail:
                        fill_q(b, 0)
                    if h:
                        out_project(b, h - 1)
                    if tail:
                        fill_q(b, 1)
                    transpose_p(b, h)
                if first:
                    fill_ln(b, 0)
                    fill_ln(b, 1)
                    fill_q(b, 0)
                    fill_q(b, 1)
                if follows:
                    fill_q(b, 2)
                    fill_q(b, 3)
                if not first:
                    fill_o(b, H - 1)
                if follows:
                    fill_q(b, 4)
                if not first:
                    out_project(b, H - 1)
                if follows:
                    for n in range(5, H):
                        fill_q(b, n)
                    if first:
                        pe.wait_ge(wkv_lo, len(pieces))
                    fill_k(b, 0)
                    banks.wait_kept(pe, b, "k0")

            banks.all_free(pe)
            every_batch(pe, body)


def ffn0(nc, a, c, x_tok):
    NF = INTER // P
    LAG = 2
    ahead = [f"ln+{k}" for k in range(KD)] + ["up+0", "gate+0", "up+1", "gate+1"]
    fills, last = [], []
    for names, follows in ((fills, True), (last, False)):
        for n in range(LAG, NF):
            names += [f"up{n}", f"gate{n}"] + ahead[:KD] * (follows and n == NF - 2)
        names += ahead[KD:] * follows

    with ExitStack() as ctx:
        def sb(name, shape, dt=F32):
            return ctx.enter_context(nc.sbuf_tensor(name, shape, dt))

        def sem(name):
            return ctx.enter_context(nc.semaphore(name))

        eff = [sb(f"f_eff_{s}", [P, KD, 2 * INTER], F32R) for s in ("hi", "lo")]
        down = [sb(f"f_down_{s}", [P, NF, D], F32R) for s in ("hi", "lo")]
        xn = c["xn"]
        norm = Norm(ctx, nc, c, "f")
        xn_ready = sem("f_xn_ready")
        with ExitStack() as inner:
            def sbi(name, shape, dt=F32):
                return inner.enter_context(nc.sbuf_tensor(name, shape, dt))

            def semi(name):
                return inner.enter_context(nc.semaphore(name))

            hada = sbi("hada", [P, P])
            hada_r = [sbi(f"hada_{s}", [P, P], F32R) for s in ("pos", "neg")]
            _, turned, wT = ffn0_landing(c)
            wT_s = [sbi(f"f_wT_{s}", [P, KD, 2 * INTER], F32R) for s in ("hi", "lo")]
            dT_s = [sbi(f"f_dT_{s}", [P, NF, D], F32R) for s in ("hi", "lo")]
            d_eff = sbi("f_d_eff", [P, NF, D])
            su_ug, su_dp = sbi("su_ug", [P, KD]), sbi("su_dp", [P, NF])
            su_ug_n, su_dp_n = sbi("su_ug_n", [P, KD]), sbi("su_dp_n", [P, NF])
            sc_dp = sbi("sc_dp", [P, D])
            PIECE, PIECES = 512, 2 * INTER // 512
            piece = [slice(n * PIECE, (n + 1) * PIECE) for n in range(PIECES)]
            ug_fills = [f"w{k}_{n}" for n in range(PIECES) for k in range(KD)]
            banks = Banks(inner, nc, "fw", ug_fills[:KD] + [f"d{n}" for n in range(NF)] + ug_fills[KD:], 8)
            s_loaded = semi("s_loaded")
            w_loaded, down_turned = c["ffn0_ug_loaded"], c["down_turned"]
            hada_ready, signs_ready = semi("hada_ready"), semi("signs_ready")
            w_hi, w_lo, d_hi, d_lo = semi("w_hi"), semi("w_lo"), semi("d_hi"), semi("d_lo")
            eff_hi, down_hi = semi("eff_hi"), semi("down_hi")
            block = inner.enter_context(nc.Block())

            @block.sync
            def _(sp):
                sp.dma_start(hada[:], a["c_hadamard"]).then_inc(s_loaded, DMA_INC)
                sp.dma_start(su_ug[:], a["L0_ffn_SU_ug"]).then_inc(s_loaded, DMA_INC)
                sp.dma_start(su_dp[:], a["L0_ffn_SU_dp"]).then_inc(s_loaded, DMA_INC)
                sp.dma_start(sc_dp[:], a["L0_ffn_Wscale_dp"].broadcast_to([P, D])).then_inc(s_loaded, DMA_INC)

            @block.scalar
            def _(act):
                def hi_of_w(n):
                    nc.scalar.activation(wT_s[0][:, :, piece[n]], wT[:, :, piece[n]], ACT.Copy).then_inc(w_hi, 1)

                def hi_of_eff(n):
                    for k in range(KD):
                        name = f"w{k}_{n}"
                        banks.wait_filled(act, 0, name)
                        nc.scalar.activation(eff[0][:, k, piece[n]], banks.bank(0, name)[:], ACT.Copy,
                                             scale=su_ug_n[:, k:k + 1]).then_inc(eff_hi, 1)

                act.wait_ge(w_loaded, 2 * DMA_INC)
                hi_of_w(0)
                act.wait_ge(down_turned, 6)
                nc.scalar.activation(dT_s[0][:], turned, ACT.Copy).then_inc(d_hi, 1)
                act.wait_ge(s_loaded, 4 * DMA_INC)
                nc.scalar.activation(hada_r[0][:], hada[:], ACT.Copy).then_inc(hada_ready, 1)
                nc.scalar.activation(hada_r[1][:], hada[:], ACT.Copy, scale=-1.0).then_inc(hada_ready, 1)
                for n in range(1, PIECES):
                    hi_of_w(n)
                act.wait_ge(signs_ready, 2)
                hi_of_eff(0)
                for n in range(NF):
                    banks.wait_kept(act, 0, f"d{n}")
                    nc.scalar.activation(down[0][:, n], d_eff[:, n], ACT.Copy).then_inc(down_hi, 1)
                for n in range(1, PIECES):
                    hi_of_eff(n)

            @block.gpsimd
            def _(pool):
                pool.wait_ge(d_hi, 1)
                nc.gpsimd.tensor_tensor(dT_s[1][:], turned, rounded(dT_s[0][:]), ALU.subtract).then_inc(d_lo, 1)
                norm.inverse(pool, 0)
                for n in range(NF):
                    pool.wait_ge(down_hi, n + 1)
                    nc.gpsimd.tensor_tensor(down[1][:, n], d_eff[:, n], rounded(down[0][:, n]), ALU.subtract)

            @block.vector
            def _(dve):
                def lo_of_w(n):
                    dve.wait_ge(w_hi, n + 1)
                    nc.vector.tensor_tensor(wT_s[1][:, :, piece[n]], wT[:, :, piece[n]],
                                            rounded(wT_s[0][:, :, piece[n]]), ALU.subtract).then_inc(w_lo, 1)

                def lo_of_eff(n):
                    for k in range(KD):
                        name = f"w{k}_{n}"
                        dve.wait_ge(eff_hi, n * KD + k + 1)
                        banks.freed_by(nc.vector.scalar_tensor_tensor(
                            out=eff[1][:, k, piece[n]], in0=banks.bank(0, name)[:], scalar=su_ug_n[:, k:k + 1],
                            in1=rounded(eff[0][:, k, piece[n]]), op0=ALU.mult, op1=ALU.subtract), 0, name)

                lo_of_w(0)
                dve.wait_ge(s_loaded, 4 * DMA_INC)
                nc.vector.tensor_scalar(su_ug_n[:], su_ug[:], float(D) ** -0.5, None, ALU.mult).then_inc(
                    signs_ready, 1)
                nc.vector.tensor_scalar(su_dp_n[:], su_dp[:], float(INTER) ** -0.5, None, ALU.mult).then_inc(
                    signs_ready, 1)
                norm.moments(dve, lambda i: x_tok[:, i, :])
                for n in range(1, PIECES):
                    lo_of_w(n)
                dve.wait_ge(signs_ready, 2)
                lo_of_eff(0)
                for n in range(NF):
                    banks.wait_filled(dve, 0, f"d{n}")
                    banks.freed_by(nc.vector.scalar_tensor_tensor(
                        out=d_eff[:, n], in0=banks.bank(0, f"d{n}")[:, 0:D], scalar=su_dp_n[:, n:n + 1], in1=sc_dp[:],
                        op0=ALU.mult, op1=ALU.mult), 0, f"d{n}")
                norm.wait_inverse(dve, 0)
                for i in range(TT):
                    norm.apply(xn[:, i, :], x_tok[:, i, :], i).then_inc(xn_ready, 1)
                for n in range(1, PIECES):
                    lo_of_eff(n)

            @block.tensor
            def _(pe):
                def transformed(name, out, sources, row, tiles):
                    banks.wait_freed(pe, 0, name)
                    for j in range(tiles):
                        sign = hada_r[bin(row & j).count("1") % 2]
                        for n, half in enumerate(sources):
                            ins = pe.matmul(out, sign[:], half(j), start=(j == 0 and n == 0),
                                            stop=(j == tiles - 1 and n == 1))
                    banks.filled_by(ins)

                def up_and_gate(n):
                    pe.wait_ge(w_lo, n + 1)
                    for k in range(KD):
                        name = f"w{k}_{n}"
                        transformed(name, banks.bank(0, name)[:], [lambda j, w=w: w[:, j, piece[n]] for w in wT_s],
                                    k, KD)

                banks.all_free(pe)
                pe.wait_ge(hada_ready, 2)
                up_and_gate(0)
                pe.wait_ge(d_lo, 1)
                for n in range(NF):
                    name = f"d{n}"
                    transformed(name, banks.bank(0, name)[:, 0:D], [lambda j, w=w: w[:, n, :] for w in dT_s], 0, 1)
                for n in range(1, PIECES):
                    up_and_gate(n)

        xT = [sb(f"f_xT_{s}", [P, KD, B * T], F32R) for s in ("hi", "lo")]
        y = sb("f_y", [P, TT, D])
        gate = sb("f_gate", [P, 2, T])
        h = sb("f_h", [P, 2, T])
        h_s = [sb(f"f_h_{s}", [P, 2 * LAG, T], F32R) for s in ("hi", "lo")]
        su, sg = sb("f_scale_up", [P, NF]), sb("f_scale_gate", [P, NF])
        banks = Banks(ctx, nc, "f", fills, 6, before=ahead, last=last, rounds=B)
        y_ps = [ctx.enter_context(nc.psum_tensor(f"f_y_ps{n}", [P, 512], F32)) for n in range(2)]
        scales = sem("f_scales_loaded")
        xT_hi = sem("f_xT_hi_ready")
        h_hi, h_lo = sem("f_h_hi_ready"), sem("f_h_lo_ready")
        y_done, y_freed, y_normed = sem("f_y_done"), sem("f_y_freed"), sem("f_y_normed")

        def tiles(b, follows):
            own = [] if isinstance(b, int) and b < 0 else [(0, n) for n in range(LAG, NF)]
            return own + [(1, n) for n in range(LAG)] * follows

        def name_of(kind, tile):
            return f"{kind}{'+' * tile[0]}{tile[1]}"

        block = ctx.enter_context(nc.Block())

        @block.sync
        def _(sp):
            sp.dma_start(su[:], a["L0_ffn_Wscale_up"]).then_inc(scales, DMA_INC)
            sp.dma_start(sg[:], a["L0_ffn_Wscale_gate"]).then_inc(scales, DMA_INC)
            load_attention1(sp, a, c)

        @block.gpsimd
        def _(pool):
            def body(b, follows):
                first = isinstance(b, int) and b < 0
                for f, n in tiles(b, follows):
                    pool.wait_ge(h_hi, (b + f) * NF + n + 1)
                    nc.gpsimd.tensor_tensor(h_s[1][:, n % (2 * LAG)], h[:, n % 2], rounded(h_s[0][:, n % (2 * LAG)]),
                                            ALU.subtract).then_inc(h_lo, 1)
                    if not f and n == 3:
                        norm.inverse(pool, nth_before(b + 1))
                if not first:
                    norm.inverse(pool, b * 2 + 2)

            every_batch(pool, body)

        @block.scalar
        def _(act):
            def hi_of_x(b):
                for k in range(KD):
                    banks.wait_filled(act, b, f"ln+{k}")
                    nc.scalar.activation(xT[0][:, k, bass.ds((b + 1) * T, T)], banks.bank(b, f"ln+{k}")[:],
                                         ACT.Copy).then_inc(xT_hi, 1)

            def body(b, follows):
                first = isinstance(b, int) and b < 0
                if first:
                    hi_of_x(b)
                for f, n in tiles(b, follows):
                    up, gt = name_of("up", (f, n)), name_of("gate", (f, n))
                    banks.wait_filled(act, b, gt)
                    banks.freed_by(nc.scalar.activation(gate[:, n % 2], banks.bank(b, gt)[:], ACT.Silu,
                                                        scale=sg[:, n:n + 1]), b, gt)
                    banks.wait_kept(act, b, up)
                    nc.scalar.activation(h_s[0][:, n % (2 * LAG)], h[:, n % 2], ACT.Copy).then_inc(h_hi, 1)
                    if follows and not f and n == NF - 2:
                        hi_of_x(b)
                if not first:
                    act.wait_ge(y_done, b + 1)
                    for n in range(2):
                        ins = nc.scalar.activation(y[:, 2 * n:2 * n + 2, :].rearrange("p t d -> p (t d)"), y_ps[n][:],
                                                   ACT.Copy)
                    ins.then_inc(y_freed, 1)

            act.wait_ge(scales, 2 * DMA_INC)
            every_batch(act, body)

        @block.vector
        def _(dve):
            def x_behind(b, i):
                return x_tok[:, bass.ds((0 if isinstance(b, int) and b + 1 == B else b + 1) * TT + i, 1), :]

            def norm_before(b):
                norm.wait_inverse(dve, nth_before(b + 1))
                for i in range(TT):
                    norm.apply(xn[:, i, :], x_behind(b, i), i).then_inc(xn_ready, 1)

            def lo_of_x(b):
                cols = bass.ds((b + 1) * T, T)
                for k in range(KD):
                    dve.wait_ge(xT_hi, (b + 1) * KD + k + 1)
                    banks.freed_by(nc.vector.tensor_tensor(xT[1][:, k, cols], banks.bank(b, f"ln+{k}")[:],
                                                           rounded(xT[0][:, k, cols]), ALU.subtract), b, f"ln+{k}")

            def norm_behind(b):
                nth = b * 2 + 2
                dve.wait_ge(y_freed, b + 2)
                norm.moments(dve, lambda i: y[:, i, :])
                norm.wait_inverse(dve, nth)
                for i in range(TT):
                    ins = norm.apply(y[:, i, :], y[:, i, :], i)
                ins.then_inc(y_normed, 1)
                dve.wait_ge(y_normed, b + 1)
                x_b = x_tok[:, bass.ds(b * TT, TT), :]
                nc.vector.tensor_tensor(x_b, x_b, y[:], ALU.add)

            def body(b, follows):
                first = isinstance(b, int) and b < 0
                if first:
                    lo_of_x(b)
                for f, n in tiles(b, follows):
                    up, gt = name_of("up", (f, n)), name_of("gate", (f, n))
                    banks.wait_filled(dve, b, up)
                    banks.wait_kept(dve, b, gt)
                    before = (b + f) * NF + n - 1
                    if not isinstance(b, int) or before >= 1:
                        dve.wait_ge(h_lo, before)
                    ins = nc.vector.scalar_tensor_tensor(out=h[:, n % 2], in0=banks.bank(b, up)[:],
                                                         scalar=su[:, n:n + 1], in1=gate[:, n % 2], op0=ALU.mult,
                                                         op1=ALU.mult)
                    banks.freed_by(ins, b, up)
                    if not f and n == 3:
                        norm.moments(dve, lambda i: x_behind(b, i))
                    if not f and n == 4:
                        norm_before(b)
                    if follows and not f and n == NF - 2:
                        lo_of_x(b)
                if not first:
                    norm_behind(b)

            dve.wait_ge(scales, 2 * DMA_INC)
            every_batch(dve, body)

        @block.tensor
        def _(pe):
            def transpose_x(b):
                for k in range(KD):
                    banks.wait_freed(pe, b, f"ln+{k}")
                    for i in range(TT):
                        if k == 0:
                            pe.wait_ge(xn_ready, (b + 1) * TT + i + 1)
                        ins = pe.transpose(banks.bank(b, f"ln+{k}")[:, i * P:(i + 1) * P],
                                           xn[:, i, k * P:(k + 1) * P], c["ident"][:])
                    banks.filled_by(ins)

            def project_down(nb, n):
                pe.wait_ge(h_lo, nb * NF + n + 1)
                for i in range(TT):
                    ins = three_passes(pe, y_ps[i // 2][:, i % 2 * D:(i % 2 + 1) * D],
                                       [x[:, n % (2 * LAG), i * P:(i + 1) * P] for x in h_s],
                                       [w[:, n, :] for w in down],
                                       start=(n == 0 and i % 2 == 0), stop=(n == NF - 1), skip_group_check=True)
                return ins

            def body(b, follows):
                first = isinstance(b, int) and b < 0
                if first:
                    transpose_x(b)
                for f, n in tiles(b, follows):
                    if f and n == 0:
                        for k in range(KD):
                            banks.wait_kept(pe, b, f"ln+{k}")
                    for kind, col in (("up", n * P), ("gate", INTER + n * P)):
                        name = name_of(kind, (f, n))
                        banks.wait_freed(pe, b, name)
                        for k in range(KD):
                            ins = three_passes(pe, banks.bank(b, name)[:], [w[:, k, col:col + P] for w in eff],
                                               [x[:, k, bass.ds((b + f) * T, T)] for x in xT], start=(k == 0),
                                               stop=(k == KD - 1))
                        banks.filled_by(ins)
                    if follows and not f and n == NF - 2:
                        transpose_x(b)
                    if n == LAG:
                        pe.wait_ge(y_freed, b + 1)
                    if not f:
                        project_down(b, n - LAG)
                    elif not first:
                        ins = project_down(b, NF - LAG + n)
                if not follows:
                    for n in range(NF - LAG, NF):
                        ins = project_down(b, n)
                if not first:
                    ins.then_inc(y_done, 1)

            banks.all_free(pe)
            pe.sem_inc(y_freed, 1)
            every_batch(pe, body)


def attention1(nc, a, c, x_tok):
    PAD = WINDOW
    NS, NB = 4, H1 // 2

    def name_of(kind, tile):
        return f"{kind}{'+' * tile[0]}{tile[1]}"

    def steps(b, follows):
        if isinstance(b, int) and b < 0:
            return [dict(ln=(1, 0)), dict(ln=(1, 1), qk=(1, 0)), dict(ln=(1, 2), qk=(1, 1), s=(1, 0)),
                    dict(ln=(1, 3), qk=(1, 2), s=(1, 1), o=(1, 0))]
        out = []
        for t in range(2, TT + 2):
            tiles = [(0, n) if n < TT else (1, n - TT) for n in (t + 2, t + 1, t, t - 1, t - 2)]
            out.append({kind: tile for kind, tile in zip(("ln", "qk", "s", "o", "y"), tiles)
                        if follows or not tile[0]})
        return out

    def fills_of(b, follows):
        names = []
        for step in steps(b, follows):
            for kind, stage in (("qk", ("qk",)), ("p", ("p0_", "p1_", "p2_", "p3_")),
                                ("s", ("s0_", "s1_", "s2_", "s3_")), ("y", ("oT",)), ("o", ("o",)), ("ln", ("ln",)),
                                ("qk", ("ta", "tb", "tk"))):
                tile = step.get("o" if kind == "p" else kind)
                names += [name_of(n, tile) for n in stage] if tile else []
        return names

    with ExitStack() as ctx:
        def sb(name, shape, dt=F32):
            return ctx.enter_context(nc.sbuf_tensor(name, shape, dt))

        def sem(name):
            return ctx.enter_context(nc.semaphore(name))

        QK = D + DH1
        w_raw, wo, bo, rot_c, rot_s, mask_raw = attention1_landing(c)
        w_s = [sb(f"g_w_{s}", [P, KD, QK + DH1], F32R) for s in ("hi", "lo")]
        mask = sb("g_mask", [P, 2, NS, P], BF16)
        xT = [sb(f"g_xT_{s}", [P, KD, PAD + T], F32R) for s in ("hi", "lo")]
        xn, y = c["xn"], sb("g_y", [P, TT, D])
        qk = sb("g_qk", [P, H1 + 1, DH1])
        turned = sb("g_turned", [P, H1 + 1, ROPE])
        q_st = sb("g_q_st", [P, H1, 4, DH1])
        k_st = sb("g_k_st", [P, 2, 4, DH1])
        qT = sb("g_qT", [P, 2, 2, NB, 64], F32R)
        kT = sb("g_kT", [P, PAD + T], F32R)
        vw = sb("g_vw", [P, 2 * TT, DH1 + 1])
        p = sb("g_p", [P, NS, 4 * P])
        pT = sb("g_pT", [P, NS, 4 * P])
        top = sb("g_top", [P, NS, 4])
        o = sb("g_o", [P, H1, DH1])
        oT = sb("g_oT", [P, KD, P])
        rinv = sb("g_rinv", [P, H1])
        banks = Banks(ctx, nc, "g", fills_of(0, True), 6, before=fills_of(-1, True), last=fills_of(B - 1, False),
                      rounds=B)
        y_ps = [ctx.enter_context(nc.psum_tensor(f"g_y_ps{n}", [P, 512], F32)) for n in range(2)]
        norm, norm_y = Norm(ctx, nc, c, "g"), Norm(ctx, nc, c, "gy")
        loaded = c["attention1_loaded"]
        w_ready, w_hi, mask_ready, pads = (sem(f"g_{s}") for s in ("w_ready", "w_hi", "mask_ready", "pads_ready"))
        xn_ready, xT_hi = sem("g_xn_ready"), sem("g_xT_hi_ready")
        rotated, qk_copied, keys_ready = sem("g_rotated"), sem("g_qk_copied"), sem("g_keys_ready")
        st_hi, st_ready = sem("g_st_hi_ready"), sem("g_st_ready")
        top_ready, exp_ready = sem("g_top_ready"), sem("g_exp_ready")
        rinv_ready = sem("g_rinv_ready")
        y_done, y_freed, y_normed, x_updated = (sem(f"g_{s}") for s in (
            "y_done", "y_freed", "y_normed", "x_updated"))
        block = ctx.enter_context(nc.Block())

        @block.sync
        def _(sp):
            load_experts(sp, a, c)

        @block.gpsimd
        def _(pool):
            nc.gpsimd.memset(kT[:, 0:PAD].bitcast(F32), 0.0).then_inc(pads, 1)
            for x in xT:
                nc.gpsimd.memset(x[:, :, 0:PAD].bitcast(F32), 0.0).then_inc(pads, 1)
            nc.gpsimd.memset(vw[:], 1.0).then_inc(pads, 1)

            def body(b, follows):
                if not isinstance(b, int) or b >= 0:
                    norm.inverse(pool, b)
                    norm_y.inverse(pool, b)
                if follows and (not isinstance(b, int) or b >= 0):
                    pool.drain()
                    for i in range(TT):
                        ins = nc.gpsimd.tensor_scalar(y[:, i, :], y[:, i, :], norm_y.mv[:, i, 0:1],
                                                      norm_y.rstd[:, i:i + 1], ALU.subtract, ALU.mult)
                    ins.then_inc(y_normed, 1)
                    pool.wait_ge(y_normed, b + 1)
                    x_b = x_tok[:, bass.ds(b * TT, TT), :]
                    nc.gpsimd.tensor_tensor(x_b, x_b, y[:], ALU.add).then_inc(x_updated, 1)

            every_batch(pool, body)

        @block.scalar
        def _(act):
            act.wait_ge(loaded, 8 * DMA_INC)
            nc.scalar.activation(w_s[0][:], w_raw, ACT.Copy).then_inc(w_hi, 1)
            for v in range(2):
                nc.scalar.activation(mask[:, v], mask_raw[:, v].unsqueeze(1).broadcast_to([P, NS, P]),
                                     ACT.Copy).then_inc(mask_ready, 1)
            act.wait_ge(pads, 4)

            def hi_of_x(b, tile):
                f, t = tile
                banks.wait_filled(act, b, name_of("ln", tile))
                nc.scalar.activation(xT[0][:, :, PAD + t * P:PAD + (t + 1) * P],
                                     banks.bank(b, name_of("ln", tile))[:, 0:D].rearrange("p (k t) -> p k t", k=KD),
                                     ACT.Copy).then_inc(xT_hi, 1)

            def plain_qk(b, tile):
                f, t = tile
                name = name_of("qk", tile)
                banks.wait_filled(act, b, name)
                src = banks.bank(b, name)[:, 0:QK].rearrange("p (h d) -> p h d", d=DH1)
                if not (isinstance(b, int) and (b + f) * TT + t == 0):
                    act.wait_ge(st_ready, (b + f) * TT + t)
                nc.scalar.activation(qk[:, :, ROPE:DH1], src[:, :, ROPE:DH1], ACT.Copy).then_inc(qk_copied, 1)

            def keep_transposed(b, tile):
                t = tile[1]
                for n, kind in enumerate(("ta", "tb")):
                    name = name_of(kind, tile)
                    banks.wait_filled(act, b, name)
                    banks.freed_by(nc.scalar.activation(
                        qT[:, t % 2, :, 4 * n:4 * n + 4, :].rearrange("p s n q -> p n s q"),
                        banks.bank(b, name)[:].rearrange("p (n s q) -> p n s q", s=2, q=64), ACT.Copy), b, name)
                name = name_of("tk", tile)
                banks.wait_filled(act, b, name)
                bank = banks.bank(b, name)
                nc.scalar.activation(kT[:, PAD + t * P:PAD + (t + 1) * P], bank[:, 0:P], ACT.Copy).then_inc(
                    keys_ready, 1)
                banks.freed_by(nc.scalar.activation(
                    vw[:, 2 * t:2 * t + 2, 0:DH1], bank[:, P:P + 2 * DH1].rearrange("p (w d) -> p w d", d=DH1),
                    ACT.Copy), b, name)

            def exps(b, tile):
                for n in range(NS):
                    banks.wait_kept(act, b, name_of(f"s{n}_", tile))
                    nc.scalar.activation(p[:, n], p[:, n], ACT.Exp, scale=float(DH1) ** -0.5).then_inc(exp_ready, 1)

            def keep_pT(b, tile):
                for n in range(NS):
                    name = name_of(f"p{n}_", tile)
                    banks.wait_filled(act, b, name)
                    banks.freed_by(nc.scalar.activation(pT[:, n], banks.bank(b, name)[:], ACT.Copy), b, name)

            def keep_oT(b, tile):
                name = name_of("oT", tile)
                banks.wait_filled(act, b, name)
                banks.freed_by(nc.scalar.activation(oT[:].rearrange("p k t -> p (k t)"),
                                                    banks.bank(b, name)[:, 0:D], ACT.Copy), b, name)

            def body(b, follows):
                for step in steps(b, follows):
                    if "qk" in step:
                        plain_qk(b, step["qk"])
                    if "o" in step:
                        keep_pT(b, step["o"])
                    if "y" in step:
                        keep_oT(b, step["y"])
                    if "s" in step:
                        exps(b, step["s"])
                    if "ln" in step:
                        hi_of_x(b, step["ln"])
                    if "qk" in step:
                        keep_transposed(b, step["qk"])

            every_batch(act, body)

        @block.vector
        def _(dve):
            dve.wait_ge(w_hi, 1)
            nc.vector.tensor_tensor(w_s[1][:], w_raw, rounded(w_s[0][:]), ALU.subtract).then_inc(w_ready, 1)

            def rotate_and_stack(b, tile):
                f, t = tile
                nth = (b + f) * TT + t + 1
                name = name_of("qk", tile)
                dve.wait_ge(qk_copied, nth)
                src = banks.bank(b, name)[:, 0:QK].rearrange("p (h d) -> p h d", d=DH1)
                half = ROPE // 2

                def table(tab, lo, hi):
                    return tab[:, t, lo:hi].unsqueeze(1).broadcast_to([P, H1 + 1, hi - lo])

                nc.vector.tensor_tensor(qk[:, :, 0:ROPE], src[:, :, 0:ROPE], table(rot_c, 0, ROPE),
                                        ALU.mult)
                nc.vector.tensor_tensor(turned[:, :, 0:half], src[:, :, half:ROPE], table(rot_s, 0, half), ALU.mult)
                ins = nc.vector.tensor_tensor(turned[:, :, half:ROPE], src[:, :, 0:half], table(rot_s, half, ROPE),
                                              ALU.mult)
                banks.freed_by(ins, b, name)
                banks.wait_kept(dve, b, name)
                nc.vector.tensor_tensor(qk[:, :, 0:ROPE], qk[:, :, 0:ROPE], turned[:], ALU.add).then_inc(rotated, 1)
                dve.wait_ge(rotated, nth)
                q = qk[:, 0:H1, :].unsqueeze(2).broadcast_to([P, H1, 2, DH1])
                k = qk[:, H1:H1 + 1, :].broadcast_to([P, 2, DH1])
                nc.vector.tensor_copy(q_st[:, :, 0:2].bitcast(F32R), q)
                for r in (0, 2):
                    ins = nc.vector.tensor_copy(k_st[:, :, r].bitcast(F32R), k)
                ins.then_inc(st_hi, 1)
                dve.wait_ge(st_hi, nth)
                nc.vector.tensor_tensor(q_st[:, :, 2:4], q, q_st[:, :, 0:2], ALU.subtract)
                for r in (1, 3):
                    ins = nc.vector.tensor_tensor(k_st[:, :, r], k, k_st[:, :, r - 1], ALU.subtract)
                ins.then_inc(st_ready, 1)

            def shift_scores(b, tile):
                f, t = tile
                for n in range(NS):
                    nth = ((b + f) * TT + t) * NS + n + 1
                    name = name_of(f"s{n}_", tile)
                    banks.wait_filled(dve, b, name)
                    s = banks.bank(b, name)[:].rearrange("p (m k) -> p m k", k=P)
                    nc.vector.tensor_reduce(top[:, n], s, AX_X, ALU.max).then_inc(top_ready, 1)
                    dve.wait_ge(top_ready, nth)
                    banks.freed_by(nc.vector.tensor_tensor(
                        p[:, n].rearrange("p (m k) -> p m k", k=P), s,
                        top[:, n].unsqueeze(2).broadcast_to([P, 4, P]), ALU.subtract), b, name)

            def norm_o(b, tile):
                f, t = tile
                name = name_of("o", tile)
                banks.wait_filled(dve, b, name)
                src = banks.bank(b, name)[:, 0:H1 * (DH1 + 1)].rearrange("p (h d) -> p h d", d=DH1 + 1)
                nc.vector.reciprocal(rinv[:], src[:, :, DH1]).then_inc(rinv_ready, 1)
                dve.wait_ge(rinv_ready, (b + f) * TT + t + 1)
                banks.freed_by(nc.vector.tensor_tensor(o[:], src[:, :, 0:DH1],
                                                       rinv[:].unsqueeze(2).broadcast_to([P, H1, DH1]), ALU.mult),
                               b, name)

            def lo_of_x(b, tile):
                f, t = tile
                dve.wait_ge(xT_hi, (b + f) * TT + t + 1)
                cols = slice(PAD + t * P, PAD + (t + 1) * P)
                banks.freed_by(nc.vector.tensor_tensor(
                    xT[1][:, :, cols], banks.bank(b, name_of("ln", tile))[:, 0:D].rearrange("p (k t) -> p k t", k=KD),
                    rounded(xT[0][:, :, cols]), ALU.subtract), b, name_of("ln", tile))

            def x_behind(b, i):
                return x_tok[:, bass.ds((0 if isinstance(b, int) and b + 1 == B else b + 1) * TT + i, 1), :]

            def norm_before(b):
                norm.wait_inverse(dve, b)
                for i in range(TT):
                    norm.apply(xn[:, i, :], x_behind(b, i), i).then_inc(xn_ready, 1)

            def moments_behind(b, follows):
                dve.wait_ge(y_done, b + 1)
                if not follows:
                    dve.wait_ge(x_updated, b)
                for n in range(2):
                    ins = nc.vector.tensor_tensor(y[:, 2 * n:2 * n + 2, :],
                                                  y_ps[n][:].rearrange("p (t d) -> p t d", d=D),
                                                  bo.unsqueeze(1).broadcast_to([P, 2, D]), ALU.add)
                ins.then_inc(y_freed, 1)
                dve.wait_ge(y_freed, b + 2)
                norm_y.moments(dve, lambda i: y[:, i, :])
                if not follows:
                    norm_y.wait_inverse(dve, b)
                    for i in range(TT):
                        ins = norm_y.apply(y[:, i, :], y[:, i, :], i)
                    ins.then_inc(y_normed, 1)
                    dve.wait_ge(y_normed, b + 1)
                    x_b = x_tok[:, bass.ds(b * TT, TT), :]
                    nc.vector.tensor_tensor(x_b, x_b, y[:], ALU.add).then_inc(x_updated, 1)

            def body(b, follows):
                first = isinstance(b, int) and b < 0
                if not first:
                    if not follows:
                        dve.wait_ge(x_updated, 1)
                    norm.moments(dve, lambda i: x_behind(b, i))
                for n, step in enumerate(steps(b, follows)):
                    if "qk" in step:
                        rotate_and_stack(b, step["qk"])
                    if not first and n == 0:
                        norm_before(b)
                    if "s" in step:
                        shift_scores(b, step["s"])
                    if "o" in step:
                        norm_o(b, step["o"])
                    if "ln" in step:
                        lo_of_x(b, step["ln"])
                if not first:
                    moments_behind(b, follows)

            every_batch(dve, body)

        @block.tensor
        def _(pe):
            def transpose_x(b, tile):
                f, t = tile
                name = name_of("ln", tile)
                banks.wait_freed(pe, b, name)
                pe.wait_ge(xn_ready, (b + f) * TT + t + 1)
                for k in range(KD):
                    ins = pe.transpose(banks.bank(b, name)[:, k * P:(k + 1) * P], xn[:, t, k * P:(k + 1) * P],
                                       c["ident"][:])
                banks.filled_by(ins)

            def project_qk(b, tile):
                t = tile[1]
                name = name_of("qk", tile)
                banks.wait_freed(pe, b, name)
                if tile[0]:
                    banks.wait_kept(pe, b, name_of("ln", tile))
                for k in range(KD):
                    ins = three_passes(pe, banks.bank(b, name)[:, 0:QK],
                                       [x[:, k, PAD + t * P:PAD + (t + 1) * P] for x in xT],
                                       [w[:, k, 0:QK] for w in w_s], start=(k == 0), stop=(k == KD - 1))
                banks.filled_by(ins)

            def transpose_qk(b, tile):
                f, t = tile
                pe.wait_ge(st_ready, (b + f) * TT + t + 1)
                for n, kind in enumerate(("ta", "tb")):
                    name = name_of(kind, tile)
                    banks.wait_freed(pe, b, name)
                    for m in range(4):
                        two = q_st[:, 8 * n + 2 * m:8 * n + 2 * m + 2].rearrange("p h r d -> p (h r d)")
                        ins = pe.transpose(banks.bank(b, name)[:, m * P:(m + 1) * P], two, c["ident"][:])
                    banks.filled_by(ins)
                name = name_of("tk", tile)
                banks.wait_freed(pe, b, name)
                pe.transpose(banks.bank(b, name)[:, 0:P], k_st[:].rearrange("p h r d -> p (h r d)"), c["ident"][:])
                for w in range(2 * t, 2 * t + 2):
                    col = P + (w - 2 * t) * DH1
                    for k in range(KD):
                        ins = three_passes(pe, banks.bank(b, name)[:, col:col + DH1],
                                           [x[:, k, w * 64:w * 64 + P] for x in xT],
                                           [ww[:, k, QK:QK + DH1] for ww in w_s], start=(k == 0),
                                           stop=(k == KD - 1))
                banks.filled_by(ins)

            def scores(b, tile):
                f, t = tile
                pe.wait_ge(keys_ready, (b + f) * TT + t + 1)
                for n in range(NS):
                    half, odd = n // 2, n % 2
                    w = 2 * t + half
                    name = name_of(f"s{n}_", tile)
                    banks.wait_freed(pe, b, name)
                    rows = slice(64 * odd, 64 * odd + 64)
                    pe.matmul(banks.bank(b, name)[:], c["ident_bf"][:],
                              mask[:, min(w, 1)].rearrange("p m k -> p (m k)"), start=True, stop=False)
                    for m in range(4):
                        ins = pe.matmul(banks.bank(b, name)[:, m * P:(m + 1) * P],
                                        qT[rows, t % 2, half, 2 * m:2 * m + 2, :].rearrange("p n q -> p (n q)"),
                                        kT[rows, w * 64:w * 64 + P], start=False, stop=(m == 3))
                    banks.filled_by(ins)

            def transpose_p(b, tile):
                f, t = tile
                for n in range(NS):
                    name = name_of(f"p{n}_", tile)
                    pe.wait_ge(exp_ready, ((b + f) * TT + t) * NS + n + 1)
                    banks.wait_freed(pe, b, name)
                    for m in range(4):
                        ins = pe.transpose(banks.bank(b, name)[:, m * P:(m + 1) * P], p[:, n, m * P:(m + 1) * P],
                                           c["ident"][:])
                    banks.filled_by(ins)

            def attend(b, tile):
                t = tile[1]
                name = name_of("o", tile)
                banks.wait_freed(pe, b, name)
                for n in range(NS):
                    banks.wait_kept(pe, b, name_of(f"p{n}_", tile))
                    for m in range(4):
                        col = (n * 4 + m) * (DH1 + 1)
                        ins = pe.matmul(banks.bank(b, name)[:, col:col + DH1 + 1], pT[:, n, m * P:(m + 1) * P],
                                        vw[:, 2 * t + n // 2, :], start=True, stop=True)
                banks.filled_by(ins)

            def transpose_o(b, tile):
                t = tile[1]
                name = name_of("oT", tile)
                banks.wait_freed(pe, b, name)
                if t:
                    banks.wait_kept(pe, b, name_of("o", tile))
                for k in range(KD):
                    ins = pe.transpose(banks.bank(b, name)[:, k * P:(k + 1) * P],
                                       o[:].rearrange("p h d -> p (h d)")[:, k * P:(k + 1) * P], c["ident"][:])
                banks.filled_by(ins)

            def out_project(b, tile):
                t = tile[1]
                banks.wait_kept(pe, b, name_of("oT", tile))
                if t == 0:
                    pe.wait_ge(y_freed, b + 1)
                for half in range(2):
                    for two in range(2):
                        ins = pe.matmul(y_ps[t // 2][64 * half:64 * half + 64, t % 2 * D:(t % 2 + 1) * D],
                                        oT[:, half, 64 * two:64 * two + 64], wo[:, two, :], start=(two == 0),
                                        stop=(two == 1))
                if t == TT - 1:
                    ins.then_inc(y_done, 1)

            def body(b, follows):
                for step in steps(b, follows):
                    if "qk" in step:
                        project_qk(b, step["qk"])
                    if "o" in step:
                        transpose_p(b, step["o"])
                    if "s" in step:
                        scores(b, step["s"])
                    if "y" in step:
                        transpose_o(b, step["y"])
                    if "o" in step:
                        attend(b, step["o"])
                    if "y" in step:
                        out_project(b, step["y"])
                    if "ln" in step:
                        transpose_x(b, step["ln"])
                    if "qk" in step:
                        transpose_qk(b, step["qk"])
                if follows:
                    banks.wait_kept(pe, b, name_of("ln", (1, TT - 1)))
                    banks.wait_kept(pe, b, name_of("o", (1, 0)))

            banks.all_free(pe)
            pe.sem_inc(y_freed, 1)
            pe.sem_inc(xn_ready, TT)
            pe.wait_ge(w_ready, 1)
            pe.wait_ge(mask_ready, 2)
            every_batch(pe, body)


def experts(nc, a, c, x_tok, out):
    E1 = E + 1
    ROWS = E * NT
    LAG = 2
    AHEAD = [(1, e) for e in range(LAG)]
    ahead = [f"{kind}+{e}" for _, e in AHEAD for kind in "ab"]
    fills, last = [], []
    for names, follows in ((fills, True), (last, False)):
        for e in range(LAG, E1):
            names += [f"a{e}", f"b{e}", f"y{e - LAG}_0", f"y{e - LAG}_1"]
        for e in range(LAG):
            names += ahead[2 * e:2 * e + 2] * follows + [f"y{E1 - LAG + e}_0", f"y{E1 - LAG + e}_1"]

    with ExitStack() as ctx:
        def sb(name, shape, dt=F32):
            return ctx.enter_context(nc.sbuf_tensor(name, shape, dt))

        def sem(name):
            return ctx.enter_context(nc.semaphore(name))

        w1_s = [sb(f"m_w1_{s}", [P, KD, E1, 2 * P], F32R) for s in ("hi", "lo")]
        w2_s = [sb(f"m_w2_{s}", [P, E1, D], F32R) for s in ("hi", "lo")]
        xT = [sb(f"m_xT_{s}", [P, KD, B * T], F32R) for s in ("hi", "lo")]
        w_tok = sb("m_w_tok", [P, E, NT])
        gate = sb("m_gate", [P, 2, T])
        h = sb("m_h", [P, 2, T])
        h_s = [sb(f"m_h_{s}", [P, 2 * LAG, T], F32R) for s in ("hi", "lo")]
        banks = Banks(ctx, nc, "m", fills, 8, before=ahead, last=last, rounds=B)
        h_hi, h_lo = sem("m_h_hi_ready"), sem("m_h_lo_ready")

        def turns(follows):
            return [(0, e) for e in range(LAG, E1)] + AHEAD * follows

        def name_of(kind, turn):
            return f"{kind}{'+' * turn[0]}{turn[1]}"

        def up_and_gate(pe, b, turn):
            f, e = turn
            for kind, half in (("a", 0), ("b", 1)):
                name = name_of(kind, turn)
                banks.wait_freed(pe, b, name)
                for k in range(KD):
                    ins = three_passes(pe, banks.bank(b, name)[:],
                                       [w[:, k, e, half * P:(half + 1) * P] for w in w1_s],
                                       [x[:, k, bass.ds((b + f) * T, T)] for x in xT], start=(k == 0),
                                       stop=(k == KD - 1))
                banks.filled_by(ins)

        def gate_and_hi(act, b, turn):
            e, name = turn[1], name_of("b", turn)
            banks.wait_filled(act, b, name)
            banks.freed_by(nc.scalar.activation(gate[:, e % 2], banks.bank(b, name)[:], ACT.Silu), b, name)
            banks.wait_kept(act, b, name_of("a", turn))
            nc.scalar.activation(h_s[0][:, e % (2 * LAG)], h[:, e % 2], ACT.Copy).then_inc(h_hi, 1)

        def make_h(dve, b, turn):
            f, e = turn
            up, gt = name_of("a", turn), name_of("b", turn)
            banks.wait_filled(dve, b, up)
            banks.wait_kept(dve, b, gt)
            before = (b + f) * E1 + e - 1
            if not isinstance(b, int) or before >= 1:
                dve.wait_ge(h_lo, before)
            banks.freed_by(nc.vector.tensor_tensor(h[:, e % 2], banks.bank(b, up)[:], gate[:, e % 2], ALU.mult), b, up)

        def lo_of_h(pool, b, turn):
            f, e = turn
            pool.wait_ge(h_hi, (b + f) * E1 + e + 1)
            nc.gpsimd.tensor_tensor(h_s[1][:, e % (2 * LAG)], h[:, e % 2], rounded(h_s[0][:, e % (2 * LAG)]),
                                    ALU.subtract).then_inc(h_lo, 1)

        with ExitStack() as inner:
            def sbi(name, shape, dt=F32):
                return inner.enter_context(nc.sbuf_tensor(name, shape, dt))

            def semi(name):
                return inner.enter_context(nc.semaphore(name))

            w1, w2 = experts_landing(c)
            gw = sbi("m_gw", [P, KD, E1])
            gw_s = [sbi(f"m_gw_{s}", [P, KD, E1], F32R) for s in ("hi", "lo")]
            bias = sbi("m_bias", [E1, 1])
            below = sbi("m_below", [P, E, E])
            same, before = sbi("m_same", [P, ROWS]), sbi("m_before", [P, ROWS])
            units, steps = sbi("m_units", [P, DIGITS], I32), sbi("m_steps", [P, DIGITS, WAYS], I32)
            xn = sbi("m_xn", [P, NT - TT, D])
            logits_t = sbi("m_logits_t", [P, T])
            logits = sbi("m_logits", [P, E, NT])
            aff = sbi("m_aff", [P, E, NT])
            more, ties = sbi("m_more", [P, NT, E, E]), sbi("m_ties", [P, NT, E, E])
            rank, off = sbi("m_rank", [P, E, NT]), sbi("m_off", [P, E, NT])
            score = sbi("m_score", [P, E, NT])
            s_row, gt, eq, upto = (sbi(f"m_{s}", [P, P]) for s in ("s_row", "gt", "eq", "upto"))
            zeros = sbi("m_zeros", [P, P])
            found, step = (sbi(f"m_{s}", [P, 1], I32) for s in ("found", "step"))
            cand = sbi("m_cand", [P, WAYS], I32)
            unused = sbi("m_unused", [P, WAYS, P])
            reached = sbi("m_reached", [P, WAYS])
            counts, digit = sbi("m_counts", [P, WAYS]), sbi("m_digit", [P, 1])
            n_gt, n_eq, room = (sbi(f"m_{s}", [P, 1]) for s in ("n_gt", "n_eq", "room"))
            gate_banks = Banks(inner, nc, "n", ["lt", "ln+0", "ln+1", "logits"], banks.psum[4:],
                               before=["ln+0", "ln+1"], last=["lt", "logits"], rounds=B)
            sel_ps = banks.psum[4:7]
            norm = Norm(inner, nc, c, "n", NT)
            loaded, w_hi, w_lo, gw_hi, gw_ready = (semi(f"n_{s}") for s in ("loaded", "w_hi", "w_lo", "gw_hi",
                                                                            "gw_ready"))
            zeroed = semi("n_zeroed")
            xn_ready, xT_hi = semi("n_xn_ready"), semi("n_xT_hi_ready")
            exp_ready = semi("n_exp_ready")
            searched = semi("n_search_step")
            chain = semi("n_selection_step")
            score_ready, score_t = semi("n_score_ready"), semi("n_score_transposed")
            counted, summed = semi("n_counted"), semi("n_summed")
            totals_asked, totals = semi("n_totals_asked"), semi("n_totals")
            weights_ready, weights_t = semi("n_weights_ready"), semi("n_weights_transposed")
            block = inner.enter_context(nc.Block())

            @block.sync
            def _(sp):
                for dst, src in ((gw, "L1_ffn_gate_w"), (bias, "L1_ffn_expert_bias"), (below, "c_below"),
                                 (same, "c_same"), (before, "c_before"), (units, "c_units"), (steps, "c_steps")):
                    sp.dma_start(dst[:], a[src]).then_inc(loaded, DMA_INC)

            @block.gpsimd
            def _(pool):
                nc.gpsimd.memset(logits_t[:], 0.0).then_inc(zeroed, 1)
                nc.gpsimd.memset(zeros[:], 0.0).then_inc(zeroed, 1)
                nc.gpsimd.memset(found[:], 0).then_inc(zeroed, 1)
                for b in range(1, B):
                    norm.inverse(pool, b - 1, b * TT)
                pool.wait_ge(w_hi, KD + 1)
                for part in (slice(0, LAG), slice(LAG, E1)):
                    for k in range(KD):
                        nc.gpsimd.tensor_tensor(w1_s[1][:, k, part], w1[:, k, part], rounded(w1_s[0][:, k, part]),
                                                ALU.subtract).then_inc(w_lo, 1)
                nc.gpsimd.tensor_tensor(w2_s[1][:], w2, rounded(w2_s[0][:]), ALU.subtract)
                for turn in AHEAD:
                    lo_of_h(pool, -1, turn)

            @block.scalar
            def _(act):
                def body(b, follows):
                    if b >= 0:
                        gate_banks.wait_filled(act, b, "lt")
                        gate_banks.freed_by(nc.scalar.activation(logits_t[0:E1, :], gate_banks.bank(b, "lt")[0:E1, :],
                                                            ACT.Identity, bias=bias[:, 0:1]), b, "lt")
                    for k in range(KD if follows else 0):
                        gate_banks.wait_filled(act, b, f"ln+{k}")
                        nc.scalar.activation(xT[0][:, k, bass.ds((b + 1) * T, T)], gate_banks.bank(b, f"ln+{k}")[:],
                                             ACT.Copy).then_inc(xT_hi, 1)

                for b in range(-1, B):
                    body(b, b + 1 < B)
                    if b < 0:
                        act.wait_ge(loaded, 7 * DMA_INC)
                        nc.scalar.activation(gw_s[0][:], gw[:], ACT.Copy).then_inc(gw_hi, 1)
                        act.wait_ge(zeroed, 1)
                        act.wait_ge(c["experts_loaded"], 2 * DMA_INC)
                        for k in range(KD):
                            nc.scalar.activation(w1_s[0][:, k], w1[:, k], ACT.Copy).then_inc(w_hi, 1)
                    if b == 0:
                        nc.scalar.activation(w2_s[0][:], w2, ACT.Copy).then_inc(w_hi, 1)
                gate_banks.wait_kept(act, B - 1, "logits")
                nc.scalar.activation(aff[:], logits[:], ACT.Exp, scale=-1.0).then_inc(exp_ready, 1)
                for turn in AHEAD:
                    gate_and_hi(act, -1, turn)

            @block.vector
            def _(dve):
                def moments(b):
                    norm.moments(dve, lambda i: x_tok[:, i, :], b * TT)

                def apply(b):
                    norm.wait_inverse(dve, b - 1)
                    for i in range(b * TT, (b + 1) * TT):
                        norm.apply(xn[:, i - TT, :], x_tok[:, i, :], i).then_inc(xn_ready, 1)

                moments(1)

                def body(b, follows):
                    first = b < 0
                    if not first:
                        gate_banks.wait_filled(dve, b, "logits")
                        src = gate_banks.bank(b, "logits")[:].rearrange("p (t e) -> p e t", e=P)[:, 0:E, :]
                        gate_banks.freed_by(nc.vector.tensor_copy(logits[:, :, bass.ds(b * TT, TT)], src), b, "logits")
                    for k in range(KD if follows else 0):
                        cols = bass.ds((b + 1) * T, T)
                        dve.wait_ge(xT_hi, (b + 1) * KD + k + 1)
                        gate_banks.freed_by(nc.vector.tensor_tensor(xT[1][:, k, cols], gate_banks.bank(b, f"ln+{k}")[:],
                                                               rounded(xT[0][:, k, cols]), ALU.subtract),
                                       b, f"ln+{k}")
                    if first:
                        dve.wait_ge(gw_hi, 1)
                        nc.vector.tensor_tensor(gw_s[1][:], gw[:], rounded(gw_s[0][:]), ALU.subtract).then_inc(
                            gw_ready, 1)
                    if b + 2 < B:
                        apply(b + 2)
                    if b + 3 < B:
                        moments(b + 3)

                for b in range(-1, B):
                    body(b, b + 1 < B)
                done = [0]

                def then(ins):
                    done[0] += 1
                    ins.then_inc(chain, 1)
                    dve.wait_ge(chain, done[0])

                dve.wait_ge(exp_ready, 1)
                then(nc.vector.tensor_scalar(aff[:], aff[:], 1.0, None, ALU.add))
                then(nc.vector.reciprocal(aff[:], aff[:]))
                rival = aff[:].rearrange("p e t -> p t e").unsqueeze(2).broadcast_to([P, NT, E, E])
                own = aff[:].rearrange("p e t -> p t e").unsqueeze(3).broadcast_to([P, NT, E, E])
                nc.vector.tensor_tensor(more[:], rival, own, ALU.is_gt)
                then(nc.vector.tensor_tensor(ties[:], rival, own, ALU.is_equal))
                lower = below[:].unsqueeze(1).broadcast_to([P, NT, E, E])
                then(nc.vector.tensor_tensor(ties[:], ties[:], lower, ALU.mult))
                then(nc.vector.tensor_tensor(more[:], more[:], ties[:], ALU.add))
                then(nc.vector.tensor_reduce(rank[:].rearrange("p e t -> p t e"), more[:], AX_X, ALU.add))
                then(nc.vector.tensor_scalar(off[:], rank[:], TOP_K - 0.5, -1.0, ALU.is_lt, ALU.add))
                then(nc.vector.scalar_tensor_tensor(out=score[:], in0=off[:], scalar=1.0, in1=aff[:], op0=ALU.add,
                                                    op1=ALU.mult))
                nc.vector.tensor_tensor(score[:], score[:], off[:], ALU.add).then_inc(score_ready, 1)
                make_h(dve, -1, AHEAD[0])
                dve.wait_ge(score_t, 1)
                then(nc.vector.tensor_copy(s_row[0:ROWS, :], sel_ps[0][0:ROWS, 0:P]))
                dve.wait_ge(zeroed, 3)

                def search_digit(n):
                    nc.vector.tensor_tensor(cand[0:ROWS], found[0:ROWS].broadcast_to([ROWS, WAYS]),
                                            steps[0:ROWS, bass.ds(n, 1), :].rearrange("p o w -> p (o w)"),
                                            ALU.bitwise_or).then_inc(searched, 1)
                    dve.wait_ge(searched, n * 4 + 1)
                    for w in range(WAYS):
                        ins = nc.vector.tensor_scalar(unused[0:ROWS, w], s_row[0:ROWS],
                                                      cand[0:ROWS, w:w + 1].bitcast(F32), None, ALU.is_ge,
                                                      ALU.add, accum_out=counts[0:ROWS, w:w + 1])
                    ins.then_inc(counted, 1)
                    dve.wait_ge(summed, n + 1)
                    nc.vector.tensor_scalar(reached[0:ROWS], sel_ps[1][0:ROWS, 0:WAYS], float(CAPACITY), None,
                                            ALU.is_ge, ALU.add, accum_out=digit[0:ROWS]).then_inc(searched, 1)
                    dve.wait_ge(searched, n * 4 + 2)
                    nc.vector.tensor_tensor(step[0:ROWS], digit[0:ROWS], units[0:ROWS, bass.ds(n, 1)],
                                            ALU.mult).then_inc(searched, 1)
                    dve.wait_ge(searched, n * 4 + 3)
                    nc.vector.tensor_tensor(found[0:ROWS], found[0:ROWS], step[0:ROWS],
                                            ALU.bitwise_or).then_inc(searched, 1)
                    dve.wait_ge(searched, n * 4 + 4)
                with dve.Fori(0, DIGITS // UNROLL) as turn:
                    for k in range(UNROLL):
                        search_digit(turn * UNROLL + k)
                bound = found[0:ROWS, 0:1].bitcast(F32)
                nc.vector.tensor_scalar(gt[0:ROWS], s_row[0:ROWS], bound, None, ALU.is_gt, ALU.add,
                                        accum_out=n_gt[0:ROWS])
                nc.vector.tensor_scalar(eq[0:ROWS], s_row[0:ROWS], bound, None, ALU.is_equal, ALU.add,
                                        accum_out=n_eq[0:ROWS]).then_inc(totals_asked, 1)
                dve.wait_ge(totals_asked, 1)
                then(nc.vector.tensor_tensor_scan(upto[0:ROWS], eq[0:ROWS], zeros[0:ROWS], 0.0, ALU.add, ALU.add))
                for turn in AHEAD[1:]:
                    make_h(dve, -1, turn)
                dve.wait_ge(totals, 1)
                then(nc.vector.tensor_scalar(room[0:ROWS], sel_ps[1][0:ROWS, 0:1], -1.0, float(CAPACITY), ALU.mult,
                                             ALU.add))
                then(nc.vector.scalar_tensor_tensor(out=eq[0:ROWS], in0=upto[0:ROWS], scalar=room[0:ROWS, 0:1],
                                                    in1=eq[0:ROWS], op0=ALU.is_le, op1=ALU.mult))
                then(nc.vector.tensor_tensor(gt[0:ROWS], gt[0:ROWS], eq[0:ROWS], ALU.add))
                nc.vector.tensor_tensor(s_row[0:ROWS], s_row[0:ROWS], gt[0:ROWS], ALU.mult).then_inc(weights_ready, 1)
                dve.wait_ge(weights_t, 1)
                nc.vector.tensor_copy(w_tok[:].rearrange("p e t -> p (e t)"), sel_ps[2][:, 0:ROWS])

            @block.tensor
            def _(pe):
                gate_banks.all_free(pe)
                banks.all_free(pe)

                def body(b, follows):
                    first = b < 0
                    if not first:
                        gate_banks.wait_freed(pe, b, "lt")
                        if b == 0:
                            pe.wait_ge(gw_ready, 1)
                        for k in range(KD):
                            ins = three_passes(pe, gate_banks.bank(b, "lt")[0:E1, :], [w[:, k, :] for w in gw_s],
                                               [x[:, k, bass.ds(b * T, T)] for x in xT], start=(k == 0),
                                               stop=(k == KD - 1))
                        gate_banks.filled_by(ins)
                    for k in range(KD if follows else 0):
                        gate_banks.wait_freed(pe, b, f"ln+{k}")
                        for i in range(TT):
                            if k == 0 and b >= 0:
                                pe.wait_ge(xn_ready, b * TT + i + 1)
                            source = c["xn"][:, i] if b < 0 else xn[:, b * TT + i]
                            ins = pe.transpose(gate_banks.bank(b, f"ln+{k}")[:, i * P:(i + 1) * P],
                                               source[:, k * P:(k + 1) * P], c["ident"][:])
                        gate_banks.filled_by(ins)
                    if not first:
                        gate_banks.wait_freed(pe, b, "logits")
                        gate_banks.wait_kept(pe, b, "lt")
                        for i in range(TT):
                            ins = pe.transpose(gate_banks.bank(b, "logits")[:, i * P:(i + 1) * P],
                                               logits_t[:, i * P:(i + 1) * P], c["ident"][:])
                        gate_banks.filled_by(ins)
                    for k in range(KD if follows else 0):
                        gate_banks.wait_kept(pe, b, f"ln+{k}")

                for b in range(-1, B):
                    body(b, b + 1 < B)
                pe.wait_ge(w_lo, KD)
                for turn in AHEAD:
                    up_and_gate(pe, -1, turn)
                pe.wait_ge(score_ready, 1)
                pe.transpose(sel_ps[0][0:ROWS, 0:P], score[:].rearrange("p e t -> p (e t)"), c["ident"][:]).then_inc(
                    score_t, 1)
                with pe.Fori(0, DIGITS // UNROLL) as turn:
                    for k in range(UNROLL):
                        pe.wait_ge(counted, turn * UNROLL + k + 1)
                        pe.matmul(sel_ps[1][0:ROWS, 0:WAYS], same[0:ROWS, 0:ROWS], counts[0:ROWS], start=True,
                                  stop=True).then_inc(summed, 1)
                pe.wait_ge(totals_asked, 1)
                pe.matmul(sel_ps[1][0:ROWS, 0:1], same[0:ROWS, 0:ROWS], n_gt[0:ROWS, 0:1], start=True, stop=False)
                pe.matmul(sel_ps[1][0:ROWS, 0:1], before[0:ROWS, 0:ROWS], n_eq[0:ROWS, 0:1], start=False,
                          stop=True).then_inc(totals, 1)
                pe.wait_ge(weights_ready, 1)
                pe.transpose(sel_ps[2][:, 0:ROWS], s_row[0:ROWS, :], c["ident"][0:ROWS, 0:ROWS]).then_inc(weights_t, 1)

        acc = sb("m_acc", [P, TT, D])
        norm = Norm(ctx, nc, c, "m")
        y_normed, x_updated, stored = (sem(f"m_{s}") for s in ("y_normed", "x_updated", "stored"))

        block = ctx.enter_context(nc.Block())

        @block.sync
        def _(sp):
            for b in range(B):
                sp.wait_ge(x_updated, b + 1)
                sp.dma_start(out[b].rearrange("(t p) d -> p t d", p=P), x_tok[:, b * TT:(b + 1) * TT, :]).then_inc(
                    stored, DMA_INC)
            sp.wait_ge(stored, B * DMA_INC)

        @block.gpsimd
        def _(pool):
            def body(b, follows):
                for turn in turns(follows):
                    lo_of_h(pool, b, turn)
                norm.inverse(pool, b)

            batches(pool, body)

        @block.scalar
        def _(act):
            def body(b, follows):
                for turn in turns(follows):
                    gate_and_hi(act, b, turn)

            batches(act, body)

        @block.vector
        def _(dve):
            def gather(b, e):
                for n in range(2):
                    name = f"y{e}_{n}"
                    banks.wait_filled(dve, b, name)
                    if e:
                        banks.wait_kept(dve, b, f"y{e - 1}_{n}")
                    for j in range(2):
                        i = 2 * n + j
                        y = banks.bank(b, name)[:, j * D:(j + 1) * D]
                        if e == 0:
                            ins = nc.vector.tensor_copy(acc[:, i, :], y)
                        else:
                            ins = nc.vector.scalar_tensor_tensor(
                                out=acc[:, i, :], in0=y, scalar=w_tok[:, e - 1, bass.ds(b * TT + i, 1)],
                                in1=acc[:, i, :], op0=ALU.mult, op1=ALU.add)
                    banks.freed_by(ins, b, name)

            def body(b, follows):
                for f, e in turns(follows):
                    make_h(dve, b, (f, e))
                    gather(b, E1 - LAG + e if f else e - LAG)
                if not follows:
                    for e in range(E1 - LAG, E1):
                        gather(b, e)
                for n in range(2):
                    banks.wait_kept(dve, b, f"y{E1 - 1}_{n}")
                norm.moments(dve, lambda i: acc[:, i, :])
                norm.wait_inverse(dve, b)
                for i in range(TT):
                    ins = norm.apply(acc[:, i, :], acc[:, i, :], i)
                ins.then_inc(y_normed, 1)
                dve.wait_ge(y_normed, b + 1)
                x_b = x_tok[:, bass.ds(b * TT, TT), :]
                nc.vector.tensor_tensor(x_b, x_b, acc[:], ALU.add).then_inc(x_updated, 1)
                dve.wait_ge(x_updated, b + 1)

            batches(dve, body)

        @block.tensor
        def _(pe):
            def project_down(b, e):
                pe.wait_ge(h_lo, b * E1 + e + 1)
                for n in range(2):
                    name = f"y{e}_{n}"
                    banks.wait_freed(pe, b, name)
                    for j in range(2):
                        i = 2 * n + j
                        ins = three_passes(pe, banks.bank(b, name)[:, j * D:(j + 1) * D],
                                           [x[:, e % (2 * LAG), i * P:(i + 1) * P] for x in h_s],
                                           [w[:, e, :] for w in w2_s], start=True, stop=True)
                    banks.filled_by(ins)

            def body(b, follows):
                for f, e in turns(follows):
                    up_and_gate(pe, b, (f, e))
                    project_down(b, E1 - LAG + e if f else e - LAG)
                if not follows:
                    for e in range(E1 - LAG, E1):
                        project_down(b, e)

            batches(pe, body)


def layers(nc, a, out):
    with ExitStack() as ctx:
        c = {}
        x_tok = ctx.enter_context(nc.sbuf_tensor("x_tok", [P, NT, D], F32))
        c["ident"] = ctx.enter_context(nc.sbuf_tensor("ident", [P, P], F32))
        c["ident_bf"] = ctx.enter_context(nc.sbuf_tensor("ident_bf", [P, P], BF16))
        c["causal"] = ctx.enter_context(nc.sbuf_tensor("causal", [P, P], F32))
        c["causal_bf"] = ctx.enter_context(nc.sbuf_tensor("causal_bf", [P, P], BF16))
        c["minus_half"] = ctx.enter_context(nc.sbuf_tensor("minus_half", [P, TT], F32))
        c["landing"] = ctx.enter_context(nc.sbuf_tensor("landing", [P, T * H], F32))
        for name in ("x", "ffn0_ug", "ffn0_down", "attention1", "experts"):
            c[f"{name}_loaded"] = ctx.enter_context(nc.semaphore(f"{name}_loaded"))
        c["down_turned"] = ctx.enter_context(nc.semaphore("down_turned"))
        const_loaded = ctx.enter_context(nc.semaphore("const_loaded"))
        const_ready = ctx.enter_context(nc.semaphore("const_ready"))
        with nc.Block() as block:
            @block.sync
            def _(sp):
                sp.dma_start(x_tok[:, 0:TT, :], a["L0_attn_x"][0].rearrange("(t p) d -> p t d", p=P)).then_inc(
                    c["x_loaded"], DMA_INC)
                sp.dma_start(c["ident"][:], a["c_ident"]).then_inc(const_loaded, DMA_INC)
                sp.dma_start(c["causal"][:], a["c_causal"]).then_inc(const_loaded, DMA_INC)
            @block.gpsimd
            def _(pool):
                nc.gpsimd.memset(c["minus_half"][:], -0.5).then_inc(const_ready, 1)
            @block.vector
            def _(dve):
                dve.wait_ge(const_loaded, 2 * DMA_INC)
                nc.vector.tensor_copy(c["ident_bf"][:], c["ident"][:]).then_inc(const_ready, 1)
                nc.vector.tensor_copy(c["causal_bf"][:], c["causal"][:]).then_inc(const_ready, 1)
        attention0(nc, a, c, x_tok)
        c["xn"] = ctx.enter_context(nc.sbuf_tensor("xn_of_layer", [P, TT, D], F32))
        ffn0(nc, a, c, x_tok)
        attention1(nc, a, c, x_tok)
        experts(nc, a, c, x_tok, out)


_INS = ['L0_attn_x', 'L0_attn_Wq', 'L0_attn_bq', 'L0_attn_Wk', 'L0_attn_bk', 'L0_attn_Wv', 'L0_attn_bv', 'L0_attn_Wo',
        'L0_attn_bo', 'L0_ffn_SU_ug', 'L0_ffn_SU_dp', 'L0_ffn_Wscale_ug', 'L0_ffn_Wscale_dp', 'L0_ffn_W_up',
        'L0_ffn_W_gate', 'L0_ffn_W_down', 'L1_attn_Wq', 'L1_attn_Wk', 'L1_attn_Wv', 'L1_attn_Wo', 'L1_attn_bo',
        'L1_ffn_gate_w', 'L1_ffn_expert_bias', 'L1_ffn_shared_w1', 'L1_ffn_shared_w2', 'L1_ffn_routed_w1',
        'L1_ffn_routed_w2']


def kernel(**inputs):
    import concourse.bacc as _bacc
    from concourse.bass_utils import run_bass_kernel_spmd as _run

    nc = _bacc.Bacc("TRN2", target_bir_lowering=False, num_devices=1)
    arrays, args = {}, {}
    given = {name: np.asarray(inputs[name]) for name in _INS}
    for name in ("L0_attn_bq", "L0_attn_bk", "L0_attn_bv"):
        given[name] = given[name].reshape(H, DH).T
    for name in ("L0_attn_bo", "L0_ffn_Wscale_dp", "L1_attn_bo"):
        given[name] = given[name].reshape(1, -1)
    for name in ("L0_ffn_SU_ug", "L0_ffn_SU_dp"):
        given[name] = given[name].reshape(-1, P).T
    scales = given.pop("L0_ffn_Wscale_ug").reshape(2, -1, P)
    given["L0_ffn_Wscale_up"], given["L0_ffn_Wscale_gate"] = scales[0].T, scales[1].T
    w1 = np.concatenate([given.pop("L1_ffn_shared_w1"), given.pop("L1_ffn_routed_w1")])
    given["L1_ffn_w1"] = w1.reshape(E + 1, KD, P, D).transpose(2, 1, 0, 3)
    w2 = np.concatenate([given.pop("L1_ffn_shared_w2"), given.pop("L1_ffn_routed_w2")])
    given["L1_ffn_w2"] = w2.transpose(1, 0, 2)
    given["L1_ffn_expert_bias"] = np.pad(given["L1_ffn_expert_bias"], (0, 1)).reshape(-1, 1)
    gate = np.pad(given["L1_ffn_gate_w"], ((0, 0), (0, 1)))
    given["L1_ffn_gate_w"] = gate.reshape(KD, P, E + 1).transpose(1, 0, 2)
    given["L1_attn_Wo"] = given["L1_attn_Wo"].reshape(4, 2, 2, DH1, D).transpose(1, 2, 0, 3, 4).reshape(D, D)
    for name in ("L0_ffn_W_up", "L0_ffn_W_gate", "L0_ffn_W_down"):
        given[name] = given[name].T
    for name, a in (given | shape_constants()).items():
        a = np.ascontiguousarray(a)
        arrays[f"in_{name}"] = a
        args[name] = nc.dram_tensor(f"in_{name}", a.shape, mybir.dt.from_np(a.dtype), kind="ExternalInput").ap()
    out = nc.dram_tensor("out_x", (B, T, D), F32, kind="ExternalOutput").ap()
    layers(nc, args, out)
    r = _run(nc, [arrays], core_ids=[0])
    return r.results[0]["out_x"]
```
